# Optimizing a Trainium2 kernel written in Bass

```python
import numpy as np
import jax
import jax.numpy as jnp

def _softmax(x, axis=-1):
    return jax.nn.softmax(x, axis=axis)

def _gelu(x):
    return jax.nn.gelu(x, approximate=True)

def _silu(x):
    return jax.nn.silu(x)

def _sigmoid(x):
    return jax.nn.sigmoid(x)

def _layernorm(x, axis=-1, eps=1e-05):
    m = jnp.mean(x, axis=axis, keepdims=True)
    v = jnp.var(x, axis=axis, keepdims=True)
    return (x - m) / jnp.sqrt(v + eps)

def _scatter_add(tgt, idx, src, axis=0):
    return tgt.at[idx].add(src)

def _segment_sum(src, seg, n):
    return jax.ops.segment_sum(src, seg, n)
kernel_name = 'mk_xattn_ffn_d2_seqx_r4_8605e3'

def setup_inputs(seed: int=0):
    np.random.seed(seed)
    _w = jnp.asarray

    def _rec_inputs():
        import jax
        import jax.numpy as jnp
        _rk = jax.random.key(seed)
        x = -0.0003929 + 0.9999 * jax.random.normal(jax.random.fold_in(_rk, 1), (4, 512, 512), jnp.float32)
        _lenS = 512 - jax.random.randint(jax.random.fold_in(_rk, 7), (4,), 0, max(1, 512 // 4) + 1, jnp.int32)
        _lenS2 = 64 - jax.random.randint(jax.random.fold_in(_rk, 8), (4,), 0, max(1, 64 // 4) + 1, jnp.int32)
        _ctx_1024P = jax.random.normal(jax.random.fold_in(_rk, 11), (4, 16, 256), jnp.float32)
        _ctx_1024c = jax.random.dirichlet(jax.random.fold_in(_rk, 511), 0.3 * jnp.ones((16,), jnp.float32), (4, 64))
        _ctx_1024t = jnp.einsum('bsk,bkd->bsd', _ctx_1024c, _ctx_1024P)
        _ctx_1024t = _ctx_1024t * jax.lax.rsqrt(jnp.mean(jnp.square(_ctx_1024t)) + 1e-12) * 0.953939
        ctx_1024 = -0.000494167 + 1.00018 * (_ctx_1024t + 0.3 * jax.random.normal(jax.random.fold_in(_rk, 611), (4, 64, 256), jnp.float32))
        _validS = jnp.arange(512)[None, :] < _lenS[:, None]
        _validS2 = jnp.arange(64)[None, :] < _lenS2[:, None]
        _causal = jnp.tril(jnp.ones((512, 512), dtype=bool))
        mask_BxS2_bf1 = jnp.ones((4, 64), dtype=bool)
        return (x, ctx_1024, mask_BxS2_bf1)
    x, ctx_1024, mask_BxS2_bf1 = _rec_inputs()

    def _L0_xattn_setup():
        import jax, jax.numpy as jnp
        import numpy as np
        N_HEADS = 16
        N_KV_HEADS = 8
        HEAD_DIM = 128
        D_TEXT = 512
        D_VISION = 256
        GROUPS = N_HEADS // N_KV_HEADS
        key = jax.random.key(seed)
        ks = jax.random.split(key, 6)
        B, T_text, T_vis = (4, 512, 144)
        text_hidden = jax.random.normal(ks[0], (B, T_text, D_TEXT), dtype=jnp.float32)
        vision_tokens = jax.random.normal(ks[1], (B, T_vis, D_VISION), dtype=jnp.float32)
        vision_mask = jnp.ones((B, T_vis), dtype=bool)
        s = 0.02
        Wq = jax.random.normal(ks[2], (D_TEXT, N_HEADS * HEAD_DIM), dtype=jnp.float32) * s
        Wk = jax.random.normal(ks[3], (D_VISION, N_KV_HEADS * HEAD_DIM), dtype=jnp.float32) * s
        Wv = jax.random.normal(ks[4], (D_VISION, N_KV_HEADS * HEAD_DIM), dtype=jnp.float32) * s
        Wo = jax.random.normal(ks[5], (N_HEADS * HEAD_DIM, D_TEXT), dtype=jnp.float32) * s
        return {'text_hidden': text_hidden, 'vision_tokens': vision_tokens, 'vision_mask': vision_mask, 'Wq': Wq, 'Wk': Wk, 'Wv': Wv, 'Wo': Wo}
    _L0_xattn_all = _L0_xattn_setup()
    _L0_xattn_in = {k: v for k, v in _L0_xattn_all.items() if k in ('Wq', 'Wk', 'Wv', 'Wo')}
    del _L0_xattn_all

    def _L0_ffn_setup():
        import jax, jax.numpy as jnp
        import numpy as np
        TOP_K = 2
        key = jax.random.key(seed)
        ks = jax.random.split(key, 6)
        B, S, H, F, E = (1, 512, 512, 352, 8)
        Fs = 2 * F
        std = jnp.float32(0.02)
        return {'hidden_states': jax.random.normal(ks[0], (B, S, H), jnp.float32), 'gate_weight': jax.random.normal(ks[1], (E, H), jnp.float32) * std, 'gate_up_weights': jax.random.normal(ks[2], (E, 2 * F, H), jnp.float32) * std, 'down_weights': jax.random.normal(ks[3], (E, H, F), jnp.float32) * std, 'shared_gate_up': jax.random.normal(ks[4], (2 * Fs, H), jnp.float32) * std, 'shared_down': jax.random.normal(ks[5], (H, Fs), jnp.float32) * std}
    _L0_ffn_all = _L0_ffn_setup()
    _L0_ffn_in = {k: v for k, v in _L0_ffn_all.items() if k in ('gate_weight', 'gate_up_weights', 'down_weights', 'shared_gate_up', 'shared_down')}
    del _L0_ffn_all

    def _L1_xattn_setup():
        import jax, jax.numpy as jnp
        import numpy as np
        EPS = 1e-05

        def rmsnorm(x, g, eps=EPS):
            var = jnp.mean(jnp.square(x), axis=-1, keepdims=True)
            return x * jax.lax.rsqrt(var + eps) * g
        key = jax.random.key(seed)
        ks = jax.random.split(key, 8)
        B, Sq, Skv = (2, 1024, 128)
        dim, cdim, H, D = (512, 256, 16, 128)
        inner = H * D
        s = lambda f: 1.0 / np.sqrt(f)
        return {'hidden_states': jax.random.normal(ks[0], (B, Sq, dim), jnp.float32), 'encoder_hidden_states': jax.random.normal(ks[1], (B, Skv, cdim), jnp.float32), 'Wq': jax.random.normal(ks[2], (dim, inner), jnp.float32) * s(dim), 'Wk': jax.random.normal(ks[3], (cdim, inner), jnp.float32) * s(cdim), 'Wv': jax.random.normal(ks[4], (cdim, inner), jnp.float32) * s(cdim), 'Wo': jax.random.normal(ks[5], (inner, dim), jnp.float32) * s(inner), 'gq': jnp.ones((D,), jnp.float32), 'gk': jnp.ones((D,), jnp.float32)}
    _L1_xattn_all = _L1_xattn_setup()
    _L1_xattn_in = {k: v for k, v in _L1_xattn_all.items() if k in ('Wq', 'Wk', 'Wv', 'Wo', 'gq', 'gk')}
    del _L1_xattn_all

    def _L1_ffn_setup():
        import jax, jax.numpy as jnp
        import numpy as np
        E = 8
        K = 2
        C = 512
        I = 352
        IS = I * 2
        B, T = (2, 512)
        key = jax.random.key(seed)
        ks = jax.random.split(key, 9)
        s = 0.02
        return {'x': jax.random.normal(ks[0], (B, T, C), dtype=jnp.float32), 'gate_w': jax.random.normal(ks[1], (E, C), dtype=jnp.float32) * s, 'w1': jax.random.normal(ks[2], (E, I, C), dtype=jnp.float32) * s, 'w2': jax.random.normal(ks[3], (E, I, C), dtype=jnp.float32) * s, 'w3': jax.random.normal(ks[4], (E, C, I), dtype=jnp.float32) * s, 'sw1': jax.random.normal(ks[5], (IS, C), dtype=jnp.float32) * s, 'sw2': jax.random.normal(ks[6], (IS, C), dtype=jnp.float32) * s, 'sw3': jax.random.normal(ks[7], (C, IS), dtype=jnp.float32) * s}
    _L1_ffn_all = _L1_ffn_setup()
    _L1_ffn_in = {k: v for k, v in _L1_ffn_all.items() if k in ('gate_w', 'w1', 'w2', 'w3', 'sw1', 'sw2', 'sw3')}
    del _L1_ffn_all
    return {'x': x, 'ctx_1024': ctx_1024, 'mask_BxS2_bf1': mask_BxS2_bf1, 'L0_xattn_Wq': _L0_xattn_in['Wq'], 'L0_xattn_Wk': _L0_xattn_in['Wk'], 'L0_xattn_Wv': _L0_xattn_in['Wv'], 'L0_xattn_Wo': _L0_xattn_in['Wo'], 'L0_ffn_gate_weight': _L0_ffn_in['gate_weight'], 'L0_ffn_gate_up_weights': _L0_ffn_in['gate_up_weights'], 'L0_ffn_down_weights': _L0_ffn_in['down_weights'], 'L0_ffn_shared_gate_up': _L0_ffn_in['shared_gate_up'], 'L0_ffn_shared_down': _L0_ffn_in['shared_down'], 'L1_xattn_Wq': _L1_xattn_in['Wq'], 'L1_xattn_Wk': _L1_xattn_in['Wk'], 'L1_xattn_Wv': _L1_xattn_in['Wv'], 'L1_xattn_Wo': _L1_xattn_in['Wo'], 'L1_xattn_gq': _L1_xattn_in['gq'], 'L1_xattn_gk': _L1_xattn_in['gk'], 'L1_ffn_gate_w': _L1_ffn_in['gate_w'], 'L1_ffn_w1': _L1_ffn_in['w1'], 'L1_ffn_w2': _L1_ffn_in['w2'], 'L1_ffn_w3': _L1_ffn_in['w3'], 'L1_ffn_sw1': _L1_ffn_in['sw1'], 'L1_ffn_sw2': _L1_ffn_in['sw2'], 'L1_ffn_sw3': _L1_ffn_in['sw3']}

def reference(x, ctx_1024, mask_BxS2_bf1, L0_xattn_Wq, L0_xattn_Wk, L0_xattn_Wv, L0_xattn_Wo, L0_ffn_gate_weight, L0_ffn_gate_up_weights, L0_ffn_down_weights, L0_ffn_shared_gate_up, L0_ffn_shared_down, L1_xattn_Wq, L1_xattn_Wk, L1_xattn_Wv, L1_xattn_Wo, L1_xattn_gq, L1_xattn_gk, L1_ffn_gate_w, L1_ffn_w1, L1_ffn_w2, L1_ffn_w3, L1_ffn_sw1, L1_ffn_sw2, L1_ffn_sw3):
    import jax
    import jax.numpy as jnp

    def _L0_xattn_ref(text_hidden, vision_tokens, vision_mask, Wq, Wk, Wv, Wo):
        import jax, jax.numpy as jnp
        import numpy as np
        N_HEADS = 16
        N_KV_HEADS = 8
        HEAD_DIM = 128
        D_TEXT = 512
        D_VISION = 256
        GROUPS = N_HEADS // N_KV_HEADS
        B, T_text, _ = text_hidden.shape
        T_vis = vision_tokens.shape[1]
        scale = jnp.float32(np.sqrt(HEAD_DIM))
        q = (text_hidden @ Wq).reshape(B, T_text, N_HEADS, HEAD_DIM).transpose(0, 2, 1, 3)
        k = (vision_tokens @ Wk).reshape(B, T_vis, N_KV_HEADS, HEAD_DIM).transpose(0, 2, 1, 3)
        v = (vision_tokens @ Wv).reshape(B, T_vis, N_KV_HEADS, HEAD_DIM).transpose(0, 2, 1, 3)
        k = jnp.repeat(k, GROUPS, axis=1)
        v = jnp.repeat(v, GROUPS, axis=1)
        scores = jnp.einsum('bhtd,bhsd->bhts', q, k) / scale
        mask = vision_mask[:, None, None, :]
        scores = jnp.where(mask, scores, -jnp.inf)
        attn = jax.nn.softmax(scores, axis=-1)
        attn = jnp.nan_to_num(attn, nan=0.0)
        out = jnp.einsum('bhts,bhsd->bhtd', attn, v)
        out = out.transpose(0, 2, 1, 3).reshape(B, T_text, N_HEADS * HEAD_DIM)
        return out @ Wo

    def _L0_ffn_ref(hidden_states, gate_weight, gate_up_weights, down_weights, shared_gate_up, shared_down):
        import jax, jax.numpy as jnp
        import numpy as np
        TOP_K = 2
        B, S, H = hidden_states.shape
        E, twoF, _ = gate_up_weights.shape
        F = twoF // 2
        T = B * S
        x = hidden_states.reshape(T, H)
        logits = x @ gate_weight.T
        scores = jax.nn.softmax(logits, axis=-1)
        topk_w, topk_idx = jax.lax.top_k(scores, TOP_K)
        combine = jnp.zeros((T, E), x.dtype).at[jnp.arange(T)[:, None], topk_idx].add(topk_w)
        gu = jnp.einsum('th,efh->tef', x, gate_up_weights)
        act = jax.nn.silu(gu[..., :F]) * gu[..., F:]
        y = jnp.einsum('tef,te,ehf->th', act, combine, down_weights)
        Fs = shared_gate_up.shape[0] // 2
        sgu = x @ shared_gate_up.T
        sact = jax.nn.silu(sgu[:, :Fs]) * sgu[:, Fs:]
        y = y + sact @ shared_down.T
        return y.reshape(B, S, H)

    def _L1_xattn_ref(hidden_states, encoder_hidden_states, Wq, Wk, Wv, Wo, gq, gk):
        import jax, jax.numpy as jnp
        import numpy as np
        EPS = 1e-05

        def rmsnorm(x, g, eps=EPS):
            var = jnp.mean(jnp.square(x), axis=-1, keepdims=True)
            return x * jax.lax.rsqrt(var + eps) * g
        B, Sq, _ = hidden_states.shape
        Skv = encoder_hidden_states.shape[1]
        D = gq.shape[0]
        H = Wq.shape[1] // D
        scale = 1.0 / np.sqrt(D)
        q = (hidden_states @ Wq).reshape(B, Sq, H, D)
        k = (encoder_hidden_states @ Wk).reshape(B, Skv, H, D)
        v = (encoder_hidden_states @ Wv).reshape(B, Skv, H, D)
        q = rmsnorm(q, gq)
        k = rmsnorm(k, gk)
        scores = jnp.einsum('bqhd,bkhd->bhqk', q, k) * scale
        attn = jax.nn.softmax(scores, axis=-1)
        out = jnp.einsum('bhqk,bkhd->bqhd', attn, v)
        out = out.reshape(B, Sq, H * D)
        return out @ Wo

    def _L1_ffn_ref(x, gate_w, w1, w2, w3, sw1, sw2, sw3):
        import jax, jax.numpy as jnp
        import numpy as np
        E = 8
        K = 2
        C = 512
        I = 352
        IS = I * 2
        B, T = (2, 512)
        Bq, Tq, Cq = x.shape
        xf = x.reshape(-1, Cq)
        logits = xf @ gate_w.T
        probs = jax.nn.softmax(logits.astype(jnp.float32), axis=-1)
        topk_p, topk_i = jax.lax.top_k(probs, K)
        comb = (jax.nn.one_hot(topk_i, E, dtype=jnp.float32) * topk_p[..., None]).sum(axis=1).astype(x.dtype)
        h1 = jnp.einsum('nc,eic->eni', xf, w1)
        h2 = jnp.einsum('nc,eic->eni', xf, w2)
        h = jax.nn.silu(h1) * h2
        eo = jnp.einsum('eni,eci->enc', h, w3)
        y = jnp.einsum('enc,ne->nc', eo, comb).reshape(Bq, Tq, Cq)
        sh = jax.nn.silu(xf @ sw1.T) * (xf @ sw2.T) @ sw3.T
        return y + sh.reshape(Bq, Tq, Cq)
    x = x + _L0_xattn_ref(_layernorm(x, axis=-1), ctx_1024, mask_BxS2_bf1, L0_xattn_Wq, L0_xattn_Wk, L0_xattn_Wv, L0_xattn_Wo)
    x = x + _L0_ffn_ref(_layernorm(x, axis=-1), L0_ffn_gate_weight, L0_ffn_gate_up_weights, L0_ffn_down_weights, L0_ffn_shared_gate_up, L0_ffn_shared_down)
    x = x + _L1_xattn_ref(_layernorm(x, axis=-1), ctx_1024, L1_xattn_Wq, L1_xattn_Wk, L1_xattn_Wv, L1_xattn_Wo, L1_xattn_gq, L1_xattn_gk)
    x = x + _L1_ffn_ref(_layernorm(x, axis=-1), L1_ffn_gate_w, L1_ffn_w1, L1_ffn_w2, L1_ffn_w3, L1_ffn_sw1, L1_ffn_sw2, L1_ffn_sw3)
    return x

_drawn_inputs = setup_inputs


def setup_inputs(seed=0):
    import zlib

    import numpy as np

    out = dict(_drawn_inputs(seed))
    spreads = {'L1_xattn_gq': (1.0, 0.6), 'L1_xattn_gk': (1.0, 0.6)}
    factors = {'L0_xattn_Wq': 7.378,
     'L0_xattn_Wk': 7.384,
     'L0_ffn_gate_weight': 6.187,
     'L0_ffn_gate_up_weights': 5.273,
     'L0_ffn_down_weights': 5.294,
     'L1_ffn_gate_w': 6.325,
     'L1_ffn_w1': 5.493,
     'L1_ffn_w2': 5.398,
     'L1_ffn_w3': 5.418,
     'L1_ffn_sw1': 8.0,
     'L1_ffn_sw2': 8.0,
     'L1_ffn_sw3': 8.0,
     'L0_ffn_shared_gate_up': 3.367,
     'L0_ffn_shared_down': 3.356}
    for name, (base, spread) in spreads.items():
        noise = np.random.default_rng([zlib.crc32(name.encode()), seed]).standard_normal(out[name].shape)
        drawn = base * np.exp(spread * noise) if base else spread * noise
        out[name] = jnp.asarray(drawn.astype(out[name].dtype))
    for name, factor in factors.items():
        out[name] = (out[name] * factor).astype(out[name].dtype)
    return out
```

```python
from contextlib import ExitStack

import concourse.bass as bass
from concourse import mybir

ALU = mybir.AluOpType
ACT = mybir.ActivationFunctionType
F32 = mybir.dt.float32
F32R = mybir.dt.float32r
I32 = mybir.dt.int32
U8 = mybir.dt.uint8
AX = mybir.AxisListType.X

P = 128
B, T, D = 4, 512, 512
KC = D // P
NT = B * T // P
TB = T // P
H, DH, S, CD = 16, 128, 64, 256
HS = H * S
BS = B * S
CC = CD // P
HG = 4
NG = H // HG
NQ = HS // P
E, F = 8, 352
NJ = 2
FC = -(-F // P)
LAP = FC * P - F
MAX_BLOCKS = (2 * NT * P + E * (P - 1)) // P
EPS = 1e-5
SCALE = float(DH) ** -0.5
MASKED = -(2.0 ** 100)
STAGES = 4


def after(eng, sem, value):
    if not isinstance(value, int) or value > 0:
        eng.wait_ge(sem, value)


class Chain:

    def __init__(self, eng, sem):
        self.eng, self.sem, self.n = eng, sem, 0

    def __call__(self, ins):
        self.n += 1
        ins.then_inc(self.sem, 1)
        self.eng.wait_ge(self.sem, self.n)


def names(ctx, nc, tag):
    def sb(name, shape, dt=F32):
        return ctx.enter_context(nc.sbuf_tensor(f"{tag}_{name}", shape, dt))

    def ps(name, shape, dt=F32):
        return ctx.enter_context(nc.psum_tensor(f"{tag}_{name}", shape, dt))

    sems = []

    def sem(name):
        sems.append(nc.alloc_semaphore(f"{tag}_{name}"))
        return sems[-1]

    def release():
        if sems:
            nc.clear_and_free_semaphores(sems)
            nc.all_engine_barrier()
    ctx.callback(release)
    return sb, ps, sem


def matmul3(pe, out, hi_w, lo_w, hi_x, lo_x, start, stop):
    pe.matmul(out, hi_w, hi_x, start=start, stop=False)
    pe.matmul(out, hi_w, lo_x, start=False, stop=False)
    return pe.matmul(out, lo_w, hi_x, start=False, stop=stop)


def prep(nc, tag, kv_heads, ctx_t, wk, wv, wq_t, wo, gq, gk, mask, ident_d, a_d, v_d):
    normed = gq is not None
    rep = H // kv_heads
    GK = HG // rep
    cols = GK * DH
    with ExitStack() as ctx:
        sb, ps, sem = names(ctx, nc, tag)
        ctx_sb = sb("ctx", [P, CC, BS])
        wk_sb = sb("wk", [P, 2, CC, cols])
        wv_sb = sb("wv", [P, 2, CC, cols])
        wq_sb = sb("wq", [P, 2, HG, D])
        wo_sb = sb("wo", [P, 2, HG, D])
        kT = sb("kT", [P, 2, GK, BS])
        vT = sb("vT", [P, 2, GK, BS])
        a_st = sb("a_st", [P, 2, KC, B, HG * S])
        v_st = sb("v_st", [P, 2, 2, HG, D])
        maskcol = sb("maskcol", [P, 2])
        mask_u8 = sb("mask_u8", [P, 2], U8)
        if normed:
            gq_sb = sb("gq", [P, 1])
            gk_sb = sb("gk", [P, 1])
            g_sb = sb("g", [P, 1])
            ones = sb("ones", [P, P])
            ksq = sb("ksq", [P, GK, BS])
            krs = sb("krs", [P, GK, BS])
        k_ps = ps("k_ps", [P, GK, 256])
        v_ps = ps("v_ps", [P, GK, 256])
        unit_ps = ps("unit_ps", [P, 2, 1024])

        s_ctx = sem("ctx")
        s_small = sem("small")
        s_w = [sem(f"w{i}") for i in range(2)]
        s_g = sem("g")
        s_kproj = sem("kproj")
        s_vproj = sem("vproj")
        s_sq = sem("sq")
        s_ss = sem("ss")
        s_rs = sem("rs")
        s_rsl = sem("rsl")
        s_root = sem("root")
        s_k = sem("k")
        s_v = sem("v")
        s_aunit = sem("aunit")
        s_vunit = sem("vunit")
        s_acopy = sem("acopy")
        s_vcopy = sem("vcopy")
        s_astored = [sem(f"astored{i}") for i in range(2)]
        s_vstored = [sem(f"vstored{i}") for i in range(2)]

        wk_v = wk.rearrange("(c p) n -> p c n", p=P)
        wv_v = wv.rearrange("(c p) n -> p c n", p=P)
        wq_v = wq_t.rearrange("(h d) n -> d h n", d=DH)
        wo_v = wo.rearrange("(h d) n -> d h n", d=DH)
        block = ctx.enter_context(nc.Block())

        @block.sync
        def _(sp):
            sp.dma_start(ctx_sb[:], ctx_t.rearrange("(c p) n -> p c n", p=P)).then_inc(s_ctx, 16)

            def load_group(g, par):
                sp.dma_start(wk_sb[:, par], wk_v[:, :, bass.ds(g * cols, cols)]).then_inc(s_w[par], 16)
                sp.dma_start(wv_sb[:, par], wv_v[:, :, bass.ds(g * cols, cols)]).then_inc(s_w[par], 16)
                sp.dma_start(wq_sb[:, par], wq_v[:, bass.ds(g * HG, HG), :]).then_inc(s_w[par], 16)
                sp.dma_start(wo_sb[:, par], wo_v[:, bass.ds(g * HG, HG), :]).then_inc(s_w[par], 16)
            load_group(0, 0)
            load_group(1, 1)
            for par in range(2):
                sp.sem_inc(s_vstored[par], 64)
            for g in range(NG):
                sp.wait_ge(s_vcopy, HG * (g + 1) + 1)
                for b in range(B):
                    sp.dma_start(v_d[b, g * HG:(g + 1) * HG].rearrange("h s n -> s h n"),
                                 v_st[(b % 2) * S:(b % 2 + 1) * S, g % 2, b // 2]).then_inc(s_vstored[g % 2], 16)
                if g + 2 < NG:
                    sp.wait_ge(s_aunit, HG * (g + 1))
                    sp.wait_ge(s_vunit, HG * (g + 1))
                    load_group(g + 2, g % 2)
            for par in range(2):
                sp.wait_ge(s_vstored[par], 64 * (NG // 2 + 1))

        @block.tensor
        def _(pe):
            pe.wait_ge(s_ctx, 16)
            if normed:
                pe.wait_ge(s_g, 1)

            def group(i, par):
                g = 2 * i + par
                pe.wait_ge(s_w[par], 64 * (i + 1))
                pe.wait_ge(s_k, g + 1)
                for h in range(GK):
                    for c in range(CC):
                        mm = pe.matmul(k_ps[:, h, 0:BS], wk_sb[:, par, c, h * DH:(h + 1) * DH], ctx_sb[:, c, :],
                                       start=(c == 0), stop=(c == CC - 1))
                mm.then_inc(s_kproj, 1)
                pe.wait_ge(s_v, g + 1)
                for h in range(GK):
                    for c in range(CC):
                        mm = pe.matmul(v_ps[:, h, 0:BS], wv_sb[:, par, c, h * DH:(h + 1) * DH], ctx_sb[:, c, :],
                                       start=(c == 0), stop=(c == CC - 1))
                mm.then_inc(s_vproj, 1)
                if normed:
                    pe.wait_ge(s_sq, 2 * (g + 1))
                    for h in range(GK):
                        mm = pe.matmul(k_ps[:, h, 0:BS], ones[:], ksq[:, h, :], start=True, stop=True)
                    mm.then_inc(s_ss, 1)
                pe.wait_ge(s_v, g + 2)
                for u in range(HG):
                    pe.wait_ge(s_vcopy, HG * g + u + 1)
                    h = u // rep
                    for p in range(2):
                        mm = pe.matmul(unit_ps[:, 0, p * 512:(p + 1) * 512], vT[:, par, h, p * P:(p + 1) * P],
                                       wo_sb[:, par, u, :], start=True, stop=True)
                    mm.then_inc(s_vunit, 1)
                    if u == 0:
                        pe.wait_ge(s_k, g + 2)
                    pe.wait_ge(s_acopy, HG * g + u + 1)
                    for c in range(KC):
                        mm = pe.matmul(unit_ps[:, 1, c * BS:(c + 1) * BS], wq_sb[:, par, u, c * P:(c + 1) * P],
                                       kT[:, par, h, :], start=True, stop=True)
                    mm.then_inc(s_aunit, 1)
            with pe.Fori(0, NG // 2) as i:
                group(i, 0)
                group(i, 1)

        @block.scalar
        def _(act):
            act.sem_inc(s_acopy, 1)
            for par in range(2):
                act.sem_inc(s_astored[par], 64)

            def group(i, par):
                g = 2 * i + par
                if normed:
                    act.wait_ge(s_sq, 2 * g + 1)
                    act.wait_ge(s_rs, g + 1)
                    act.activation(ksq[:], k_ps[:, :, 0:BS], ACT.Square).then_inc(s_sq, 1)
                    act.wait_ge(s_rsl, 3 * g + 3)
                    act.activation(krs[:], krs[:], ACT.Sqrt).then_inc(s_root, 1)
                act.wait_ge(s_astored[par], 64 * (i + 1))
                for u in range(HG):
                    act.wait_ge(s_aunit, HG * g + u + 1)
                    act.activation(a_st[:, par, :, :, u * S:(u + 1) * S],
                                   unit_ps[:, 1, :].rearrange("p (c b s) -> p c b s", c=KC, b=B),
                                   ACT.Copy).then_inc(s_acopy, 1)
                act.wait_ge(s_acopy, HG * (g + 1) + 1)
                for b in range(B):
                    act.dma_start(a_d[b].rearrange("p (c n) -> p c n", c=KC)[:, :, bass.ds(g * HG * S, HG * S)],
                                  a_st[:, par, :, b, :]).then_inc(s_astored[par], 16)
            with act.Fori(0, NG // 2) as i:
                group(i, 0)
                group(i, 1)
            for par in range(2):
                act.wait_ge(s_astored[par], 64 * (NG // 2 + 1))

        @block.vector
        def _(dve):
            dve.sem_inc(s_vcopy, 1)
            dve.sem_inc(s_k, 1)
            dve.sem_inc(s_v, 1)
            dve.wait_ge(s_small, 32)
            if mask is not None:
                dve.tensor_copy(maskcol[:], mask_u8[:]).then_inc(s_rsl, 1)
            else:
                dve.memset(maskcol[:], 1.0).then_inc(s_rsl, 1)
            if normed:
                dve.sem_inc(s_rs, 1)
                dve.memset(ones[:], 1.0)
                dve.tensor_tensor(g_sb[:], gq_sb[:], gk_sb[:], ALU.mult).then_inc(s_g, 1)

            def group(i, par):
                g = 2 * i + par
                dve.wait_ge(s_kproj, g + 1)
                if normed:
                    dve.tensor_scalar(kT[:, par], k_ps[:, :, 0:BS], g_sb[:, 0:1], None, ALU.mult).then_inc(s_sq, 1)
                else:
                    dve.tensor_copy(kT[:, par], k_ps[:, :, 0:BS]).then_inc(s_k, 1)
                dve.wait_ge(s_vproj, g + 1)
                dve.tensor_copy(vT[:, par], v_ps[:, :, 0:BS]).then_inc(s_v, 1)
                if normed:
                    dve.wait_ge(s_ss, g + 1)
                    dve.tensor_scalar(krs[:], k_ps[:, :, 0:BS], 1.0 / DH, EPS, ALU.mult, ALU.add).then_inc(s_rsl, 1)
                    dve.wait_ge(s_rsl, 3 * g + 2)
                    dve.reciprocal(krs[:], krs[:]).then_inc(s_rsl, 1)
                    dve.wait_ge(s_root, g + 1)
                    dve.tensor_tensor(kT[:, par], kT[:, par], krs[:], ALU.mult).then_inc(s_rsl, 1)
                    dve.wait_ge(s_rsl, 3 * g + 4)
                    dve.sem_inc(s_rs, 1)
                    dve.sem_inc(s_k, 1)
                for u in range(HG):
                    dve.wait_ge(s_vunit, HG * g + u + 1)
                    if u == 0:
                        dve.wait_ge(s_vstored[par], 64 * (i + 1))
                        if not normed:
                            dve.wait_ge(s_rsl, 1)
                    dve.tensor_tensor(v_st[:, par, :, u, :], unit_ps[:, 0, :].rearrange("p (a n) -> p a n", a=2),
                                      maskcol[:].unsqueeze(2).to_broadcast([P, 2, D]), ALU.mult).then_inc(s_vcopy, 1)
            with dve.Fori(0, NG // 2) as i:
                group(i, 0)
                group(i, 1)

        @block.gpsimd
        def _(pool):
            if mask is not None:
                for p in range(2):
                    pool.dma_start(mask_u8[:, p:p + 1], mask[2 * p:2 * p + 2, :].rearrange("b (s o) -> (b s) o", o=1)
                                   ).then_inc(s_small, 16)
            else:
                pool.dma_start(gq_sb[:], gq.rearrange("(d o) -> d o", o=1)).then_inc(s_small, 16)
                pool.dma_start(gk_sb[:], gk.rearrange("(d o) -> d o", o=1)).then_inc(s_small, 16)


def moments(dve, sem, count, x, stats, mv, carrier):
    dve.bn_stats(stats, x).then_inc(sem, 1)
    dve.wait_ge(sem, count + 1)
    dve.memset(carrier, 0.0)
    dve.bn_aggr(mv, stats).then_inc(sem, 1)
    dve.wait_ge(sem, count + 2)
    dve.tensor_scalar(mv[:, 1:2], mv[:, 1:2], EPS, None, ALU.add).then_inc(sem, 1)


def attend(nc, tag, x_in, x_out, a_d, v_d, wq, mask, ident_d):
    normed = wq is not None
    with ExitStack() as ctx:
        sb, ps, sem = names(ctx, nc, tag)
        ident = sb("ident", [P, P])
        a_raw = sb("a_raw", [P, KC * HS])
        v_raw = sb("v_raw", [P, NQ * D])
        a_hi = sb("a_hi", [P, KC, HS], F32R)
        a_lo = sb("a_lo", [P, KC, HS], F32R)
        v_hi = sb("v_hi", [P, NQ, D], F32R)
        v_lo = sb("v_lo", [P, NQ, D], F32R)
        x = sb("x", [P, TB, D])
        xn = sb("xn", [P, D])
        stats = sb("stats", [P, 6])
        mv = sb("mv", [P, 2])
        carrier = sb("carrier", [P, 1])
        rstd = sb("rstd", [P, 1])
        power = sb("power", [P, 1])
        x_hi = sb("x_hi", [P, 2, KC, P], F32R)
        x_lo = sb("x_lo", [P, 2, KC, P], F32R)
        top = sb("top", [P, H])
        z = sb("z", [P, H, S])
        p_sb = sb("p", [P, H, S])
        total = sb("total", [P, H])
        recip = sb("recip", [P, H])
        p_hi = sb("p_hi", [P, NQ, P], F32R)
        p_lo = sb("p_lo", [P, NQ, P], F32R)
        y = sb("y", [P, D])
        if normed:
            wq_hi = sb("wq_hi", [P, KC, H * DH], F32R)
            wq_lo = sb("wq_lo", [P, KC, H * DH], F32R)
            qsq = sb("qsq", [P, 512])
            ssq = sb("ssq", [P, H])
            rq = sb("rq", [P, H])
        if mask is not None:
            mask_u8 = sb("mask_u8", [1, BS], U8)
            maskf = sb("maskf", [1, B, S])
            bias = sb("bias", [1, B, HS], F32R)
            one_f = sb("one_f", [1, P])
            one_row = sb("one_row", [1, P], F32R)
        xt_ps = ps("xt_ps", [P, KC, P])
        s_ps = ps("s_ps", [P, H, S])
        pt_ps = ps("pt_ps", [P, NQ, P])
        o_ps = ps("o_ps", [P, D])
        NQG = H * DH // 512
        if normed:
            q_ps = ps("q_ps", [P, 2, 512])

        s_id = sem("id")
        s_araw = sem("araw")
        s_vraw = sem("vraw")
        s_ahi = sem("ahi")
        s_alo = sem("alo")
        s_vhi = sem("vhi")
        s_vlo = sem("vlo")
        s_x = [sem(f"x{i}") for i in range(TB)]
        s_ln = sem("ln")
        s_rstd = sem("rstd")
        s_xn = sem("xn")
        s_xt = sem("xt")
        s_xhi = sem("xhi")
        s_xlo = sem("xlo")
        s_scores = sem("scores")
        s_top = sem("top")
        s_sub = sem("sub")
        s_zq = sem("zq")
        s_exp = sem("exp")
        s_sum = sem("sum")
        s_rec = sem("rec")
        s_prob = sem("prob")
        s_pt = sem("pt")
        s_phi = sem("phi")
        s_plo = sem("plo")
        s_o = sem("o")
        s_y = sem("y")
        s_store = sem("store")
        s_q = sem("q")
        s_qsq = sem("qsq")
        s_qsum = sem("qsum")
        s_rq = sem("rq")
        s_rqp = sem("rqp")
        s_wqa = sem("wqa")
        s_wqv = sem("wqv")
        s_wqhi = sem("wqhi")
        s_wqlo = sem("wqlo")
        s_mask = sem("mask")
        s_bias = sem("bias")

        block = ctx.enter_context(nc.Block())

        @block.sync
        def _(sp):
            sp.dma_start(ident[:], ident_d).then_inc(s_id, 16)
            for t in range(TB):
                sp.dma_start(x[:, t], x_in[t * P:(t + 1) * P, :]).then_inc(s_x[t], 16)
            sp.sem_inc(s_store, 16)
            if mask is not None:
                sp.dma_start(mask_u8[:], mask.rearrange("(o b) s -> o (b s)", o=1)).then_inc(s_mask, 16)
            if normed:
                for c in range(KC):
                    if c >= 2:
                        sp.wait_ge(s_wqlo, c - 1)
                    stage, landed = ((a_raw, s_wqa), (v_raw, s_wqv))[c % 2]
                    sp.dma_start(stage[:, 0:H * DH], wq[c * P:(c + 1) * P, :]).then_inc(landed, 16)
                sp.wait_ge(s_wqlo, KC)
            sp.dma_start(a_raw[:], a_d[0]).then_inc(s_araw, 16)
            sp.dma_start(v_raw[:].rearrange("p (q n) -> p q n", q=NQ),
                         v_d[0].rearrange("(q a) s n -> (a s) q n", a=2)).then_inc(s_vraw, 16)

            def batch(b, last):
                for j in range(TB):
                    if j == 0 and not last:
                        sp.wait_ge(s_alo, b + 1)
                        sp.dma_start(a_raw[:], a_d[bass.ds(b + 1, 1)].rearrange("b p n -> p (b n)")).then_inc(
                            s_araw, 16)
                        sp.wait_ge(s_vlo, b + 1)
                        sp.dma_start(v_raw[:].rearrange("p (q n) -> p q n", q=NQ),
                                     v_d[bass.ds(b + 1, 1)].rearrange("b (q a) s n -> (a s) (b q) n", a=2)
                                     ).then_inc(s_vraw, 16)
                    t = TB * b + j
                    sp.wait_ge(s_y, t + 2)
                    sp.dma_start(x_out[bass.ds(t * P, P), :], y[:]).then_inc(s_store, 16)
                    if not last:
                        sp.dma_start(x[:, j], x_in[bass.ds((t + TB) * P, P), :]).then_inc(s_x[j], 16)
            with sp.Fori(0, B - 1) as b:
                batch(b, False)
            batch(B - 1, True)
            sp.wait_ge(s_store, 16 * (NT + 1))

        @block.tensor
        def _(pe):
            def transposes(t):
                pe.wait_ge(s_xn, t + 1)
                pe.wait_ge(s_xlo, t + 1)
                for c in range(KC):
                    mm = pe.transpose(xt_ps[:, c, :], xn[:, c * P:(c + 1) * P], ident[:])
                mm.then_inc(s_xt, 1)

            def queries(t, j):
                pe.wait_ge(s_xlo, t + 2)
                for n in range(NQG):
                    pe.wait_ge(s_qsq, NQG * t + n + 1)
                    for c in range(KC):
                        mm = matmul3(pe, q_ps[:, n % 2, :], x_hi[:, j % 2, c, :], x_lo[:, j % 2, c, :],
                                     wq_hi[:, c, n * 512:(n + 1) * 512], wq_lo[:, c, n * 512:(n + 1) * 512],
                                     c == 0, c == KC - 1)
                    mm.then_inc(s_q, 1)

            def scores(t, j, b, half):
                if half == 0:
                    pe.wait_ge(s_xlo, t + 2)
                    pe.wait_ge(s_sub, t + 1)
                    if j == 0:
                        pe.wait_ge(s_alo, b + 1)
                out = s_ps[:, half * 8:(half + 1) * 8, :]
                cols = slice(half * 512, (half + 1) * 512)
                for c in range(KC):
                    mm = matmul3(pe, out, x_hi[:, j % 2, c, :], x_lo[:, j % 2, c, :], a_hi[:, c, cols],
                                 a_lo[:, c, cols], c == 0, c == KC - 1 and mask is None)
                if mask is not None:
                    mm = pe.matmul(out, one_row[:],
                                   bias[:, bass.ds(b, 1), cols].rearrange("o b n -> o (b n)"), start=False, stop=True)
                mm.then_inc(s_scores, 1)

            def prob_transposes(t):
                pe.wait_ge(s_prob, t + 1)
                pe.wait_ge(s_plo, t + 1)
                for q in range(NQ):
                    mm = pe.transpose(pt_ps[:, q, :], p_sb[:, 2 * q:2 * q + 2, :].rearrange("p a s -> p (a s)"),
                                      ident[:])
                mm.then_inc(s_pt, 1)

            def outputs(t, j, b):
                pe.wait_ge(s_plo, t + 2)
                pe.wait_ge(s_y, t + 1)
                if j == 0:
                    pe.wait_ge(s_vlo, b + 1)
                for q in range(NQ):
                    mm = matmul3(pe, o_ps[:], p_hi[:, q, :], p_lo[:, q, :], v_hi[:, q, :], v_lo[:, q, :],
                                 q == 0, q == NQ - 1)
                mm.then_inc(s_o, 1)

            def step(b, j, left=TB):
                t = TB * b + j
                jn, bn = (j + 1) % TB, b + (j + 1) // TB
                if left >= 2:
                    if normed:
                        queries(t + 1, jn)
                    scores(t + 1, jn, bn, 0)
                prob_transposes(t)
                if left >= 2:
                    scores(t + 1, jn, bn, 1)
                if left >= 3:
                    transposes(t + 2)
                outputs(t, j, b)

            pe.wait_ge(s_id, 16)
            transposes(0)
            if normed:
                pe.wait_ge(s_wqlo, KC)
                queries(0, 0)
            transposes(1)
            if mask is not None:
                pe.wait_ge(s_bias, 4)
            scores(0, 0, 0, 0)
            scores(0, 0, 0, 1)
            with pe.Fori(0, B - 1) as b:
                for j in range(TB):
                    step(b, j)
            for j in range(TB):
                step(B - 1, j, TB - j)

        @block.scalar
        def _(act):
            def split_x(t, j):
                act.wait_ge(s_xt, t + 1)
                if not isinstance(t, int) or t >= 2:
                    act.wait_ge(s_scores, 2 * (t - 1))
                act.activation(x_hi[:, j % 2], xt_ps[:], ACT.Copy).then_inc(s_xhi, 1)

            def query_squares(t):
                for n in range(NQG):
                    act.wait_ge(s_q, NQG * t + n + 1)
                    act.wait_ge(s_qsum, NQG * t + n + 1)
                    act.activation(qsq[:], q_ps[:, n % 2, :], ACT.Square).then_inc(s_qsq, 1)

            def split_a(b):
                act.wait_ge(s_araw, 16 * (b + 1))
                after(act, s_scores, 2 * TB * b)
                act.activation(a_hi[:], a_raw[:].rearrange("p (c n) -> p c n", c=KC), ACT.Copy).then_inc(s_ahi, 1)

            def split_v(b):
                act.wait_ge(s_vraw, 16 * (b + 1))
                after(act, s_o, TB * b + 1)
                act.activation(v_hi[:], v_raw[:].rearrange("p (q n) -> p q n", q=NQ), ACT.Copy).then_inc(s_vhi, 1)

            def exps(t):
                if normed:
                    act.wait_ge(s_zq, t + 1)
                else:
                    act.wait_ge(s_sub, t + 2)
                act.wait_ge(s_pt, t + 1)
                act.activation(p_sb[:], z[:], ACT.Exp, scale=1.0 if normed else SCALE).then_inc(s_exp, 1)

            def split_p(t):
                act.wait_ge(s_pt, t + 2)
                act.wait_ge(s_o, t + 1)
                act.activation(p_hi[:], pt_ps[:], ACT.Copy).then_inc(s_phi, 1)

            def step(b, j, left=TB):
                t = TB * b + j
                if normed and left >= 2:
                    query_squares(t + 1)
                split_p(t)
                if left >= 3:
                    split_x(t + 2, (j + 2) % TB)
                if left >= 2:
                    exps(t + 1)
                if left == TB and j == TB - 2:
                    split_a(b + 1)
                if left == TB and j == TB - 1:
                    split_v(b + 1)

            if normed:
                act.sem_inc(s_qsq, 2)
                for c in range(KC):
                    stage, landed = ((a_raw, s_wqa), (v_raw, s_wqv))[c % 2]
                    act.wait_ge(landed, 16 * (c // 2 + 1))
                    act.activation(wq_hi[:, c, :], stage[:, 0:H * DH], ACT.Copy).then_inc(s_wqhi, 1)
            split_x(0, 0)
            if normed:
                query_squares(0)
            split_a(0)
            split_x(1, 1)
            split_v(0)
            exps(0)
            with act.Fori(0, B - 1) as b:
                for j in range(TB):
                    step(b, j)
            for j in range(TB):
                step(B - 1, j, TB - j)

        @block.vector
        def _(dve):
            def norm_start(t, j, b):
                dve.wait_ge(s_x[j], 16 * (b + 1))
                moments(dve, s_ln, 3 * t, x[:, j, :], stats[:], mv[:], carrier[:])

            def norm_end(t, j):
                dve.wait_ge(s_rstd, t + 2)
                after(dve, s_xt, t)
                dve.tensor_scalar(xn[:], x[:, j, :], mv[:, 0:1], rstd[:, 0:1], ALU.subtract, ALU.mult).then_inc(
                    s_xn, 1)

            def split_x(t, j):
                dve.wait_ge(s_xhi, t + 1)
                dve.tensor_tensor(x_lo[:, j % 2], xt_ps[:], x_hi[:, j % 2].bitcast(F32), ALU.subtract).then_inc(
                    s_xlo, 1)

            def query_sums(t):
                for n in range(NQG):
                    dve.wait_ge(s_qsq, NQG * t + n + 3)
                    if n == 0:
                        after(dve, s_rq, t)
                    dve.tensor_reduce(ssq[:, 4 * n:4 * n + 4], qsq[:].rearrange("p (h d) -> p h d", d=DH), AX,
                                      ALU.add).then_inc(s_qsum, 1)
                dve.wait_ge(s_qsum, NQG * (t + 1) + 1)
                after(dve, s_zq, t)
                dve.tensor_scalar(rq[:], ssq[:], DH * EPS, None, ALU.add).then_inc(s_rq, 1)

            def split_a(b):
                dve.wait_ge(s_ahi, b + 1)
                dve.tensor_tensor(a_lo[:], a_raw[:].rearrange("p (c n) -> p c n", c=KC), a_hi[:].bitcast(F32),
                                  ALU.subtract).then_inc(s_alo, 1)

            def split_v(b):
                dve.wait_ge(s_vhi, b + 1)
                dve.tensor_tensor(v_lo[:], v_raw[:].rearrange("p (q n) -> p q n", q=NQ), v_hi[:].bitcast(F32),
                                  ALU.subtract).then_inc(s_vlo, 1)

            def shift(t):
                dve.wait_ge(s_scores, 2 * (t + 1))
                dve.tensor_reduce(top[:], s_ps[:], AX, ALU.max).then_inc(s_top, 1)
                dve.wait_ge(s_top, t + 1)
                after(dve, s_exp, t)
                dve.tensor_tensor(z[:], s_ps[:], top[:].unsqueeze(2).to_broadcast([P, H, S]),
                                  ALU.subtract).then_inc(s_sub, 1)

            def sums(t):
                dve.wait_ge(s_exp, t + 1)
                dve.tensor_reduce(total[:], p_sb[:], AX, ALU.add).then_inc(s_sum, 1)
                dve.wait_ge(s_sum, t + 1)
                after(dve, s_prob, t)
                dve.reciprocal(recip[:], total[:]).then_inc(s_rec, 1)

            def split_p(t):
                dve.wait_ge(s_phi, t + 1)
                dve.tensor_tensor(p_lo[:], pt_ps[:], p_hi[:].bitcast(F32), ALU.subtract).then_inc(s_plo, 1)

            def add_output(t, j):
                dve.wait_ge(s_o, t + 2)
                dve.wait_ge(s_store, 16 * (t + 1))
                dve.tensor_tensor(y[:], x[:, j, :], o_ps[:], ALU.add).then_inc(s_y, 1)

            def step(b, j, left=TB):
                t = TB * b + j
                if normed and left >= 2:
                    query_sums(t + 1)
                split_p(t)
                if left >= 2:
                    shift(t + 1)
                if left >= 3:
                    split_x(t + 2, (j + 2) % TB)
                if left >= 4:
                    norm_start(t + 3, (j + 3) % TB, b + (j + 3) // TB)
                if left >= 2:
                    sums(t + 1)
                if left >= 4:
                    norm_end(t + 3, (j + 3) % TB)
                if left >= TB and j == TB - 2:
                    split_a(b + 1)
                add_output(t, j)
                if left >= TB and j == TB - 1:
                    split_v(b + 1)

            for s in (s_xlo, s_sub, s_pt, s_plo, s_o, s_y):
                dve.sem_inc(s, 1)
            norm_start(0, 0, 0)
            norm_end(0, 0)
            if normed:
                dve.sem_inc(s_qsum, 1)
                for c in range(KC):
                    dve.wait_ge(s_wqhi, c + 1)
                    dve.tensor_tensor(wq_lo[:, c, :], (a_raw, v_raw)[c % 2][:, 0:H * DH],
                                      wq_hi[:, c, :].bitcast(F32), ALU.subtract).then_inc(s_wqlo, 1)
            if mask is not None:
                dve.wait_ge(s_mask, 16)
                dve.memset(one_f[:], 1.0).then_inc(s_bias, 1)
                dve.tensor_copy(maskf[:].rearrange("o b s -> o (b s)"), mask_u8[:]).then_inc(s_bias, 1)
                dve.wait_ge(s_bias, 2)
                dve.tensor_copy(one_row[:], one_f[:]).then_inc(s_bias, 1)
                for b in range(B):
                    ins = dve.tensor_scalar(bias[:, b].rearrange("o (h s) -> o h s", h=H),
                                            maskf[:, b:b + 1, :].to_broadcast([1, H, S]), -MASKED, MASKED,
                                            ALU.mult, ALU.add)
                ins.then_inc(s_bias, 1)
            split_x(0, 0)
            norm_start(1, 1, 0)
            norm_end(1, 1)
            if normed:
                query_sums(0)
            split_a(0)
            split_x(1, 1)
            norm_start(2, 2, 0)
            norm_end(2, 2)
            split_v(0)
            shift(0)
            sums(0)
            with dve.Fori(0, B - 1) as b:
                for j in range(TB):
                    step(b, j)
            for j in range(TB):
                step(B - 1, j, TB - j)

        @block.gpsimd
        def _(pool):
            def power_half(t):
                pool.wait_ge(s_ln, 3 * (t + 1))
                after(pool, s_xn, t)
                pool.tensor_tensor(rstd[:], mv[:, 1:2], power[:], ALU.pow).then_inc(s_rstd, 1)

            def query_factors(t):
                pool.wait_ge(s_rq, t + 1)
                pool.tensor_tensor(rq[:], rq[:], power[:].to_broadcast([P, H]), ALU.pow).then_inc(s_rqp, 1)

            def scale_scores(t):
                pool.wait_ge(s_rqp, t + 1)
                pool.wait_ge(s_sub, t + 2)
                pool.tensor_tensor(z[:], z[:], rq[:].unsqueeze(2).to_broadcast([P, H, S]), ALU.mult).then_inc(s_zq, 1)

            def normalise(t):
                pool.wait_ge(s_rec, t + 1)
                pool.tensor_tensor(p_sb[:], p_sb[:], recip[:].unsqueeze(2).to_broadcast([P, H, S]),
                                   ALU.mult).then_inc(s_prob, 1)

            def step(b, j, left=TB):
                t = TB * b + j
                if left >= 2:
                    if normed:
                        query_factors(t + 1)
                        scale_scores(t + 1)
                    if left >= 4:
                        power_half(t + 3)
                    normalise(t + 1)

            pool.memset(power[:], -0.5).then_inc(s_rstd, 1)
            pool.wait_ge(s_rstd, 1)
            power_half(0)
            power_half(1)
            if normed:
                query_factors(0)
            power_half(2)
            if normed:
                scale_scores(0)
            normalise(0)
            with pool.Fori(0, B - 1) as b:
                for j in range(TB):
                    step(b, j)
            for j in range(TB):
                step(B - 1, j, TB - j)


def gate(nc, tag, x_in, xn_all, logits_ps, gate_t, ident_d, load_weights, w_d):
    with ExitStack() as ctx:
        sb, ps, sem = names(ctx, nc, tag)
        ident = sb("ident", [P, P])
        gate_sb = sb("gate", [P, KC, E])
        x = sb("x", [P, 2, D])
        xn = sb("xn", [P, 2, D])
        stats = sb("stats", [P, 6])
        mv = sb("mv", [P, 2])
        carrier = sb("carrier", [P, 1])
        rstd = sb("rstd", [P, 1])
        power = sb("power", [P, 1])
        xT = sb("xT", [P, 2, KC, P])
        xt_ps = ps("xt_ps", [P, 2, KC, P])
        s_const = sem("const")
        s_x = [sem(f"x{i}") for i in range(2)]
        s_ln = sem("ln")
        s_rstd = sem("rstd")
        s_xn = sem("xn")
        s_keep = sem("keep")
        s_xt = sem("xt")
        s_xT = sem("xT")
        s_gate = sem("gate")
        block = ctx.enter_context(nc.Block())

        @block.sync
        def _(sp):
            sp.dma_start(ident[:], ident_d).then_inc(s_const, 16)
            sp.dma_start(gate_sb[:], gate_t.rearrange("(c p) e -> p c e", p=P)).then_inc(s_const, 16)
            with sp.Fori(0, NT // 2) as i:
                for par in range(2):
                    t = 2 * i + par
                    sp.wait_ge(s_xn, t + 1)
                    sp.dma_start(x[:, par], x_in[bass.ds(t * P, P), :]).then_inc(s_x[par], 16)

        @block.vector
        def _(dve):
            for s in (s_xn, s_keep, s_xt, s_xT, s_gate):
                dve.sem_inc(s, 2)
            dve.memset(w_d[0:LAP, :, FC - 1, :], 0.0)
            with dve.Fori(0, NT // 2) as i:
                for par in range(2):
                    t = 2 * i + par
                    dve.wait_ge(s_x[par], 16 * (i + 1))
                    dve.wait_ge(s_xt, t + 1)
                    dve.wait_ge(s_keep, t + 1)
                    moments(dve, s_ln, 3 * t, x[:, par, :], stats[:], mv[:], carrier[:])
                    dve.wait_ge(s_rstd, t + 2)
                    dve.tensor_scalar(xn[:, par, :], x[:, par, :], mv[:, 0:1], rstd[:, 0:1], ALU.subtract,
                                      ALU.mult).then_inc(s_xn, 1)

        @block.gpsimd
        def _(pool):
            pool.memset(power[:], -0.5).then_inc(s_rstd, 1)
            pool.wait_ge(s_rstd, 1)
            with pool.Fori(0, NT // 2) as i:
                for par in range(2):
                    t = 2 * i + par
                    pool.wait_ge(s_ln, 3 * (t + 1))
                    pool.wait_ge(s_xn, t + 2)
                    pool.tensor_tensor(rstd[:], mv[:, 1:2], power[:], ALU.pow).then_inc(s_rstd, 1)
                    pool.wait_ge(s_xn, t + 3)
                    pool.tensor_copy(xn_all[:, bass.ds(t, 1), :].rearrange("p t n -> p (t n)"),
                                     xn[:, par, :]).then_inc(s_keep, 1)

        @block.scalar
        def _(act):
            load_weights(act)
            with act.Fori(0, NT // 2) as i:
                for par in range(2):
                    t = 2 * i + par
                    act.wait_ge(s_xt, t + 3)
                    act.wait_ge(s_gate, t + 1)
                    act.activation(xT[:, par], xt_ps[:, par], ACT.Copy).then_inc(s_xT, 1)

        @block.tensor
        def _(pe):
            pe.wait_ge(s_const, 32)
            with pe.Fori(0, NT // 2) as i:
                for par in range(2):
                    t = 2 * i + par
                    pe.wait_ge(s_xn, t + 3)
                    pe.wait_ge(s_xT, t + 1)
                    for c in range(KC):
                        mm = pe.transpose(xt_ps[:, par, c, :], xn[:, par, c * P:(c + 1) * P], ident[:])
                    mm.then_inc(s_xt, 1)
                    pe.wait_ge(s_xT, t + 3)
                    for c in range(KC):
                        mm = pe.matmul(logits_ps[:, bass.ds(t * E, E)], xT[:, par, c, :], gate_sb[:, c, :],
                                       start=(c == 0), stop=(c == KC - 1))
                    mm.then_inc(s_gate, 1)


def route(nc, tag, logits_ps, weight, slot, block_expert):
    with ExitStack() as ctx:
        sb, ps, sem = names(ctx, nc, tag)
        logits = sb("logits", [P, NT, E])
        best = sb("best", [P, NT])
        probs = sb("probs", [P, NT, E])
        left = sb("left", [P, NT, E])
        equal = sb("equal", [P, NT, E])
        chosen = sb("chosen", [P, 2, NT, E])
        padded = sb("padded", [P, 2 * NT - 1, E])
        rank_code = sb("rank_code", [P, E])
        earlier = sb("earlier", [P, P])
        ones = sb("ones", [P, P])
        count = sb("count", [P, E])
        count_i = sb("count_i", [P, E], I32)
        rest = sb("rest", [P, E])
        ends = [sb(f"ends{i}", [P, E]) for i in range(2)]
        row = sb("row", [P, NT, E])
        slot_f = sb("slot_f", [P, 2, NT])
        block_start = sb("block_start", [1, MAX_BLOCKS + 1])
        past = sb("past", [1, MAX_BLOCKS + 1, E])
        expert_f = sb("expert_f", [1, MAX_BLOCKS + 1])
        rank_ps = ps("rank_ps", [P, NT, E])
        count_ps = ps("count_ps", [P, E])
        s_const = sem("const")
        s_step = sem("step")
        s_shift = sem("shift")
        s_exp = sem("exp")
        s_either = sem("either")
        s_rank = sem("rank")
        block = ctx.enter_context(nc.Block())

        @block.gpsimd
        def _(pool):
            pool.iota(rank_code[:], [[-1, E]], base=E, channel_multiplier=0,
                      allow_small_or_imprecise_dtypes=True).then_inc(s_const, 1)
            pool.iota(block_start[:], [[P, MAX_BLOCKS + 1]], base=0, channel_multiplier=0,
                      allow_small_or_imprecise_dtypes=True).then_inc(s_const, 1)
            pool.memset(ones[:], 1.0).then_inc(s_const, 1)
            pool.wait_ge(s_const, 3)
            pool.affine_select(out=earlier[:], in_=ones[:], compare_op=ALU.is_gt, fill=0.0, base=0,
                               pattern=[[1, P]], channel_multiplier=-1).then_inc(s_const, 1)

        @block.scalar
        def _(act):
            act.wait_ge(s_shift, 1)
            act.activation(probs[:], left[:], ACT.Exp).then_inc(s_exp, 1)

        @block.tensor
        def _(pe):
            pe.wait_ge(s_const, 4)
            pe.wait_ge(s_either, 1)
            pe.matmul(rank_ps[:], earlier[:], padded[:, NT - 1:, :], start=True, stop=False)
            for d in range(1, NT):
                pe.matmul(rank_ps[:], ones[:], padded[:, NT - 1 - d:2 * NT - 1 - d, :], start=False,
                          stop=(d == NT - 1))
            for t in range(NT):
                mm = pe.matmul(count_ps[:], ones[:], padded[:, NT - 1 + t, :], start=(t == 0), stop=(t == NT - 1))
            mm.then_inc(s_rank, 1)

        @block.vector
        def _(dve):
            step = Chain(dve, s_step)

            def over_experts(a):
                return a.unsqueeze(2).to_broadcast([P, NT, E])
            codes = rank_code[:].unsqueeze(1).to_broadcast([P, NT, E])
            step(dve.memset(padded[:, 0:NT - 1, :], 0.0))
            step(dve.tensor_copy(logits[:].rearrange("p t e -> p (t e)"), logits_ps[:, 0:NT * E]))
            step(dve.tensor_reduce(best[:], logits[:], AX, ALU.max))
            dve.tensor_tensor(left[:], logits[:], over_experts(best[:]), ALU.subtract).then_inc(s_shift, 1)
            dve.wait_ge(s_exp, 1)
            step(dve.tensor_reduce(best[:], probs[:], AX, ALU.add))
            step(dve.reciprocal(best[:], best[:]))
            step(dve.tensor_tensor(probs[:], probs[:], over_experts(best[:]), ALU.mult))
            dve.wait_ge(s_const, 4)
            scores = probs
            for k in range(2):
                step(dve.tensor_reduce(weight[:, k], scores[:], AX, ALU.max))
                step(dve.tensor_tensor(equal[:], scores[:], over_experts(weight[:, k]), ALU.is_equal))
                step(dve.tensor_tensor(equal[:], equal[:], codes, ALU.mult))
                step(dve.tensor_reduce(best[:], equal[:], AX, ALU.max))
                step(dve.tensor_tensor(chosen[:, k], codes, over_experts(best[:]), ALU.is_equal))
                if k == 0:
                    step(dve.scalar_tensor_tensor(left[:], chosen[:, 0], -4.0, probs[:], ALU.mult, ALU.add))
                    scores = left
            dve.tensor_tensor(padded[:, NT - 1:, :], chosen[:, 0], chosen[:, 1], ALU.add).then_inc(s_either, 1)
            dve.wait_ge(s_rank, 1)
            step(dve.tensor_scalar(count[:], count_ps[:], float(P - 1), None, ALU.add))
            step(dve.tensor_copy(count_i[:], count[:]))
            step(dve.tensor_scalar(count_i[:], count_i[:], ~(P - 1) & 0xffff, None, ALU.bitwise_and))
            step(dve.tensor_copy(count[:], count_i[:]))
            step(dve.tensor_copy(ends[0][:], count[:]))
            src = 0
            for d in (1, 2, 4):
                step(dve.tensor_copy(ends[1 - src][:, 0:d], ends[src][:, 0:d]))
                step(dve.tensor_tensor(ends[1 - src][:, d:E], ends[src][:, d:E], ends[src][:, 0:E - d], ALU.add))
                src = 1 - src
            end = ends[src]
            step(dve.tensor_tensor(past[:], end[0:1, :].unsqueeze(1).to_broadcast([1, MAX_BLOCKS + 1, E]),
                                   block_start[:].unsqueeze(2).to_broadcast([1, MAX_BLOCKS + 1, E]), ALU.is_le))
            step(dve.tensor_reduce(expert_f[:], past[:], AX, ALU.add))
            step(dve.tensor_scalar(expert_f[:], expert_f[:], float(E - 1), None, ALU.min))
            step(dve.tensor_copy(block_expert[:], expert_f[:]))
            step(dve.tensor_tensor(rest[:], end[:], count[:], ALU.subtract))
            step(dve.tensor_tensor(row[:], rank_ps[:], rest[:].unsqueeze(1).to_broadcast([P, NT, E]), ALU.add))
            for k in range(2):
                step(dve.tensor_tensor(equal[:], row[:], chosen[:, k], ALU.mult))
                step(dve.tensor_reduce(slot_f[:, k], equal[:], AX, ALU.add))
            step(dve.tensor_copy(slot[:], slot_f[:]))


def expert_blocks(nc, tag, shared, w_gu, w_d, src_tile, res_tile, out_tile, count, ident_d, block_expert,
                  weights_landed, extra_pool=None, load_weights=None):
    per = NJ if shared else 1
    total = count * per
    with ExitStack() as ctx:
        sb, ps, sem = names(ctx, nc, tag)
        ident = sb("ident", [P, P])
        src = sb("src", [P, 2, D])
        xT = sb("xT", [P, 2, KC, P])
        act_gate = sb("act_gate", [P, 2, F])
        hidden = sb("hidden", [P, 2, F])
        hT = sb("hT", [P, FC, P])
        y = sb("y", [P, 2, D])
        res = sb("res", [P, 2, D]) if shared else None
        xt_ps = ps("xt_ps", [P, KC, P])
        gu_ps = ps("gu_ps", [P, 2, 2, 512])
        ht_ps = ps("ht_ps", [P, FC, P])
        y_ps = ps("y_ps", [P, 2, D])
        s_id = sem("id")
        s_src = [sem(f"src{i}") for i in range(2)]
        s_res = [sem(f"res{i}") for i in range(2)]
        s_xt = sem("xt")
        s_xT = sem("xT")
        s_gu = sem("gu")
        s_gate = sem("gate")
        s_h = sem("h")
        s_ht = sem("ht")
        s_hT = sem("hT")
        s_down = sem("down")
        s_y = sem("y")
        s_store = [sem(f"store{i}") for i in range(2)]
        block = ctx.enter_context(nc.Block())
        loops = (total - 1) // (2 * per)

        def stream(eng, step):
            with eng.Fori(0, loops) as i:
                for u in range(2 * per):
                    step(2 * per * i + u, u, 2 * i + u // per, i, True)
            for n in range(2 * per * loops, total):
                step(n, n % (2 * per), n // per, loops, n + 1 < total)

        @block.sync
        def _(sp):
            sp.dma_start(ident[:], ident_d).then_inc(s_id, 16)
            if load_weights is not None:
                load_weights(sp)
            for par in range(2):
                sp.sem_inc(s_store[par], 16)
                sp.dma_start(src[:, par], src_tile(par)).then_inc(s_src[par], 16)
                if shared:
                    sp.dma_start(res[:, par], res_tile(par)).then_inc(s_res[par], 16)

            def tile(m, par, more):
                if more:
                    sp.wait_ge(s_xt, m + 3)
                    sp.dma_start(src[:, par], src_tile(m + 2)).then_inc(s_src[par], 16)
                sp.wait_ge(s_y, m + 3)
                sp.dma_start(out_tile(m), y[:, par]).then_inc(s_store[par], 16)
                if more and shared:
                    sp.dma_start(res[:, par], res_tile(m + 2)).then_inc(s_res[par], 16)
            with sp.Fori(0, (count - 2) // 2) as i:
                for par in range(2):
                    tile(2 * i + par, par, True)
            for m in range((count - 2) // 2 * 2, count):
                tile(m, m % 2, m + 2 < count)
            for par in range(2):
                sp.wait_ge(s_store[par], 16 * ((count + 1 - par) // 2 + 1))

        @block.tensor
        def _(pe):
            def transposes(m, par, i):
                pe.wait_ge(s_src[par], 16 * (i + 1))
                pe.wait_ge(s_xT, m + 1)
                for c in range(KC):
                    mm = pe.transpose(xt_ps[:, c, :], src[:, par, c * P:(c + 1) * P], ident[:])
                mm.then_inc(s_xt, 1)

            def weights(n, u):
                if shared:
                    return slice(E - NJ + u % NJ, E - NJ + u % NJ + 1)
                return bass.ds(pe.value_load(block_expert[0:1, bass.ds(n, 1)], min_val=0, max_val=E - 1), 1)

            def gate_up(n, u, m, e):
                pe.wait_ge(s_xT, m + 2)
                pe.wait_ge(s_h, n + 1)
                for k in range(2):
                    for c in range(KC):
                        mm = pe.matmul(gu_ps[:, u % 2, k, 0:F], xT[:, (u // per) % 2, c, :],
                                       w_gu[:, e, c, k * F:(k + 1) * F].rearrange("p e n -> p (e n)"),
                                       start=(c == 0), stop=(c == KC - 1))
                mm.then_inc(s_gu, 1)

            def hidden_transposes(n, u):
                pe.wait_ge(s_h, n + 3)
                pe.wait_ge(s_hT, n + 1)
                for j in range(FC):
                    f0 = min(j * P, F - P)
                    mm = pe.transpose(ht_ps[:, j, :], hidden[:, u % 2, f0:f0 + P], ident[:])
                mm.then_inc(s_ht, 1)

            def down(n, u, m, e):
                pe.wait_ge(s_hT, n + 2)
                if u % per == 0:
                    pe.wait_ge(s_y, m + 1)
                for j in range(FC):
                    mm = pe.matmul(y_ps[:, (u // per) % 2, :], hT[:, j, :],
                                   w_d[:, e, j, :].rearrange("p e n -> p (e n)"),
                                   start=(u % per == 0 and j == 0), stop=(u % per == per - 1 and j == FC - 1))
                mm.then_inc(s_down, 1)

            def step(n, u, m, i, more):
                if more:
                    un = (u + 1) % (2 * per)
                    mn, i_next = (m + (u % per + 1) // per), (i + (u + 1) // (2 * per))
                    if un % per == 0:
                        transposes(mn, un // per, i_next)
                    gate_up(n + 1, un, mn, weights(n + 1, un))
                hidden_transposes(n, u)
                down(n, u, m, weights(n, u))

            pe.wait_ge(s_id, 16)
            transposes(0, 0, 0)
            for s, value in weights_landed:
                pe.wait_ge(s, value)
            gate_up(0, 0, 0, weights(0, 0))
            stream(pe, step)

        @block.scalar
        def _(act):
            def split(m, par):
                act.wait_ge(s_xt, m + 3)
                act.wait_ge(s_gu, per * m + per)
                act.activation(xT[:, par], xt_ps[:], ACT.Copy).then_inc(s_xT, 1)

            def silu(n, u):
                act.wait_ge(s_gu, n + 1 + 2 * per)
                act.wait_ge(s_h, n + 1)
                act.activation(act_gate[:, u % 2], gu_ps[:, u % 2, 0, 0:F], ACT.Silu).then_inc(s_gate, 1)

            def step(n, u, m, i, more):
                if more:
                    un = (u + 1) % (2 * per)
                    if un % per == 0:
                        split(m + 1, un // per)
                act.wait_ge(s_ht, n + 3)
                act.wait_ge(s_down, n + 1)
                act.activation(hT[:], ht_ps[:], ACT.Copy).then_inc(s_hT, 1)
                if more:
                    silu(n + 1, (u + 1) % (2 * per))
            act.sem_inc(s_gu, 2 * per)
            act.sem_inc(s_hT, 1)
            split(0, 0)
            silu(0, 0)
            stream(act, step)

        @block.vector
        def _(dve):
            def product(n, u):
                dve.wait_ge(s_gate, n + 1)
                dve.wait_ge(s_ht, n + 1)
                dve.tensor_tensor(hidden[:, u % 2], act_gate[:, u % 2], gu_ps[:, u % 2, 1, 0:F],
                                  ALU.mult).then_inc(s_h, 1)

            def result(m, par, i):
                dve.wait_ge(s_down, per * (m + 1) + 1)
                dve.wait_ge(s_store[par], 16 * (i + 1))
                if shared:
                    dve.wait_ge(s_res[par], 16 * (i + 1))
                    dve.tensor_tensor(y[:, par], res[:, par], y_ps[:, par], ALU.add).then_inc(s_y, 1)
                else:
                    dve.tensor_copy(y[:, par], y_ps[:, par]).then_inc(s_y, 1)

            def step(n, u, m, i, more):
                if more:
                    product(n + 1, (u + 1) % (2 * per))
                if u % per == per - 1:
                    result(m, u // per, i)
            dve.sem_inc(s_xt, 2)
            dve.sem_inc(s_xT, 1)
            dve.sem_inc(s_h, 2)
            dve.sem_inc(s_ht, 2)
            dve.sem_inc(s_down, 1)
            dve.sem_inc(s_y, 2)
            product(0, 0)
            stream(dve, step)

        if extra_pool is not None:
            @block.gpsimd
            def _(pool):
                extra_pool(pool)


def combine(nc, tag, x_in, x_out, y_d, weight, slot):
    NB = 4
    with ExitStack() as ctx:
        sb, ps, sem = names(ctx, nc, tag)
        x = sb("x", [P, NB, D])
        rows = sb("rows", [P, NB, 2, D])
        part = sb("part", [P, D])
        out = sb("out", [P, NB, D])
        s_x = [sem(f"x{i}") for i in range(NB)]
        s_rows = [sem(f"rows{i}") for i in range(NB)]
        s_part = sem("part")
        s_out = sem("out")
        s_store = [sem(f"store{i}") for i in range(NB)]
        block = ctx.enter_context(nc.Block())

        @block.gpsimd
        def _(pool):
            for t in range(NT):
                after(pool, s_out, t - NB + 1)
                for k in range(2):
                    pool.indirect_dma_start(out=rows[:, t % NB, k], out_offset=None, in_=y_d,
                                            in_offset=bass.IndirectOffsetOnAxis(ap=slot[:, k, t:t + 1], axis=0)
                                            ).then_inc(s_rows[t % NB], 16)

        @block.scalar
        def _(act):
            for t in range(NT):
                after(act, s_out, t - NB + 1)
                act.dma_start(x[:, t % NB], x_in[t * P:(t + 1) * P, :]).then_inc(s_x[t % NB], 16)

        @block.sync
        def _(sp):
            for t in range(NT):
                sp.wait_ge(s_out, t + 1)
                sp.dma_start(x_out[t * P:(t + 1) * P, :], out[:, t % NB]).then_inc(s_store[t % NB], 16)
            for i in range(NB):
                sp.wait_ge(s_store[i], 16 * (NT // NB))

        @block.vector
        def _(dve):
            for t in range(NT):
                b = t % NB
                dve.wait_ge(s_x[b], 16 * (t // NB + 1))
                dve.wait_ge(s_rows[b], 32 * (t // NB + 1))
                after(dve, s_out, t)
                dve.scalar_tensor_tensor(part[:], rows[:, b, 0], weight[:, 0, t:t + 1], x[:, b], ALU.mult,
                                         ALU.add).then_inc(s_part, 1)
                dve.wait_ge(s_part, t + 1)
                after(dve, s_store[b], 16 * (t // NB))
                dve.scalar_tensor_tensor(out[:, b], rows[:, b, 1], weight[:, 1, t:t + 1], part[:], ALU.mult,
                                         ALU.add).then_inc(s_out, 1)


def mixture(nc, tag, x_in, x_mid, x_out, sorted_d, y_d, gate_t, gu, dn, ident_d):
    with ExitStack() as ctx:
        sb, ps, sem = names(ctx, nc, tag)
        w_gu = sb("w_gu", [P, E, KC, 2 * F])
        w_d = sb("w_d", [P, E, FC, D])
        weight = sb("weight", [P, 2, NT])
        slot = sb("slot", [P, 2, NT], I32)
        block_expert = sb("block_expert", [1, MAX_BLOCKS + 1], I32)
        s_shared = sem("w_shared")
        s_experts = sem("w_experts")
        s_late = sem("w_late")
        s_scatter = sem("scatter")

        def load(eng, source, slot_, s):
            eng.dma_start(w_gu[:, slot_], gu[source]).then_inc(s, 16)
            full = (FC - 1) * P
            eng.dma_start(w_d[:, slot_, 0:FC - 1], dn[source, 0:full].rearrange("(j p) n -> p j n", p=P)).then_inc(s, 16)
            eng.dma_start(w_d[LAP:P, slot_, FC - 1], dn[source, full:F]).then_inc(s, 16)

        def load_first(eng):
            for j in range(NJ):
                load(eng, E + j, E - NJ + j, s_shared)
            for e in range(E - NJ):
                load(eng, e, e, s_experts)

        def load_late(eng):
            for e in range(E - NJ, E):
                load(eng, e, e, s_late)

        with ExitStack() as inner:
            sb2, ps2, sem2 = names(inner, nc, tag + "n")
            xn_all = sb2("xn_all", [P, NT, D])
            with ExitStack() as l:
                logits_ps = names(l, nc, tag + "l")[1]("logits_ps", [P, 512])
                gate(nc, tag + "g", x_in, xn_all, logits_ps, gate_t, ident_d, load_first, w_d)
                route(nc, tag + "r", logits_ps, weight, slot, block_expert)

            def scatter(pool):
                for t in range(NT):
                    for k in range(2):
                        pool.indirect_dma_start(out=sorted_d, out_offset=bass.IndirectOffsetOnAxis(
                            ap=slot[:, k, t:t + 1], axis=0), in_=xn_all[:, t], in_offset=None).then_inc(s_scatter, 16)
                pool.wait_ge(s_scatter, 16 * 2 * NT)
            expert_blocks(nc, tag + "s", True, w_gu, w_d,
                          lambda m: xn_all[:, bass.ds(m, 1), :].rearrange("p t n -> p (t n)"),
                          lambda m: x_in[bass.ds(m * P, P), :], lambda m: x_mid[bass.ds(m * P, P), :], NT, ident_d,
                          None, [(s_shared, 16 * 3 * NJ)], extra_pool=scatter)
        expert_blocks(nc, tag + "e", False, w_gu, w_d, lambda m: sorted_d[bass.ds(m * P, P), :], None,
                      lambda m: y_d[bass.ds(m * P, P), :], MAX_BLOCKS, ident_d, block_expert,
                      [(s_experts, 16 * 3 * (E - NJ)), (s_late, 16 * 3 * NJ)], load_weights=load_late)
        combine(nc, tag + "c", x_mid, x_out, y_d, weight, slot)


def program(nc, ins, out):
    def dram(name, shape):
        return nc.dram_tensor(name, shape, F32, kind="Internal").ap()
    x = ins["x"].rearrange("b t d -> (b t) d")
    out = out.rearrange("b t d -> (b t) d")
    ident_d = ins["ident"]
    sorted_d = dram("sorted_rows", (MAX_BLOCKS * P, D))
    y_d = dram("expert_rows", (MAX_BLOCKS * P, D))
    a_d = dram("a", (B, P, KC * HS))
    v_d = dram("v", (B, H, S, D))
    x1, x2, x3, x4, x5 = (dram(f"x{i}", (B * T, D)) for i in range(1, 6))

    with ExitStack() as ctx:
        sb, ps, sem = names(ctx, nc, "zero")
        zeros = sb("zeros", [P, D])
        s_zero = sem("zero")
        s_zeroed = sem("zeroed")
        block = ctx.enter_context(nc.Block())

        @block.gpsimd
        def _(pool):
            pool.memset(zeros[:], 0.0).then_inc(s_zero, 1)
            pool.wait_ge(s_zero, 1)
            pool.dma_start(sorted_d.rearrange("(n p) d -> p n d", p=P),
                           zeros[:].unsqueeze(1).to_broadcast([P, MAX_BLOCKS, D])).then_inc(s_zeroed, 16)
            pool.wait_ge(s_zeroed, 16)

    def stage_out(n, tensor):
        return out if n == STAGES else tensor
    prep(nc, "p0", 8, ins["ctx_t"], ins["wk0"], ins["wv0"], ins["wq_t0"], ins["wo0"], None, None, ins["mask"],
         ident_d, a_d, v_d)
    attend(nc, "t0", x, stage_out(1, x1), a_d, v_d, None, ins["mask"], ident_d)
    if STAGES == 1:
        return
    mixture(nc, "m0", x1, x2, stage_out(2, x3), sorted_d, y_d, ins["gate_t0"], ins["gu0"], ins["dn0"], ident_d)
    if STAGES == 2:
        return
    prep(nc, "p1", 16, ins["ctx_t"], ins["wk1"], ins["wv1"], ins["wq_t1"], ins["wo1"], ins["gq"], ins["gk"], None,
         ident_d, a_d, v_d)
    attend(nc, "t1", x3, stage_out(3, x4), a_d, v_d, ins["wq1"], None, ident_d)
    if STAGES == 3:
        return
    mixture(nc, "m1", x4, x5, out, sorted_d, y_d, ins["gate_t1"], ins["gu1"], ins["dn1"], ident_d)


def kernel(**inputs):
    import numpy as np
    import concourse.bacc as bacc
    from concourse.bass_utils import run_bass_kernel_spmd as run

    a = {k: np.asarray(v) for k, v in inputs.items()}

    def chunks(w):
        return np.swapaxes(w.reshape(w.shape[:-2] + (KC, P, w.shape[-1])), -3, -2)

    def gate_up(experts, shared_gate, shared_up):
        halves = np.concatenate([shared_gate.reshape(NJ, F, D), shared_up.reshape(NJ, F, D)], axis=1)
        return chunks(np.swapaxes(np.concatenate([experts, halves], axis=0), 1, 2))

    def down(experts, shared):
        return np.concatenate([np.swapaxes(experts, 1, 2), shared.T.reshape(NJ, F, D)], axis=0)

    sgu = a["L0_ffn_shared_gate_up"]
    data = {
        "x": a["x"], "ctx_t": a["ctx_1024"].reshape(BS, CD).T, "mask": a["mask_BxS2_bf1"],
        "ident": np.eye(P, dtype=np.float32),
        "wk0": a["L0_xattn_Wk"], "wv0": a["L0_xattn_Wv"], "wq_t0": a["L0_xattn_Wq"].T, "wo0": a["L0_xattn_Wo"],
        "wk1": a["L1_xattn_Wk"], "wv1": a["L1_xattn_Wv"], "wq_t1": a["L1_xattn_Wq"].T, "wo1": a["L1_xattn_Wo"],
        "wq1": a["L1_xattn_Wq"], "gq": a["L1_xattn_gq"], "gk": a["L1_xattn_gk"],
        "gate_t0": a["L0_ffn_gate_weight"].T,
        "gu0": gate_up(a["L0_ffn_gate_up_weights"], sgu[:NJ * F], sgu[NJ * F:]),
        "dn0": down(a["L0_ffn_down_weights"], a["L0_ffn_shared_down"]),
        "gate_t1": a["L1_ffn_gate_w"].T,
        "gu1": gate_up(np.concatenate([a["L1_ffn_w1"], a["L1_ffn_w2"]], axis=1), a["L1_ffn_sw1"], a["L1_ffn_sw2"]),
        "dn1": down(a["L1_ffn_w3"], a["L1_ffn_sw3"]),
    }
    nc = bacc.Bacc("TRN2", target_bir_lowering=False, num_devices=1)
    arrays, ins = {}, {}
    for name, value in data.items():
        value = np.ascontiguousarray(value)
        arrays[f"in_{name}"] = value
        ins[name] = nc.dram_tensor(f"in_{name}", value.shape, mybir.dt.from_np(value.dtype), kind="ExternalInput").ap()
    out = nc.dram_tensor("out", (B, T, D), F32, kind="ExternalOutput").ap()
    program(nc, ins, out)
    return run(nc, [arrays], core_ids=[0]).results[0]["out"]
```

```python
from contextlib import ExitStack

import concourse.bass as bass
from concourse import mybir

ALU = mybir.AluOpType
ACT = mybir.ActivationFunctionType
F32 = mybir.dt.float32
F32R = mybir.dt.float32r
I32 = mybir.dt.int32
U8 = mybir.dt.uint8
AX = mybir.AxisListType.X

P = 128
B, T, D = 4, 512, 512
KC = D // P
NT = B * T // P
TB = T // P
H, DH, S, CD = 16, 128, 64, 256
HS = H * S
BS = B * S
CC = CD // P
HG = 4
NG = H // HG
NQ = HS // P
PARTS = 4
E, F = 8, 352
NJ = 2
FC = -(-F // P)
LAP = FC * P - F
MAX_BLOCKS = (2 * NT * P + E * (P - 1)) // P
ZERO_BLOCKS = MAX_BLOCKS // (NT - TB + 1)
EPS = 1e-5
SCALE = float(DH) ** -0.5
MASKED = -(2.0 ** 100)
STAGES = 4


assert ZERO_BLOCKS * (NT - TB + 1) == MAX_BLOCKS


def after(eng, sem, value):
    if not isinstance(value, int) or value > 0:
        eng.wait_ge(sem, value)


class Chain:

    def __init__(self, eng, sem):
        self.eng, self.sem, self.n = eng, sem, 0

    def __call__(self, ins):
        self.n += 1
        ins.then_inc(self.sem, 1)
        self.eng.wait_ge(self.sem, self.n)


def names(ctx, nc, tag):
    def sb(name, shape, dt=F32):
        return ctx.enter_context(nc.sbuf_tensor(f"{tag}_{name}", shape, dt))

    def ps(name, shape, dt=F32):
        return ctx.enter_context(nc.psum_tensor(f"{tag}_{name}", shape, dt))

    sems = []

    def sem(name):
        sems.append(nc.alloc_semaphore(f"{tag}_{name}"))
        return sems[-1]

    def release():
        if sems:
            nc.clear_and_free_semaphores(sems)
            nc.all_engine_barrier()
    ctx.callback(release)
    return sb, ps, sem


def matmul3(pe, out, hi_w, lo_w, hi_x, lo_x, start, stop):
    pe.matmul(out, hi_w, hi_x, start=start, stop=False)
    pe.matmul(out, hi_w, lo_x, start=False, stop=False)
    return pe.matmul(out, lo_w, hi_x, start=False, stop=stop)


def prep(nc, tag, kv_heads, ctx_t, wk, wv, wq_t, wo, gq, gk, mask, ident_d, a_d, v_d):
    normed = gq is not None
    rep = H // kv_heads
    GK = HG // rep
    cols = GK * DH
    with ExitStack() as ctx:
        sb, ps, sem = names(ctx, nc, tag)
        ctx_sb = sb("ctx", [P, CC, BS])
        wk_sb = sb("wk", [P, 2, CC, cols])
        wv_sb = sb("wv", [P, 2, CC, cols])
        wq_sb = sb("wq", [P, 2, HG, D])
        wo_sb = sb("wo", [P, 2, HG, D])
        kT = sb("kT", [P, 2, GK, BS])
        vT = sb("vT", [P, 2, GK, BS])
        a_st = sb("a_st", [P, 2, KC, B, HG * S])
        v_st = sb("v_st", [P, 2, 2, HG, D])
        maskcol = sb("maskcol", [P, 2])
        mask_u8 = sb("mask_u8", [P, 2], U8)
        if normed:
            gq_sb = sb("gq", [P, 1])
            gk_sb = sb("gk", [P, 1])
            g_sb = sb("g", [P, 1])
            ones = sb("ones", [P, P])
            ksq = sb("ksq", [P, GK, BS])
            krs = sb("krs", [P, GK, BS])
        k_ps = ps("k_ps", [P, GK, 256])
        v_ps = ps("v_ps", [P, GK, 256])
        unit_ps = ps("unit_ps", [P, 2, 1024])

        s_ctx = sem("ctx")
        s_small = sem("small")
        s_w = [sem(f"w{i}") for i in range(2)]
        s_g = sem("g")
        s_kproj = sem("kproj")
        s_vproj = sem("vproj")
        s_sq = sem("sq")
        s_ss = sem("ss")
        s_rs = sem("rs")
        s_rsl = sem("rsl")
        s_root = sem("root")
        s_k = sem("k")
        s_v = sem("v")
        s_aunit = sem("aunit")
        s_vunit = sem("vunit")
        s_acopy = sem("acopy")
        s_vcopy = sem("vcopy")
        s_astored = [sem(f"astored{i}") for i in range(2)]
        s_vstored = [sem(f"vstored{i}") for i in range(2)]

        wk_v = wk.rearrange("(c p) n -> p c n", p=P)
        wv_v = wv.rearrange("(c p) n -> p c n", p=P)
        wq_v = wq_t.rearrange("(h d) n -> d h n", d=DH)
        wo_v = wo.rearrange("(h d) n -> d h n", d=DH)
        block = ctx.enter_context(nc.Block())

        @block.sync
        def _(sp):
            sp.dma_start(ctx_sb[:], ctx_t.rearrange("(c p) n -> p c n", p=P)).then_inc(s_ctx, 16)

            def load_group(g, par):
                sp.dma_start(wk_sb[:, par], wk_v[:, :, bass.ds(g * cols, cols)]).then_inc(s_w[par], 16)
                sp.dma_start(wv_sb[:, par], wv_v[:, :, bass.ds(g * cols, cols)]).then_inc(s_w[par], 16)
                sp.dma_start(wq_sb[:, par], wq_v[:, bass.ds(g * HG, HG), :]).then_inc(s_w[par], 16)
                sp.dma_start(wo_sb[:, par], wo_v[:, bass.ds(g * HG, HG), :]).then_inc(s_w[par], 16)
            load_group(0, 0)
            load_group(1, 1)
            for par in range(2):
                sp.sem_inc(s_vstored[par], 64)
            for g in range(NG):
                sp.wait_ge(s_vcopy, HG * (g + 1) + 1)
                for b in range(B):
                    sp.dma_start(v_d[b, g * HG:(g + 1) * HG].rearrange("h s n -> s h n"),
                                 v_st[(b % 2) * S:(b % 2 + 1) * S, g % 2, b // 2]).then_inc(s_vstored[g % 2], 16)
                if g + 2 < NG:
                    sp.wait_ge(s_aunit, HG * (g + 1))
                    sp.wait_ge(s_vunit, HG * (g + 1))
                    load_group(g + 2, g % 2)
            for par in range(2):
                sp.wait_ge(s_vstored[par], 64 * (NG // 2 + 1))

        @block.tensor
        def _(pe):
            pe.wait_ge(s_ctx, 16)
            if normed:
                pe.wait_ge(s_g, 1)

            def group(i, par):
                g = 2 * i + par
                pe.wait_ge(s_w[par], 64 * (i + 1))
                pe.wait_ge(s_k, g + 1)
                for h in range(GK):
                    for c in range(CC):
                        mm = pe.matmul(k_ps[:, h, 0:BS], wk_sb[:, par, c, h * DH:(h + 1) * DH], ctx_sb[:, c, :],
                                       start=(c == 0), stop=(c == CC - 1))
                mm.then_inc(s_kproj, 1)
                pe.wait_ge(s_v, g + 1)
                for h in range(GK):
                    for c in range(CC):
                        mm = pe.matmul(v_ps[:, h, 0:BS], wv_sb[:, par, c, h * DH:(h + 1) * DH], ctx_sb[:, c, :],
                                       start=(c == 0), stop=(c == CC - 1))
                mm.then_inc(s_vproj, 1)
                if normed:
                    pe.wait_ge(s_sq, 2 * (g + 1))
                    for h in range(GK):
                        mm = pe.matmul(k_ps[:, h, 0:BS], ones[:], ksq[:, h, :], start=True, stop=True)
                    mm.then_inc(s_ss, 1)
                pe.wait_ge(s_v, g + 2)
                for u in range(HG):
                    pe.wait_ge(s_vcopy, HG * g + u + 1)
                    h = u // rep
                    for p in range(2):
                        mm = pe.matmul(unit_ps[:, 0, p * 512:(p + 1) * 512], vT[:, par, h, p * P:(p + 1) * P],
                                       wo_sb[:, par, u, :], start=True, stop=True)
                    mm.then_inc(s_vunit, 1)
                    if u == 0:
                        pe.wait_ge(s_k, g + 2)
                    pe.wait_ge(s_acopy, HG * g + u + 1)
                    for c in range(KC):
                        mm = pe.matmul(unit_ps[:, 1, c * BS:(c + 1) * BS], wq_sb[:, par, u, c * P:(c + 1) * P],
                                       kT[:, par, h, :], start=True, stop=True)
                    mm.then_inc(s_aunit, 1)
            with pe.Fori(0, NG // 2) as i:
                group(i, 0)
                group(i, 1)

        @block.scalar
        def _(act):
            act.sem_inc(s_acopy, 1)
            for par in range(2):
                act.sem_inc(s_astored[par], 64)

            def group(i, par):
                g = 2 * i + par
                if normed:
                    act.wait_ge(s_sq, 2 * g + 1)
                    act.wait_ge(s_rs, g + 1)
                    act.activation(ksq[:], k_ps[:, :, 0:BS], ACT.Square).then_inc(s_sq, 1)
                    act.wait_ge(s_rsl, 3 * g + 3)
                    act.activation(krs[:], krs[:], ACT.Sqrt).then_inc(s_root, 1)
                act.wait_ge(s_astored[par], 64 * (i + 1))
                for u in range(HG):
                    act.wait_ge(s_aunit, HG * g + u + 1)
                    act.activation(a_st[:, par, :, :, u * S:(u + 1) * S],
                                   unit_ps[:, 1, :].rearrange("p (c b s) -> p c b s", c=KC, b=B),
                                   ACT.Copy).then_inc(s_acopy, 1)
                act.wait_ge(s_acopy, HG * (g + 1) + 1)
                for b in range(B):
                    act.dma_start(a_d[b].rearrange("p (c n) -> p c n", c=KC)[:, :, bass.ds(g * HG * S, HG * S)],
                                  a_st[:, par, :, b, :]).then_inc(s_astored[par], 16)
            with act.Fori(0, NG // 2) as i:
                group(i, 0)
                group(i, 1)
            for par in range(2):
                act.wait_ge(s_astored[par], 64 * (NG // 2 + 1))

        @block.vector
        def _(dve):
            dve.sem_inc(s_vcopy, 1)
            dve.sem_inc(s_k, 1)
            dve.sem_inc(s_v, 1)
            dve.wait_ge(s_small, 32)
            if mask is not None:
                dve.tensor_copy(maskcol[:], mask_u8[:]).then_inc(s_rsl, 1)
            else:
                dve.memset(maskcol[:], 1.0).then_inc(s_rsl, 1)
            if normed:
                dve.sem_inc(s_rs, 1)
                dve.memset(ones[:], 1.0)
                dve.tensor_tensor(g_sb[:], gq_sb[:], gk_sb[:], ALU.mult).then_inc(s_g, 1)

            def group(i, par):
                g = 2 * i + par
                dve.wait_ge(s_kproj, g + 1)
                if normed:
                    dve.tensor_scalar(kT[:, par], k_ps[:, :, 0:BS], g_sb[:, 0:1], None, ALU.mult).then_inc(s_sq, 1)
                else:
                    dve.tensor_copy(kT[:, par], k_ps[:, :, 0:BS]).then_inc(s_k, 1)
                dve.wait_ge(s_vproj, g + 1)
                dve.tensor_copy(vT[:, par], v_ps[:, :, 0:BS]).then_inc(s_v, 1)
                if normed:
                    dve.wait_ge(s_ss, g + 1)
                    dve.tensor_scalar(krs[:], k_ps[:, :, 0:BS], 1.0 / DH, EPS, ALU.mult, ALU.add).then_inc(s_rsl, 1)
                    dve.wait_ge(s_rsl, 3 * g + 2)
                    dve.reciprocal(krs[:], krs[:]).then_inc(s_rsl, 1)
                    dve.wait_ge(s_root, g + 1)
                    dve.tensor_tensor(kT[:, par], kT[:, par], krs[:], ALU.mult).then_inc(s_rsl, 1)
                    dve.wait_ge(s_rsl, 3 * g + 4)
                    dve.sem_inc(s_rs, 1)
                    dve.sem_inc(s_k, 1)
                for u in range(HG):
                    dve.wait_ge(s_vunit, HG * g + u + 1)
                    if u == 0:
                        dve.wait_ge(s_vstored[par], 64 * (i + 1))
                        if not normed:
                            dve.wait_ge(s_rsl, 1)
                    dve.tensor_tensor(v_st[:, par, :, u, :], unit_ps[:, 0, :].rearrange("p (a n) -> p a n", a=2),
                                      maskcol[:].unsqueeze(2).to_broadcast([P, 2, D]), ALU.mult).then_inc(s_vcopy, 1)
            with dve.Fori(0, NG // 2) as i:
                group(i, 0)
                group(i, 1)

        @block.gpsimd
        def _(pool):
            if mask is not None:
                for p in range(2):
                    pool.dma_start(mask_u8[:, p:p + 1], mask[2 * p:2 * p + 2, :].rearrange("b (s o) -> (b s) o", o=1)
                                   ).then_inc(s_small, 16)
            else:
                pool.dma_start(gq_sb[:], gq.rearrange("(d o) -> d o", o=1)).then_inc(s_small, 16)
                pool.dma_start(gk_sb[:], gk.rearrange("(d o) -> d o", o=1)).then_inc(s_small, 16)


def moments(dve, sem, count, x, stats, mv, carrier):
    dve.bn_stats(stats, x).then_inc(sem, 1)
    dve.wait_ge(sem, count + 1)
    dve.memset(carrier, 0.0)
    dve.bn_aggr(mv, stats).then_inc(sem, 1)
    dve.wait_ge(sem, count + 2)
    dve.tensor_scalar(mv[:, 1:2], mv[:, 1:2], EPS, None, ALU.add).then_inc(sem, 1)


def tiles(eng, step):
    step(0, 0, 0, NT)
    with eng.Fori(0, B - 1) as b:
        for j in range(1, TB + 1):
            step(TB * b + j, j % TB, b + j // TB, TB)
    for t in range(TB * (B - 1) + 1, NT):
        step(t, t % TB, B - 1, NT - t)


def attend(nc, tag, x_in, x_out, xn_out, logits, gate_t, a_d, v_d, wq, mask, ident_d, zero_rows=None):
    normed = wq is not None
    with ExitStack() as ctx:
        sb, ps, sem = names(ctx, nc, tag)
        ident = sb("ident", [P, P])
        a_raw = sb("a_raw", [P, KC * HS])
        v_raw = sb("v_raw", [P, NQ * D])
        a_hi = sb("a_hi", [P, KC, HS], F32R)
        a_lo = sb("a_lo", [P, KC, HS], F32R)
        v_hi = sb("v_hi", [P, NQ, D], F32R)
        v_lo = sb("v_lo", [P, NQ, D], F32R)
        x = sb("x", [P, TB, D])
        xn = sb("xn", [P, D])
        stats = sb("stats", [P, 6])
        mv = sb("mv", [P, 2])
        carrier = sb("carrier", [P, 1])
        rstd = sb("rstd", [P, 1])
        power = sb("power", [P, 1])
        x_hi = sb("x_hi", [P, 2, KC, P], F32R)
        x_lo = sb("x_lo", [P, 2, KC, P], F32R)
        top = sb("top", [P, H])
        z = sb("z", [P, H, S])
        p_sb = sb("p", [P, H, S])
        total = sb("total", [P, H])
        recip = sb("recip", [P, H])
        p_hi = sb("p_hi", [P, NQ, P], F32R)
        p_lo = sb("p_lo", [P, NQ, P], F32R)
        y = sb("y", [P, D])
        mv2 = sb("mv2", [P, 2])
        rstd2 = sb("rstd2", [P, 1])
        xn2 = sb("xn2", [P, D])
        xT2 = sb("xT2", [P, KC, P])
        gate_sb = sb("gate", [P, KC, E])
        if normed:
            wq_hi = sb("wq_hi", [P, KC, H * DH], F32R)
            wq_lo = sb("wq_lo", [P, KC, H * DH], F32R)
            qsq = sb("qsq", [P, 512])
            ssq = sb("ssq", [P, H])
            rq = sb("rq", [P, H])
        if zero_rows is not None:
            zeros = sb("zeros", [P, D])
        if mask is not None:
            mask_u8 = sb("mask_u8", [1, BS], U8)
            maskf = sb("maskf", [1, B, S])
            bias = sb("bias", [1, B, HS], F32R)
            one_f = sb("one_f", [1, P])
            one_row = sb("one_row", [1, P], F32R)
        xt_ps = ps("xt_ps", [P, KC, P])
        s_ps = ps("s_ps", [P, H, S])
        pt_ps = ps("pt_ps", [P, NQ, P])
        o_ps = ps("o_ps", [P, D])
        NQG = H * DH // 512
        a_raw3 = a_raw[:].rearrange("p (c n) -> p c n", c=KC)
        v_raw3 = v_raw[:].rearrange("p (q n) -> p q n", q=NQ)
        a_part = lambda a, i: a[:, :, i * HS // PARTS:(i + 1) * HS // PARTS]
        v_part = lambda v, i: v[:, i * NQ // PARTS:(i + 1) * NQ // PARTS, :]
        if normed:
            wq_raw = lambda n: (a_raw, v_raw)[n // 2][:, n % 2 * KC * 512:(n % 2 + 1) * KC * 512].rearrange(
                "p (c n) -> p c n", c=KC)
            wq_part = lambda w, n: w[:, :, n * 512:(n + 1) * 512]
        if normed:
            q_ps = ps("q_ps", [P, 2, 512])

        s_id = sem("id")
        s_araw = [sem(f"araw{i}") for i in range(PARTS)]
        s_vraw = [sem(f"vraw{i}") for i in range(PARTS)]
        s_ahi = sem("ahi")
        s_alo = [sem(f"alo{i}") for i in range(2)]
        s_vhi = sem("vhi")
        s_vlo = [sem(f"vlo{i}") for i in range(2)]
        s_x = [sem(f"x{i}") for i in range(TB)]
        s_ln = sem("ln")
        s_rstd = sem("rstd")
        s_xn = sem("xn")
        s_xt = sem("xt")
        s_xhi = sem("xhi")
        s_xlo = sem("xlo")
        s_scores = sem("scores")
        s_top = sem("top")
        s_sub = sem("sub")
        s_zq = sem("zq")
        s_exp = sem("exp")
        s_sum = sem("sum")
        s_rec = sem("rec")
        s_prob = sem("prob")
        s_pt = sem("pt")
        s_phi = sem("phi")
        s_plo = sem("plo")
        s_o = sem("o")
        s_y = sem("y")
        s_store = sem("store")
        s_ln2 = sem("ln2")
        s_rstd2 = sem("rstd2")
        s_xn2 = sem("xn2")
        s_keep = sem("keep")
        s_xt2 = sem("xt2")
        s_xT2 = sem("xT2")
        s_gatew = sem("gatew")
        s_gate = sem("gate")
        s_logits = sem("logits")
        s_q = sem("q")
        s_qsq = sem("qsq")
        s_qsum = sem("qsum")
        s_rq = sem("rq")
        s_rqp = sem("rqp")
        s_wqraw = [sem(f"wqraw{i}") for i in range(PARTS)]
        s_wqhi = sem("wqhi")
        s_wqlo = [sem(f"wqlo{i}") for i in range(2)]
        s_mask = sem("mask")
        s_bias = sem("bias")
        s_zero = sem("zero")
        s_zeroed = sem("zeroed")

        block = ctx.enter_context(nc.Block())

        @block.sync
        def _(sp):
            def load_x(t):
                sp.dma_start(x[:, t], x_in[t * P:(t + 1) * P, :]).then_inc(s_x[t], 16)

            def load_a(b):
                a_b = a_d[bass.ds(b, 1)].rearrange("b p (c n) -> p (b c) n", c=KC)
                for i in range(PARTS):
                    sp.dma_start(a_part(a_raw3, i), a_part(a_b, i)).then_inc(s_araw[i], 16)

            def load_v(b):
                v_b = v_d[bass.ds(b, 1)].rearrange("b (q a) s n -> (a s) (b q) n", a=2)
                for i in range(PARTS):
                    sp.dma_start(v_part(v_raw3, i), v_part(v_b, i)).then_inc(s_vraw[i], 16)

            load_x(0)
            sp.dma_start(ident[:], ident_d).then_inc(s_id, 16)
            sp.sem_inc(s_keep, 16)
            sp.sem_inc(s_store, 16)
            if mask is not None:
                sp.dma_start(mask_u8[:], mask.rearrange("(o b) s -> o (b s)", o=1)).then_inc(s_mask, 16)
            if normed:
                for n in range(PARTS):
                    sp.dma_start(wq_raw(n), wq_part(wq.rearrange("(c p) n -> p c n", p=P), n)).then_inc(
                        s_wqraw[n], 16)
                    if n == 0:
                        load_x(1)
                sp.wait_ge(s_wqlo[0], 2)
            load_a(0)
            if not normed:
                load_x(1)
            load_x(2)
            sp.dma_start(gate_sb[:], gate_t.rearrange("(c p) e -> p c e", p=P)).then_inc(s_gatew, 16)
            if normed:
                sp.wait_ge(s_wqlo[1], 2)
            load_v(0)
            load_x(3)

            def step(t, j, b, left):
                if left >= 4 and not isinstance(t, int):
                    sp.dma_start(x[:, (j + 3) % TB], x_in[bass.ds((t + 3) * P, P), :]).then_inc(
                        s_x[(j + 3) % TB], 16)
                if j == 1 and left >= 4:
                    for half in range(2):
                        sp.wait_ge(s_alo[half], 2 * (b + 1))
                    load_a(b + 1)
                    for half in range(2):
                        sp.wait_ge(s_vlo[half], 2 * (b + 1))
                    load_v(b + 1)
                if zero_rows is not None and left >= TB:
                    sp.wait_ge(s_zero, 1)
                    sp.dma_start(zero_rows[bass.ds(t * ZERO_BLOCKS * P, ZERO_BLOCKS * P), :].rearrange(
                        "(n p) d -> p n d", p=P), zeros[:].unsqueeze(1).to_broadcast([P, ZERO_BLOCKS, D])
                                 ).then_inc(s_zeroed, 16)
                sp.wait_ge(s_y, t + 2)
                sp.dma_start(x_out[bass.ds(t * P, P), :], y[:]).then_inc(s_store, 16)
                sp.wait_ge(s_xn2, t + 1)
                sp.dma_start(xn_out[bass.ds(t * P, P), :], xn2[:]).then_inc(s_keep, 16)
            tiles(sp, step)
            sp.wait_ge(s_store, 16 * (NT + 1))
            sp.wait_ge(s_keep, 16 * (NT + 1))
            if zero_rows is not None:
                sp.wait_ge(s_zeroed, 16 * (MAX_BLOCKS // ZERO_BLOCKS))

        @block.tensor
        def _(pe):
            def transposes(t):
                pe.wait_ge(s_xn, t + 1)
                pe.wait_ge(s_xlo, t + 1)
                if not isinstance(t, int) or t >= 3:
                    pe.wait_ge(s_xT2, t - 2)
                for c in range(KC):
                    mm = pe.transpose(xt_ps[:, c, :], xn[:, c * P:(c + 1) * P], ident[:])
                mm.then_inc(s_xt, 1)

            def queries(t, j):
                pe.wait_ge(s_xlo, t + 2)
                for n in range(NQG):
                    if isinstance(t, int) and t == 0:
                        pe.wait_ge(s_wqlo[n // 2], n % 2 + 1)
                    pe.wait_ge(s_qsq, NQG * t + n + 1)
                    for c in range(KC):
                        mm = matmul3(pe, q_ps[:, n % 2, :], x_hi[:, j % 2, c, :], x_lo[:, j % 2, c, :],
                                     wq_hi[:, c, n * 512:(n + 1) * 512], wq_lo[:, c, n * 512:(n + 1) * 512],
                                     c == 0, c == KC - 1)
                    mm.then_inc(s_q, 1)

            def scores(t, j, b, half):
                if half == 0:
                    pe.wait_ge(s_xlo, t + 2)
                    pe.wait_ge(s_sub, t + 1)
                if j == 0:
                    pe.wait_ge(s_alo[half], 2 * (b + 1))
                out = s_ps[:, half * 8:(half + 1) * 8, :]
                cols = slice(half * 512, (half + 1) * 512)
                for c in range(KC):
                    mm = matmul3(pe, out, x_hi[:, j % 2, c, :], x_lo[:, j % 2, c, :], a_hi[:, c, cols],
                                 a_lo[:, c, cols], c == 0, c == KC - 1 and mask is None)
                if mask is not None:
                    mm = pe.matmul(out, one_row[:],
                                   bias[:, bass.ds(b, 1), cols].rearrange("o b n -> o (b n)"), start=False, stop=True)
                mm.then_inc(s_scores, 1)

            def prob_transposes(t):
                pe.wait_ge(s_prob, t + 1)
                pe.wait_ge(s_plo, t + 1)
                for q in range(NQ):
                    mm = pe.transpose(pt_ps[:, q, :], p_sb[:, 2 * q:2 * q + 2, :].rearrange("p a s -> p (a s)"),
                                      ident[:])
                mm.then_inc(s_pt, 1)

            def outputs(t, j, b):
                pe.wait_ge(s_plo, t + 2)
                pe.wait_ge(s_y, t + 1)
                after(pe, s_logits, t)
                for q in range(NQ):
                    if j == 0 and q % (NQ // 2) == 0:
                        pe.wait_ge(s_vlo[q // (NQ // 2)], 2 * (b + 1))
                    mm = matmul3(pe, o_ps[:], p_hi[:, q, :], p_lo[:, q, :], v_hi[:, q, :], v_lo[:, q, :],
                                 q == 0, q == NQ - 1)
                mm.then_inc(s_o, 1)

            def result_transposes(t):
                pe.wait_ge(s_xn2, t + 1)
                for c in range(KC):
                    mm = pe.transpose(xt_ps[:, c, :], xn2[:, c * P:(c + 1) * P], ident[:])
                mm.then_inc(s_xt2, 1)

            def gate_products(t):
                pe.wait_ge(s_xT2, t + 1)
                if isinstance(t, int) and t == 0:
                    pe.wait_ge(s_gatew, 16)
                for c in range(KC):
                    mm = pe.matmul(o_ps[:, 0:E], xT2[:, c, :], gate_sb[:, c, :], start=(c == 0), stop=(c == KC - 1))
                mm.then_inc(s_gate, 1)

            def step(t, j, b, left):
                jn, bn = (j + 1) % TB, b + (j + 1) // TB
                first = isinstance(t, int) and t == 0
                if left >= 2:
                    if normed:
                        queries(t + 1, jn)
                    scores(t + 1, jn, bn, 0)
                prob_transposes(t)
                if not first:
                    result_transposes(t - 1)
                if left >= 2:
                    scores(t + 1, jn, bn, 1)
                if not first:
                    gate_products(t - 1)
                if left >= 3:
                    transposes(t + 2)
                outputs(t, j, b)

            pe.wait_ge(s_id, 16)
            transposes(0)
            if normed:
                queries(0, 0)
            transposes(1)
            if mask is not None:
                pe.wait_ge(s_bias, 4)
            scores(0, 0, 0, 0)
            scores(0, 0, 0, 1)
            tiles(pe, step)
            result_transposes(NT - 1)
            pe.wait_ge(s_y, NT + 1)
            gate_products(NT - 1)

        @block.scalar
        def _(act):
            def split_x(t, j):
                act.wait_ge(s_xt, t + 1)
                if not isinstance(t, int) or t >= 2:
                    act.wait_ge(s_scores, 2 * (t - 1))
                act.activation(x_hi[:, j % 2], xt_ps[:], ACT.Copy).then_inc(s_xhi, 1)

            def query_squares(t, between=None):
                for n in range(NQG):
                    act.wait_ge(s_q, NQG * t + n + 1)
                    act.wait_ge(s_qsum, NQG * t + n + 1)
                    act.activation(qsq[:], q_ps[:, n % 2, :], ACT.Square).then_inc(s_qsq, 1)
                    if between is not None:
                        between(n)

            def split_a(b, i):
                act.wait_ge(s_araw[i], 16 * (b + 1))
                after(act, s_scores, 2 * TB * b - (1 if i < PARTS // 2 else 0) if not isinstance(b, int) or b else 0)
                act.activation(a_part(a_hi, i), a_part(a_raw3, i), ACT.Copy).then_inc(s_ahi, 1)

            def split_v(b, i):
                act.wait_ge(s_vraw[i], 16 * (b + 1))
                after(act, s_o, TB * b + 1)
                act.activation(v_part(v_hi, i), v_part(v_raw3, i), ACT.Copy).then_inc(s_vhi, 1)

            def exps(t):
                if normed:
                    act.wait_ge(s_zq, t + 1)
                else:
                    act.wait_ge(s_sub, t + 2)
                act.wait_ge(s_pt, t + 1)
                act.activation(p_sb[:], z[:], ACT.Exp, scale=1.0 if normed else SCALE).then_inc(s_exp, 1)

            def split_p(t):
                act.wait_ge(s_pt, t + 2)
                act.wait_ge(s_o, t + 1)
                act.activation(p_hi[:], pt_ps[:], ACT.Copy).then_inc(s_phi, 1)

            def result_copy(t):
                act.wait_ge(s_xt2, t + 1)
                after(act, s_gate, t)
                act.activation(xT2[:], xt_ps[:], ACT.Copy).then_inc(s_xT2, 1)

            def step(t, j, b, left):
                if normed and left >= 2:
                    if j == TB - 1:
                        query_squares(t + 1, lambda i: split_a(b + 1, i))
                    elif j == 0 and not (isinstance(t, int) and t == 0):
                        query_squares(t + 1, lambda i: split_v(b, i))
                    else:
                        query_squares(t + 1)
                split_p(t)
                if not isinstance(t, int) or t > 0:
                    result_copy(t - 1)
                if not normed and j == TB - 2 and left >= 3:
                    for i in range(PARTS // 2):
                        split_a(b + 1, i)
                if left >= 3:
                    split_x(t + 2, (j + 2) % TB)
                if not normed and j == TB - 2 and left >= 3:
                    for i in range(PARTS // 2, PARTS):
                        split_a(b + 1, i)
                if left >= 2:
                    exps(t + 1)
                if not normed and j == TB - 1 and left >= 2:
                    for i in range(PARTS):
                        split_v(b + 1, i)

            if normed:
                act.sem_inc(s_qsq, 2)
            split_x(0, 0)
            if normed:
                for n in range(PARTS):
                    act.wait_ge(s_wqraw[n], 16)
                    act.activation(wq_part(wq_hi, n), wq_raw(n), ACT.Copy).then_inc(s_wqhi, 1)
                query_squares(0, lambda i: split_a(0, i))
            else:
                for i in range(PARTS):
                    split_a(0, i)
            split_x(1, 1)
            for i in range(PARTS):
                split_v(0, i)
            exps(0)
            tiles(act, step)
            result_copy(NT - 1)

        @block.vector
        def _(dve):
            def norm_start(t, j, b):
                dve.wait_ge(s_x[j], 16 * (b + 1))
                moments(dve, s_ln, 3 * t, x[:, j, :], stats[:], mv[:], carrier[:])

            def norm_end(t, j):
                dve.wait_ge(s_rstd, t + 2)
                after(dve, s_xt, t)
                dve.tensor_scalar(xn[:], x[:, j, :], mv[:, 0:1], rstd[:, 0:1], ALU.subtract, ALU.mult).then_inc(
                    s_xn, 1)

            def split_x(t, j):
                dve.wait_ge(s_xhi, t + 1)
                dve.tensor_tensor(x_lo[:, j % 2], xt_ps[:], x_hi[:, j % 2].bitcast(F32), ALU.subtract).then_inc(
                    s_xlo, 1)

            def query_sums(t, between=None):
                for n in range(NQG):
                    dve.wait_ge(s_qsq, NQG * t + n + 3)
                    if n == 0:
                        after(dve, s_rq, t)
                    dve.tensor_reduce(ssq[:, 4 * n:4 * n + 4], qsq[:].rearrange("p (h d) -> p h d", d=DH), AX,
                                      ALU.add).then_inc(s_qsum, 1)
                    if between is not None and n < PARTS // 2:
                        between(n)
                dve.wait_ge(s_qsum, NQG * (t + 1) + 1)
                after(dve, s_zq, t)
                dve.tensor_scalar(rq[:], ssq[:], DH * EPS, None, ALU.add).then_inc(s_rq, 1)

            def split_a(b, i):
                dve.wait_ge(s_ahi, PARTS * b + i + 1)
                dve.tensor_tensor(a_part(a_lo, i), a_part(a_raw3, i), a_part(a_hi, i).bitcast(F32),
                                  ALU.subtract).then_inc(s_alo[0], 1)

            def split_v(b, i):
                dve.wait_ge(s_vhi, PARTS * b + i + 1)
                dve.tensor_tensor(v_part(v_lo, i), v_part(v_raw3, i), v_part(v_hi, i).bitcast(F32),
                                  ALU.subtract).then_inc(s_vlo[0], 1)

            def shift(t):
                dve.wait_ge(s_scores, 2 * (t + 1))
                dve.tensor_reduce(top[:], s_ps[:], AX, ALU.max).then_inc(s_top, 1)
                dve.wait_ge(s_top, t + 1)
                after(dve, s_exp, t)
                dve.tensor_tensor(z[:], s_ps[:], top[:].unsqueeze(2).to_broadcast([P, H, S]),
                                  ALU.subtract).then_inc(s_sub, 1)

            def sums(t):
                dve.wait_ge(s_exp, t + 1)
                dve.tensor_reduce(total[:], p_sb[:], AX, ALU.add).then_inc(s_sum, 1)
                dve.wait_ge(s_sum, t + 1)
                after(dve, s_prob, t)
                dve.reciprocal(recip[:], total[:]).then_inc(s_rec, 1)

            def split_p(t):
                dve.wait_ge(s_phi, t + 1)
                dve.tensor_tensor(p_lo[:], pt_ps[:], p_hi[:].bitcast(F32), ALU.subtract).then_inc(s_plo, 1)

            def add_output(t, j):
                dve.wait_ge(s_o, t + 2)
                dve.wait_ge(s_store, 16 * (t + 1))
                dve.tensor_tensor(y[:], x[:, j, :], o_ps[:], ALU.add).then_inc(s_y, 1)

            def result_norm(t):
                dve.wait_ge(s_y, t + 2)
                moments(dve, s_ln2, 3 * t, y[:], stats[:], mv2[:], carrier[:])
                dve.wait_ge(s_rstd2, t + 1)
                after(dve, s_xt2, t)
                dve.wait_ge(s_keep, 16 * (t + 1))
                dve.tensor_scalar(xn2[:], y[:], mv2[:, 0:1], rstd2[:, 0:1], ALU.subtract, ALU.mult).then_inc(
                    s_xn2, 1)

            def keep_logits(t):
                dve.wait_ge(s_gate, t + 1)
                dve.tensor_copy(logits[:, bass.ds(t, 1), :].rearrange("p t e -> p (t e)"), o_ps[:, 0:E]).then_inc(
                    s_logits, 1)

            def step(t, j, b, left):
                if normed and left >= 2:
                    if j == TB - 1:
                        query_sums(t + 1, lambda i: split_a(b + 1, i))
                    elif j == 0 and not (isinstance(t, int) and t == 0):
                        query_sums(t + 1, lambda i: split_v(b, i))
                    else:
                        query_sums(t + 1)
                split_p(t)
                if not isinstance(t, int) or t > 0:
                    keep_logits(t - 1)
                if not normed and j == TB - 2 and left >= 3:
                    for i in range(PARTS // 2):
                        split_a(b + 1, i)
                if left >= 2:
                    shift(t + 1)
                if left >= 3:
                    split_x(t + 2, (j + 2) % TB)
                if left >= 4:
                    norm_start(t + 3, (j + 3) % TB, b + (j + 3) // TB)
                if left >= 2:
                    sums(t + 1)
                if left >= 4:
                    norm_end(t + 3, (j + 3) % TB)
                add_output(t, j)
                result_norm(t)
                if not normed and j == TB - 1 and left >= 2:
                    for i in range(PARTS // 2):
                        split_v(b + 1, i)

            for s in (s_xlo, s_sub, s_pt, s_plo, s_o, s_y):
                dve.sem_inc(s, 1)
            norm_start(0, 0, 0)
            norm_end(0, 0)
            if normed:
                dve.sem_inc(s_qsum, 1)
            if mask is not None:
                dve.wait_ge(s_mask, 16)
                dve.memset(one_f[:], 1.0).then_inc(s_bias, 1)
                dve.tensor_copy(maskf[:].rearrange("o b s -> o (b s)"), mask_u8[:]).then_inc(s_bias, 1)
                dve.wait_ge(s_bias, 2)
                dve.tensor_copy(one_row[:], one_f[:]).then_inc(s_bias, 1)
                for b in range(B):
                    ins = dve.tensor_scalar(bias[:, b].rearrange("o (h s) -> o h s", h=H),
                                            maskf[:, b:b + 1, :].to_broadcast([1, H, S]), -MASKED, MASKED,
                                            ALU.mult, ALU.add)
                ins.then_inc(s_bias, 1)
            split_x(0, 0)
            if normed:
                for n in range(PARTS // 2):
                    dve.wait_ge(s_wqhi, n + 1)
                    dve.tensor_tensor(wq_part(wq_lo, n), wq_raw(n), wq_part(wq_hi, n).bitcast(F32),
                                      ALU.subtract).then_inc(s_wqlo[0], 1)
            norm_start(1, 1, 0)
            norm_end(1, 1)
            if normed:
                query_sums(0, lambda i: split_a(0, i))
            else:
                for i in range(PARTS // 2):
                    split_a(0, i)
            split_x(1, 1)
            norm_start(2, 2, 0)
            norm_end(2, 2)
            for i in range(PARTS // 2):
                split_v(0, i)
            shift(0)
            sums(0)
            tiles(dve, step)
            keep_logits(NT - 1)

        @block.gpsimd
        def _(pool):
            def power_half(t):
                pool.wait_ge(s_ln, 3 * (t + 1))
                after(pool, s_xn, t)
                pool.tensor_tensor(rstd[:], mv[:, 1:2], power[:], ALU.pow).then_inc(s_rstd, 1)

            def query_factors(t):
                pool.wait_ge(s_rq, t + 1)
                pool.tensor_tensor(rq[:], rq[:], power[:].to_broadcast([P, H]), ALU.pow).then_inc(s_rqp, 1)

            def scale_scores(t):
                pool.wait_ge(s_rqp, t + 1)
                pool.wait_ge(s_sub, t + 2)
                pool.tensor_tensor(z[:], z[:], rq[:].unsqueeze(2).to_broadcast([P, H, S]), ALU.mult).then_inc(s_zq, 1)

            def normalise(t):
                pool.wait_ge(s_rec, t + 1)
                pool.tensor_tensor(p_sb[:], p_sb[:], recip[:].unsqueeze(2).to_broadcast([P, H, S]),
                                   ALU.mult).then_inc(s_prob, 1)

            def result_power(t):
                pool.wait_ge(s_ln2, 3 * (t + 1))
                pool.tensor_tensor(rstd2[:], mv2[:, 1:2], power[:], ALU.pow).then_inc(s_rstd2, 1)

            def split_a(b):
                for i in range(PARTS // 2, PARTS):
                    pool.wait_ge(s_ahi, PARTS * b + i + 1)
                    pool.tensor_tensor(a_part(a_lo, i), a_part(a_raw3, i), a_part(a_hi, i).bitcast(F32),
                                       ALU.subtract).then_inc(s_alo[1], 1)

            def split_v(b):
                for i in range(PARTS // 2, PARTS):
                    pool.wait_ge(s_vhi, PARTS * b + i + 1)
                    pool.tensor_tensor(v_part(v_lo, i), v_part(v_raw3, i), v_part(v_hi, i).bitcast(F32),
                                       ALU.subtract).then_inc(s_vlo[1], 1)

            def step(t, j, b, left):
                if left >= 2 and normed:
                    if j == TB - 1:
                        split_a(b + 1)
                    elif j == 0 and not (isinstance(t, int) and t == 0):
                        split_v(b)
                if left >= 3 and not normed and j == TB - 2:
                    split_a(b + 1)
                if left >= 2:
                    if normed:
                        query_factors(t + 1)
                        scale_scores(t + 1)
                    if left >= 4:
                        power_half(t + 3)
                    normalise(t + 1)
                result_power(t)
                if left >= 2 and not normed and j == TB - 1:
                    split_v(b + 1)

            pool.memset(power[:], -0.5).then_inc(s_rstd, 1)
            pool.wait_ge(s_rstd, 1)
            power_half(0)
            if normed:
                for n in range(PARTS // 2, PARTS):
                    pool.wait_ge(s_wqhi, n + 1)
                    pool.tensor_tensor(wq_part(wq_lo, n), wq_raw(n), wq_part(wq_hi, n).bitcast(F32),
                                       ALU.subtract).then_inc(s_wqlo[1], 1)
            power_half(1)
            split_a(0)
            if normed:
                query_factors(0)
            power_half(2)
            split_v(0)
            if normed:
                scale_scores(0)
            normalise(0)
            if zero_rows is not None:
                pool.memset(zeros[:], 0.0).then_inc(s_zero, 1)
            tiles(pool, step)


def route(nc, tag, logits, weight, slot, block_expert, load_weights, split_high, split_low, clear_lap):
    with ExitStack() as ctx:
        sb, ps, sem = names(ctx, nc, tag)
        best = sb("best", [P, NT])
        probs = sb("probs", [P, NT, E])
        left = sb("left", [P, NT, E])
        equal = sb("equal", [P, NT, E])
        chosen = sb("chosen", [P, 2, NT, E])
        padded = sb("padded", [P, 2 * NT - 1, E])
        rank_code = sb("rank_code", [P, E])
        earlier = sb("earlier", [P, P])
        ones = sb("ones", [P, P])
        count = sb("count", [P, E])
        count_i = sb("count_i", [P, E], I32)
        rest = sb("rest", [P, E])
        ends = [sb(f"ends{i}", [P, E]) for i in range(2)]
        row = sb("row", [P, NT, E])
        slot_f = sb("slot_f", [P, 2, NT])
        block_start = sb("block_start", [1, MAX_BLOCKS + 1])
        past = sb("past", [1, MAX_BLOCKS + 1, E])
        expert_f = sb("expert_f", [1, MAX_BLOCKS + 1])
        rank_ps = ps("rank_ps", [P, NT, E])
        count_ps = ps("count_ps", [P, E])
        s_const = sem("const")
        s_step = sem("step")
        s_shift = sem("shift")
        s_exp = sem("exp")
        s_either = sem("either")
        s_rank = sem("rank")
        block = ctx.enter_context(nc.Block())

        @block.gpsimd
        def _(pool):
            pool.iota(rank_code[:], [[-1, E]], base=E, channel_multiplier=0,
                      allow_small_or_imprecise_dtypes=True).then_inc(s_const, 1)
            pool.iota(block_start[:], [[P, MAX_BLOCKS + 1]], base=0, channel_multiplier=0,
                      allow_small_or_imprecise_dtypes=True).then_inc(s_const, 1)
            pool.memset(ones[:], 1.0).then_inc(s_const, 1)
            pool.wait_ge(s_const, 3)
            pool.affine_select(out=earlier[:], in_=ones[:], compare_op=ALU.is_gt, fill=0.0, base=0,
                               pattern=[[1, P]], channel_multiplier=-1).then_inc(s_const, 1)
            split_low(pool)

        @block.sync
        def _(sp):
            load_weights(sp)

        @block.scalar
        def _(act):
            act.wait_ge(s_shift, 1)
            act.activation(probs[:], left[:], ACT.Exp).then_inc(s_exp, 1)
            split_high(act)

        @block.tensor
        def _(pe):
            pe.wait_ge(s_const, 4)
            pe.wait_ge(s_either, 1)
            pe.matmul(rank_ps[:], earlier[:], padded[:, NT - 1:, :], start=True, stop=False)
            for d in range(1, NT):
                pe.matmul(rank_ps[:], ones[:], padded[:, NT - 1 - d:2 * NT - 1 - d, :], start=False,
                          stop=(d == NT - 1))
            for t in range(NT):
                mm = pe.matmul(count_ps[:], ones[:], padded[:, NT - 1 + t, :], start=(t == 0), stop=(t == NT - 1))
            mm.then_inc(s_rank, 1)

        @block.vector
        def _(dve):
            step = Chain(dve, s_step)
            clear_lap(dve)

            def over_experts(a):
                return a.unsqueeze(2).to_broadcast([P, NT, E])
            codes = rank_code[:].unsqueeze(1).to_broadcast([P, NT, E])
            step(dve.memset(padded[:, 0:NT - 1, :], 0.0))
            step(dve.tensor_reduce(best[:], logits[:], AX, ALU.max))
            dve.tensor_tensor(left[:], logits[:], over_experts(best[:]), ALU.subtract).then_inc(s_shift, 1)
            dve.wait_ge(s_exp, 1)
            step(dve.tensor_reduce(best[:], probs[:], AX, ALU.add))
            step(dve.reciprocal(best[:], best[:]))
            step(dve.tensor_tensor(probs[:], probs[:], over_experts(best[:]), ALU.mult))
            dve.wait_ge(s_const, 4)
            scores = probs
            for k in range(2):
                step(dve.tensor_reduce(weight[:, k], scores[:], AX, ALU.max))
                step(dve.tensor_tensor(equal[:], scores[:], over_experts(weight[:, k]), ALU.is_equal))
                step(dve.tensor_tensor(equal[:], equal[:], codes, ALU.mult))
                step(dve.tensor_reduce(best[:], equal[:], AX, ALU.max))
                step(dve.tensor_tensor(chosen[:, k], codes, over_experts(best[:]), ALU.is_equal))
                if k == 0:
                    step(dve.scalar_tensor_tensor(left[:], chosen[:, 0], -4.0, probs[:], ALU.mult, ALU.add))
                    scores = left
            dve.tensor_tensor(padded[:, NT - 1:, :], chosen[:, 0], chosen[:, 1], ALU.add).then_inc(s_either, 1)
            dve.wait_ge(s_rank, 1)
            step(dve.tensor_scalar(count[:], count_ps[:], float(P - 1), None, ALU.add))
            step(dve.tensor_copy(count_i[:], count[:]))
            step(dve.tensor_scalar(count_i[:], count_i[:], ~(P - 1) & 0xffff, None, ALU.bitwise_and))
            step(dve.tensor_copy(count[:], count_i[:]))
            step(dve.tensor_copy(ends[0][:], count[:]))
            src = 0
            for d in (1, 2, 4):
                step(dve.tensor_copy(ends[1 - src][:, 0:d], ends[src][:, 0:d]))
                step(dve.tensor_tensor(ends[1 - src][:, d:E], ends[src][:, d:E], ends[src][:, 0:E - d], ALU.add))
                src = 1 - src
            end = ends[src]
            step(dve.tensor_tensor(past[:], end[0:1, :].unsqueeze(1).to_broadcast([1, MAX_BLOCKS + 1, E]),
                                   block_start[:].unsqueeze(2).to_broadcast([1, MAX_BLOCKS + 1, E]), ALU.is_le))
            step(dve.tensor_reduce(expert_f[:], past[:], AX, ALU.add))
            step(dve.tensor_scalar(expert_f[:], expert_f[:], float(E - 1), None, ALU.min))
            step(dve.tensor_copy(block_expert[:], expert_f[:]))
            step(dve.tensor_tensor(rest[:], end[:], count[:], ALU.subtract))
            step(dve.tensor_tensor(row[:], rank_ps[:], rest[:].unsqueeze(1).to_broadcast([P, NT, E]), ALU.add))
            for k in range(2):
                step(dve.tensor_tensor(equal[:], row[:], chosen[:, k], ALU.mult))
                step(dve.tensor_reduce(slot_f[:, k], equal[:], AX, ALU.add))
            step(dve.tensor_copy(slot[:], slot_f[:]))


def blocks(nc, tag, kind, w, src_tile, res_tile, out_tile, count, ident_d, raw=None, loaded=None,
           block_expert=None, load_next=None, next_loaded=None, slot=None, scatter_to=None, gather_from=None,
           weight=None):
    streamed = kind == "experts"
    with ExitStack() as ctx:
        sb, ps, sem = names(ctx, nc, tag)
        ident = sb("ident", [P, P])
        src = sb("src", [P, 2, D])
        xT = sb("xT", [P, 2, KC, P], F32R)
        act_gate = sb("act_gate", [P, 2, F])
        hidden = sb("hidden", [P, 2, F])
        hT = sb("hT", [P, FC, P], F32R)
        y = sb("y", [P, 2, D])
        xT_lo = sb("xT_lo", [P, 2, KC, P], F32R)
        hT_lo = sb("hT_lo", [P, FC, P], F32R)
        gu_hi, gu_lo, d_hi, d_lo = w
        if not streamed:
            res = sb("res", [P, 2, D])
        if gather_from is not None:
            rows = sb("rows", [P, 2, 2, D])
            part = sb("part", [P, 2, D])
        xt_ps = ps("xt_ps", [P, KC, P])
        gu_ps = ps("gu_ps", [P, 2, 2, 512])
        ht_ps = ps("ht_ps", [P, FC, P])
        y_ps = ps("y_ps", [P, 2, D])
        s_id = sem("id")
        s_src = [sem(f"src{i}") for i in range(2)]
        s_res = [sem(f"res{i}") for i in range(2)]
        s_rows = [sem(f"rows{i}") for i in range(2)]
        s_scatter = [sem(f"scatter{i}") for i in range(2)]
        s_xt = sem("xt")
        s_xT = sem("xT")
        s_xTl = sem("xTl")
        s_gu_ps = sem("gu_ps")
        s_guhi = sem("guhi")
        s_gulo = [sem(f"gulo{i}") for i in range(2)]
        s_gu_used = sem("gu_used")
        s_dhi = sem("dhi")
        s_dlo = sem("dlo")
        s_d_used = sem("d_used")
        s_gate = sem("gate")
        s_h = sem("h")
        s_ht = sem("ht")
        s_hT = sem("hT")
        s_hTl = sem("hTl")
        s_down = sem("down")
        s_part = sem("part")
        s_y = sem("y")
        s_store = [sem(f"store{i}") for i in range(2)]
        block = ctx.enter_context(nc.Block())
        loops = (count - 3) // 2
        middle = NT // 2 if streamed else None

        def stream(eng, step, middle=middle, between=None):
            for start, end in ((0, loops),) if middle is None else ((0, middle), (middle, loops)):
                with eng.Fori(start, end) as i:
                    for u in range(2):
                        step(2 * i + u, u, i, 4)
                if between is not None and start == 0:
                    between()
            for n in range(2 * loops, count):
                step(n, n % 2, n // 2, count - n)

        class Expert:

            def __init__(self, eng):
                self.eng, self.least = eng, 0

            def past_middle(self):
                self.least = 1

            def __call__(self, m):
                if isinstance(m, int) and m == count:
                    return 0
                return self.eng.value_load(block_expert[0:1, bass.ds(m, 1)], min_val=self.least, max_val=E - 1)

        def gu_raw(e, c):
            return raw[0][:, bass.ds(e, 1), c].rearrange("p e n -> p (e n)")

        def d_raw(e, j):
            return raw[1][:, bass.ds(e, 1), j].rearrange("p e n -> p (e n)")

        @block.sync
        def _(sp):
            sp.dma_start(ident[:], ident_d).then_inc(s_id, 16)
            for par in range(2):
                sp.sem_inc(s_store[par], 16)
                sp.dma_start(src[:, par], src_tile(par)).then_inc(s_src[par], 16)
                if not streamed:
                    sp.dma_start(res[:, par], res_tile(par)).then_inc(s_res[par], 16)

            def load_rows(m, par, i):
                sp.wait_ge(s_xt, m - 1)
                if scatter_to is not None:
                    sp.wait_ge(s_scatter[par], 32 * i)
                sp.dma_start(src[:, par], src_tile(m)).then_inc(s_src[par], 16)

            def step(m, par, i, left):
                if left >= 4:
                    load_rows(m + 3, 1 - par, i + 1 + par)
                sp.wait_ge(s_y, m + 3)
                sp.dma_start(out_tile(m), y[:, par]).then_inc(s_store[par], 16)
                if left >= 3 and not streamed:
                    sp.dma_start(res[:, par], res_tile(m + 2)).then_inc(s_res[par], 16)
            load_rows(2, 0, 1)
            if streamed:
                stream(sp, step, middle=middle + 1, between=lambda: load_next(sp))
            else:
                stream(sp, step)
            for par in range(2):
                sp.wait_ge(s_store[par], 16 * ((count + 1 - par) // 2 + 1))
                if scatter_to is not None:
                    sp.wait_ge(s_scatter[par], 32 * ((count + 1 - par) // 2))

        @block.tensor
        def _(pe):
            def transposes(m, par, i):
                pe.wait_ge(s_src[par], 16 * (i + 1))
                pe.wait_ge(s_xT, m + 1)
                pe.wait_ge(s_xTl, m + 1)
                for c in range(KC):
                    mm = pe.transpose(xt_ps[:, c, :], src[:, par, c * P:(c + 1) * P], ident[:])
                mm.then_inc(s_xt, 1)

            def gate_up(n, u, pieces):
                if 0 in pieces:
                    pe.wait_ge(s_xTl, n + 2)
                    pe.wait_ge(s_gate, n + 1)
                    pe.wait_ge(s_h, n + 1)
                for c in pieces:
                    if streamed:
                        pe.wait_ge(s_gulo[c % 2], 2 * n + c // 2 + 1)
                    for k in range(2):
                        f = slice(k * F, (k + 1) * F)
                        mm = matmul3(pe, gu_ps[:, u, k, 0:F], xT[:, u, c, :], xT_lo[:, u, c, :], gu_hi[:, c, f],
                                     gu_lo[:, c, f], c == 0, c == KC - 1)
                    if streamed:
                        mm.then_inc(s_gu_used, 1)
                if KC - 1 in pieces and not streamed:
                    mm.then_inc(s_gu_ps, 1)

            def hidden_transposes(n, u):
                pe.wait_ge(s_h, n + 3)
                pe.wait_ge(s_hT, n + 1)
                pe.wait_ge(s_hTl, n + 1)
                for j in range(FC):
                    f0 = min(j * P, F - P)
                    mm = pe.transpose(ht_ps[:, j, :], hidden[:, u, f0:f0 + P], ident[:])
                mm.then_inc(s_ht, 1)

            def down(n, u):
                pe.wait_ge(s_hTl, n + 2)
                pe.wait_ge(s_y, n + 1)
                for j in range(FC):
                    if streamed:
                        pe.wait_ge(s_dlo, FC * n + j + 1)
                    mm = matmul3(pe, y_ps[:, u, :], hT[:, j, :], hT_lo[:, j, :], d_hi[:, j, :], d_lo[:, j, :],
                                 j == 0, j == FC - 1)
                    if streamed:
                        mm.then_inc(s_d_used, 1)
                if not streamed:
                    mm.then_inc(s_down, 1)

            def step(n, u, i, left):
                if left >= 2:
                    gate_up(n + 1, 1 - u, range(KC // 2))
                hidden_transposes(n, u)
                if left >= 3:
                    transposes(n + 2, u, i + 1)
                if left >= 2:
                    gate_up(n + 1, 1 - u, range(KC // 2, KC))
                down(n, u)

            pe.wait_ge(s_id, 16)
            transposes(0, 0, 0)
            transposes(1, 1, 0)
            gate_up(0, 0, range(KC))
            stream(pe, step)

        def products_done(eng, n):
            if streamed:
                eng.wait_ge(s_gu_used, KC * (n + 1))
            else:
                eng.wait_ge(s_gu_ps, n + 1)

        def result_done(eng, n):
            if streamed:
                eng.wait_ge(s_d_used, FC * (n + 1))
            else:
                eng.wait_ge(s_down, n + 1)

        @block.scalar
        def _(act):
            expert = Expert(act)

            def rows_copy(m, par):
                act.wait_ge(s_xt, m + 1)
                if not isinstance(m, int) or m >= 2:
                    products_done(act, m - 2)
                act.activation(xT[:, par], xt_ps[:], ACT.Copy).then_inc(s_xT, 1)

            def silu(n, u):
                products_done(act, n)
                act.wait_ge(s_h, n + 1)
                act.activation(act_gate[:, u], gu_ps[:, u, 0, 0:F], ACT.Silu).then_inc(s_gate, 1)

            def gu_high(m, c, e):
                if not isinstance(m, int) or m >= 1:
                    act.wait_ge(s_gu_used, KC * (m - 1) + c + 1)
                act.activation(gu_hi[:, c], gu_raw(e, c), ACT.Copy).then_inc(s_guhi, 1)

            def d_high(m, e):
                for j in range(FC):
                    if not isinstance(m, int) or m >= 1:
                        act.wait_ge(s_d_used, FC * (m - 1) + j + 1)
                    act.activation(d_hi[:, j], d_raw(e, j), ACT.Copy).then_inc(s_dhi, 1)

            def hidden_copy(n):
                act.wait_ge(s_ht, n + 3)
                if not isinstance(n, int) or n >= 1:
                    result_done(act, n - 1)
                act.activation(hT[:], ht_ps[:], ACT.Copy).then_inc(s_hT, 1)

            def step(n, u, i, left):
                if streamed:
                    if left >= 2:
                        if left == 2:
                            act.wait_ge(next_loaded, 48)
                        e = expert(n + 2)
                        gu_high(n + 2, 0, e)
                        gu_high(n + 2, 1, e)
                    hidden_copy(n)
                    if left >= 3:
                        rows_copy(n + 2, u)
                    if left >= 2:
                        gu_high(n + 2, 2, e)
                        gu_high(n + 2, 3, e)
                        silu(n + 1, 1 - u)
                    d_high(n + 1, expert(n + 1))
                else:
                    hidden_copy(n)
                    if left >= 3:
                        rows_copy(n + 2, u)
                    if left >= 2:
                        silu(n + 1, 1 - u)
            act.sem_inc(s_xT, 1)
            act.sem_inc(s_gate, 2)
            act.sem_inc(s_hT, 1)
            rows_copy(0, 0)
            if streamed:
                act.wait_ge(loaded, 48 * E)
                e0, e1 = expert(0), expert(1)
                for c in range(KC):
                    gu_high(0, c, e0)
                rows_copy(1, 1)
                for c in range(KC):
                    gu_high(1, c, e1)
                silu(0, 0)
                d_high(0, e0)
            else:
                rows_copy(1, 1)
                silu(0, 0)
            stream(act, step, between=expert.past_middle)

        @block.vector
        def _(dve):
            expert = Expert(dve)

            def rows_low(m, par):
                dve.wait_ge(s_xT, m + 2)
                dve.tensor_tensor(xT_lo[:, par], xt_ps[:], xT[:, par].bitcast(F32), ALU.subtract).then_inc(s_xTl, 1)

            def product(n, u):
                dve.wait_ge(s_gate, n + 3)
                dve.wait_ge(s_ht, n + 1)
                dve.tensor_tensor(hidden[:, u], act_gate[:, u], gu_ps[:, u, 1, 0:F], ALU.mult).then_inc(s_h, 1)

            def gu_low(m, c, e):
                dve.wait_ge(s_guhi, KC * m + c + 1)
                dve.tensor_tensor(gu_lo[:, c], gu_raw(e, c), gu_hi[:, c].bitcast(F32), ALU.subtract).then_inc(
                    s_gulo[0], 1)

            def d_low(m, e):
                for j in range(FC):
                    dve.wait_ge(s_dhi, FC * m + j + 1)
                    dve.tensor_tensor(d_lo[:, j], d_raw(e, j), d_hi[:, j].bitcast(F32), ALU.subtract).then_inc(
                        s_dlo, 1)

            def gathered(m, par, i):
                dve.wait_ge(s_rows[par], 32 * (i + 1))
                dve.wait_ge(s_res[par], 16 * (i + 1))
                dve.scalar_tensor_tensor(part[:, 0], rows[:, par, 0], weight[:, 0, bass.ds(m, 1)], res[:, par],
                                         ALU.mult, ALU.add).then_inc(s_part, 1)
                dve.wait_ge(s_part, 2 * m + 1)
                dve.scalar_tensor_tensor(part[:, 1], rows[:, par, 1], weight[:, 1, bass.ds(m, 1)], part[:, 0],
                                         ALU.mult, ALU.add).then_inc(s_part, 1)
                dve.wait_ge(s_part, 2 * m + 2)

            def result(n, u, i):
                if gather_from is not None:
                    gathered(n, u, i)
                result_done(dve, n)
                dve.wait_ge(s_store[u], 16 * (i + 1))
                if gather_from is not None:
                    dve.tensor_tensor(y[:, u], part[:, 1], y_ps[:, u], ALU.add).then_inc(s_y, 1)
                elif streamed:
                    dve.tensor_copy(y[:, u], y_ps[:, u]).then_inc(s_y, 1)
                else:
                    dve.wait_ge(s_res[u], 16 * (i + 1))
                    dve.tensor_tensor(y[:, u], res[:, u], y_ps[:, u], ALU.add).then_inc(s_y, 1)

            def step(n, u, i, left):
                if streamed and left >= 2:
                    e = expert(n + 2)
                    gu_low(n + 2, 0, e)
                dve.wait_ge(s_hT, n + 2)
                dve.tensor_tensor(hT_lo[:], ht_ps[:], hT[:].bitcast(F32), ALU.subtract).then_inc(s_hTl, 1)
                if left >= 3:
                    rows_low(n + 2, u)
                if streamed and left >= 2:
                    gu_low(n + 2, 2, e)
                if left >= 2:
                    product(n + 1, 1 - u)
                if streamed:
                    d_low(n + 1, expert(n + 1))
                result(n, u, i)
            dve.sem_inc(s_xTl, 1)
            dve.sem_inc(s_hTl, 1)
            dve.sem_inc(s_h, 2)
            dve.sem_inc(s_ht, 2)
            dve.sem_inc(s_y, 2)
            rows_low(0, 0)
            if streamed:
                e0, e1 = expert(0), expert(1)
                gu_low(0, 0, e0)
                gu_low(0, 2, e0)
                rows_low(1, 1)
                gu_low(1, 0, e1)
                gu_low(1, 2, e1)
                product(0, 0)
                d_low(0, e0)
            else:
                rows_low(1, 1)
                product(0, 0)
            stream(dve, step, between=expert.past_middle)

        @block.gpsimd
        def _(pool):
            for m in range(count if slot is not None else 0):
                if scatter_to is not None:
                    pool.wait_ge(s_src[m % 2], 16 * (m // 2 + 1))
                    for k in range(2):
                        pool.indirect_dma_start(out=scatter_to, out_offset=bass.IndirectOffsetOnAxis(
                            ap=slot[:, k, m:m + 1], axis=0), in_=src[:, m % 2], in_offset=None).then_inc(
                                s_scatter[m % 2], 16)
                if gather_from is not None:
                    after(pool, s_part, 2 * (m - 1))
                    for k in range(2):
                        pool.indirect_dma_start(out=rows[:, m % 2, k], out_offset=None, in_=gather_from,
                                                in_offset=bass.IndirectOffsetOnAxis(ap=slot[:, k, m:m + 1], axis=0)
                                                ).then_inc(s_rows[m % 2], 16)
            if not streamed:
                return
            expert = Expert(pool)

            def gu_low(m):
                e = expert(m)
                for c in range(1, KC, 2):
                    pool.wait_ge(s_guhi, KC * m + c + 1)
                    pool.tensor_tensor(gu_lo[:, c], gu_raw(e, c), gu_hi[:, c].bitcast(F32), ALU.subtract).then_inc(
                        s_gulo[1], 1)

            def step(n, u, i, left):
                if left >= 2:
                    gu_low(n + 2)
            gu_low(0)
            gu_low(1)
            stream(pool, step, between=expert.past_middle)


def mixture(nc, tag, x_in, x_mid, x_out, xn_d, logits, sorted_d, y_d, gu, dn, ident_d):
    with ExitStack() as ctx:
        sb, ps, sem = names(ctx, nc, tag)
        weight = sb("weight", [P, 2, NT])
        slot = sb("slot", [P, 2, NT], I32)
        block_expert = sb("block_expert", [1, MAX_BLOCKS + 1], I32)
        gu_hi = sb("gu_hi", [P, KC, 2 * F], F32R)
        gu_lo = sb("gu_lo", [P, KC, 2 * F], F32R)
        d_hi = sb("d_hi", [P, FC, D], F32R)
        d_lo = sb("d_lo", [P, FC, D], F32R)
        shared_w = (gu_hi, gu_lo, d_hi, d_lo)
        s_raw = sem("raw")
        s_raw2 = sem("raw2")
        s_high = sem("high")
        s_low = sem("low")
        s_experts = sem("experts")
        s_lap = sem("lap")
        full = (FC - 1) * P

        def load(eng, source, w_gu, w_d, s):
            eng.dma_start(w_gu, gu[source]).then_inc(s, 16)
            eng.dma_start(w_d[:, 0:FC - 1], dn[source, 0:full].rearrange("(j p) n -> p j n", p=P)).then_inc(s, 16)
            eng.dma_start(w_d[LAP:P, FC - 1], dn[source, full:F]).then_inc(s, 16)

        with ExitStack() as inner:
            w_gu = inner.enter_context(nc.sbuf_tensor(tag + "w_gu", [P, E, KC, 2 * F], F32))
            w_d = inner.enter_context(nc.sbuf_tensor(tag + "w_d", [P, E, FC, D], F32))
            raw = E - 1

            def load_first(sp):
                load(sp, E, w_gu[:, raw], w_d[:, raw], s_raw)
                for e in range(E - 1):
                    load(sp, e, w_gu[:, e], w_d[:, e], s_experts)
                sp.wait_ge(s_low, 2)
                load(sp, E - 1, w_gu[:, E - 1], w_d[:, E - 1], s_experts)

            def clear_lap(dve):
                dve.memset(w_d[0:LAP, :, FC - 1, :], 0.0).then_inc(s_lap, 1)

            def split_high(act):
                act.wait_ge(s_lap, 1)
                act.wait_ge(s_raw, 48)
                act.activation(gu_hi[:], w_gu[:, raw], ACT.Copy).then_inc(s_high, 1)
                act.activation(d_hi[:], w_d[:, raw], ACT.Copy).then_inc(s_high, 1)

            def split_low(pool):
                pool.wait_ge(s_high, 1)
                pool.tensor_tensor(gu_lo[:], w_gu[:, raw], gu_hi[:].bitcast(F32), ALU.subtract).then_inc(s_low, 1)
                pool.wait_ge(s_high, 2)
                pool.tensor_tensor(d_lo[:], w_d[:, raw], d_hi[:].bitcast(F32), ALU.subtract).then_inc(s_low, 1)

            route(nc, tag + "r", logits, weight, slot, block_expert, load_first, split_high, split_low, clear_lap)
            tile_of = lambda a: lambda m: a[bass.ds(m * P, P), :]
            blocks(nc, tag + "s", "shared", shared_w, tile_of(xn_d), tile_of(x_in), tile_of(x_mid), NT, ident_d,
                   slot=slot, scatter_to=sorted_d)
            blocks(nc, tag + "e", "experts", shared_w, tile_of(sorted_d), None, tile_of(y_d), MAX_BLOCKS, ident_d,
                   raw=(w_gu, w_d), loaded=s_experts, block_expert=block_expert,
                   load_next=lambda sp: load(sp, E + 1, w_gu[:, 0], w_d[:, 0], s_raw2), next_loaded=s_raw2)
        blocks(nc, tag + "f", "shared", shared_w, tile_of(xn_d), tile_of(x_mid), tile_of(x_out), NT, ident_d,
               slot=slot, gather_from=y_d, weight=weight)


def program(nc, ins, out):
    def dram(name, shape):
        return nc.dram_tensor(name, shape, F32, kind="Internal").ap()
    x = ins["x"].rearrange("b t d -> (b t) d")
    out = out.rearrange("b t d -> (b t) d")
    ident_d = ins["ident"]
    sorted_d = dram("sorted_rows", (MAX_BLOCKS * P, D))
    y_d = dram("expert_rows", (MAX_BLOCKS * P, D))
    a_d = dram("a", (B, P, KC * HS))
    v_d = dram("v", (B, H, S, D))
    x1, x2, x3, x4, x5 = (dram(f"x{i}", (B * T, D)) for i in range(1, 6))
    xn_d = dram("xn", (B * T, D))

    def stage_out(n, tensor):
        return out if n == STAGES else tensor
    prep(nc, "p0", 8, ins["ctx_t"], ins["wk0"], ins["wv0"], ins["wq_t0"], ins["wo0"], None, None, ins["mask"],
         ident_d, a_d, v_d)
    with ExitStack() as ctx:
        logits = ctx.enter_context(nc.sbuf_tensor("logits0", [P, NT, E], F32))
        attend(nc, "t0", x, stage_out(1, x1), xn_d, logits, ins["gate_t0"], a_d, v_d, None, ins["mask"], ident_d,
               zero_rows=sorted_d)
        if STAGES == 1:
            return
        mixture(nc, "m0", x1, x2, stage_out(2, x3), xn_d, logits, sorted_d, y_d, ins["gu0"], ins["dn0"], ident_d)
    if STAGES == 2:
        return
    prep(nc, "p1", 16, ins["ctx_t"], ins["wk1"], ins["wv1"], ins["wq_t1"], ins["wo1"], ins["gq"], ins["gk"], None,
         ident_d, a_d, v_d)
    with ExitStack() as ctx:
        logits = ctx.enter_context(nc.sbuf_tensor("logits1", [P, NT, E], F32))
        attend(nc, "t1", x3, stage_out(3, x4), xn_d, logits, ins["gate_t1"], a_d, v_d, ins["wq1"], None, ident_d)
        if STAGES == 3:
            return
        mixture(nc, "m1", x4, x5, out, xn_d, logits, sorted_d, y_d, ins["gu1"], ins["dn1"], ident_d)


def kernel(**inputs):
    import numpy as np
    import concourse.bacc as bacc
    from concourse.bass_utils import run_bass_kernel_spmd as run

    a = {k: np.asarray(v) for k, v in inputs.items()}

    def chunks(w):
        return np.swapaxes(w.reshape(w.shape[:-2] + (KC, P, w.shape[-1])), -3, -2)

    def gate_up(experts, shared_gate, shared_up):
        halves = np.concatenate([shared_gate.reshape(NJ, F, D), shared_up.reshape(NJ, F, D)], axis=1)
        return chunks(np.swapaxes(np.concatenate([experts, halves], axis=0), 1, 2))

    def down(experts, shared):
        return np.concatenate([np.swapaxes(experts, 1, 2), shared.T.reshape(NJ, F, D)], axis=0)

    sgu = a["L0_ffn_shared_gate_up"]
    data = {
        "x": a["x"], "ctx_t": a["ctx_1024"].reshape(BS, CD).T, "mask": a["mask_BxS2_bf1"],
        "ident": np.eye(P, dtype=np.float32),
        "wk0": a["L0_xattn_Wk"], "wv0": a["L0_xattn_Wv"], "wq_t0": a["L0_xattn_Wq"].T, "wo0": a["L0_xattn_Wo"],
        "wk1": a["L1_xattn_Wk"], "wv1": a["L1_xattn_Wv"], "wq_t1": a["L1_xattn_Wq"].T, "wo1": a["L1_xattn_Wo"],
        "wq1": a["L1_xattn_Wq"], "gq": a["L1_xattn_gq"], "gk": a["L1_xattn_gk"],
        "gate_t0": a["L0_ffn_gate_weight"].T,
        "gu0": gate_up(a["L0_ffn_gate_up_weights"], sgu[:NJ * F], sgu[NJ * F:]),
        "dn0": down(a["L0_ffn_down_weights"], a["L0_ffn_shared_down"]),
        "gate_t1": a["L1_ffn_gate_w"].T,
        "gu1": gate_up(np.concatenate([a["L1_ffn_w1"], a["L1_ffn_w2"]], axis=1), a["L1_ffn_sw1"], a["L1_ffn_sw2"]),
        "dn1": down(a["L1_ffn_w3"], a["L1_ffn_sw3"]),
    }
    nc = bacc.Bacc("TRN2", target_bir_lowering=False, num_devices=1)
    arrays, ins = {}, {}
    for name, value in data.items():
        value = np.ascontiguousarray(value)
        arrays[f"in_{name}"] = value
        ins[name] = nc.dram_tensor(f"in_{name}", value.shape, mybir.dt.from_np(value.dtype), kind="ExternalInput").ap()
    out = nc.dram_tensor("out", (B, T, D), F32, kind="ExternalOutput").ap()
    program(nc, ins, out)
    return run(nc, [arrays], core_ids=[0]).results[0]["out"]
```

```python
from contextlib import ExitStack

import concourse.bass as bass
from concourse import mybir

ALU = mybir.AluOpType
ACT = mybir.ActivationFunctionType
F32 = mybir.dt.float32
F32R = mybir.dt.float32r
I32 = mybir.dt.int32
U8 = mybir.dt.uint8
AX = mybir.AxisListType.X

P = 128
B, T, D = 4, 512, 512
KC = D // P
NT = B * T // P
TB = T // P
H, DH, S, CD = 16, 128, 64, 256
HS = H * S
BS = B * S
CC = CD // P
HG = 4
NG = H // HG
NQ = HS // P
PARTS = 4
E, F = 8, 352
NJ = 2
FC = -(-F // P)
LAP = FC * P - F
MAX_BLOCKS = (2 * NT * P + E * (P - 1)) // P
ZERO_BLOCKS = MAX_BLOCKS // (NT - TB + 1)
EPS = 1e-5
SCALE = float(DH) ** -0.5
MASKED = -(2.0 ** 100)


assert ZERO_BLOCKS * (NT - TB + 1) == MAX_BLOCKS
assert NT == 2 * E


def after(eng, sem, value):
    if not isinstance(value, int) or value > 0:
        eng.wait_ge(sem, value)


class Chain:

    def __init__(self, eng, sem):
        self.eng, self.sem, self.n = eng, sem, 0

    def __call__(self, ins):
        self.n += 1
        ins.then_inc(self.sem, 1)
        self.eng.wait_ge(self.sem, self.n)


def names(ctx, nc, tag):
    def sb(name, shape, dt=F32):
        return ctx.enter_context(nc.sbuf_tensor(f"{tag}_{name}", shape, dt))

    def ps(name, shape, dt=F32):
        return ctx.enter_context(nc.psum_tensor(f"{tag}_{name}", shape, dt))

    sems = []

    def sem(name):
        sems.append(nc.alloc_semaphore(f"{tag}_{name}"))
        return sems[-1]

    def release():
        if sems:
            nc.clear_and_free_semaphores(sems)
            nc.all_engine_barrier()
    ctx.callback(release)
    return sb, ps, sem


def matmul3(pe, out, hi_w, lo_w, hi_x, lo_x, start, stop):
    pe.matmul(out, hi_w, hi_x, start=start, stop=False)
    pe.matmul(out, hi_w, lo_x, start=False, stop=False)
    return pe.matmul(out, lo_w, hi_x, start=False, stop=stop)


def prep(nc, tag, kv_heads, ctx_t, wk, wv, wq_t, wo, gq, gk, mask, a_d, v_d, early):
    normed = gq is not None
    rep = H // kv_heads
    GK = HG // rep
    cols = GK * DH
    with ExitStack() as ctx:
        sb, ps, sem = names(ctx, nc, tag)
        ctx_sb = sb("ctx", [P, CC, BS])
        wk_sb = sb("wk", [P, 2, CC, cols])
        wv_sb = sb("wv", [P, 2, CC, cols])
        wq_sb = sb("wq", [P, 2, HG, D])
        wo_sb = sb("wo", [P, 2, HG, D])
        kT = sb("kT", [P, 2, GK, BS])
        vT = sb("vT", [P, 2, GK, BS])
        a_st = sb("a_st", [P, 2, KC, B, HG * S])
        v_st = sb("v_st", [P, 2, 2, HG, D])
        maskcol = sb("maskcol", [P, 2])
        mask_u8 = sb("mask_u8", [P, 2], U8)
        if normed:
            gq_sb = sb("gq", [P, 1])
            gk_sb = sb("gk", [P, 1])
            g_sb = sb("g", [P, 1])
            eps = sb("eps", [P, 1])
            ones = sb("ones", [P, P])
            ksq = sb("ksq", [P, GK, BS])
            krs = sb("krs", [P, GK, BS])
        k_ps = ps("k_ps", [P, GK, 256])
        v_ps = ps("v_ps", [P, GK, 256])
        unit_ps = ps("unit_ps", [P, 2, 1024])

        s_ctx = sem("ctx")
        s_small = sem("small")
        s_wkv = [sem(f"wkv{i}") for i in range(2)]
        s_wqo = [sem(f"wqo{i}") for i in range(2)]
        s_g = sem("g")
        s_kproj = sem("kproj")
        s_vproj = sem("vproj")
        s_sq = sem("sq")
        s_ss = sem("ss")
        s_rs = sem("rs")
        s_rec = sem("rec")
        s_maskcol = sem("maskcol")
        s_root = sem("root")
        s_k = sem("k")
        s_v = sem("v")
        s_aunit = sem("aunit")
        s_vunit = sem("vunit")
        s_acopy = sem("acopy")
        s_vcopy = sem("vcopy")
        s_astored = [sem(f"astored{i}") for i in range(2)]
        s_vstored = [sem(f"vstored{i}") for i in range(2)]

        STORES = 16 * B * 2
        wk_v = wk.rearrange("(c p) n -> p c n", p=P)
        wv_v = wv.rearrange("(c p) n -> p c n", p=P)
        wq_v = wq_t.rearrange("(h d) n -> d h n", d=DH)
        wo_v = wo.rearrange("(h d) n -> d h n", d=DH)
        block = ctx.enter_context(nc.Block())

        def groups(eng, step):
            for g in range(NG):
                step(g, g % 2, g // 2, NG - 1 - g)

        @block.sync
        def _(sp):
            sp.dma_start(ctx_sb[:], ctx_t.rearrange("(c p) n -> p c n", p=P)).then_inc(s_ctx, 16)

            def load_kv(g, par):
                sp.dma_start(wk_sb[:, par], wk_v[:, :, bass.ds(g * cols, cols)]).then_inc(s_wkv[par], 16)
                sp.dma_start(wv_sb[:, par], wv_v[:, :, bass.ds(g * cols, cols)]).then_inc(s_wkv[par], 16)

            def load_qo(g, par):
                sp.dma_start(wo_sb[:, par], wo_v[:, bass.ds(g * HG, HG), :]).then_inc(s_wqo[par], 16)
                sp.dma_start(wq_sb[:, par], wq_v[:, bass.ds(g * HG, HG), :]).then_inc(s_wqo[par], 16)
            load_kv(0, 0)
            load_qo(0, 0)
            load_kv(1, 1)
            load_qo(1, 1)
            for par in range(2):
                sp.sem_inc(s_vstored[par], STORES)
            if NG > 2:
                sp.wait_ge(s_vproj, 1)
                load_kv(2, 0)
            early(sp)

            def step(g, par, i, last):
                if last >= 3:
                    sp.wait_ge(s_vproj, g + 2)
                    load_kv(g + 3, 1 - par)
                for half in range(2):
                    heads = slice(half * HG // 2, (half + 1) * HG // 2)
                    sp.wait_ge(s_vcopy, HG * g + heads.stop + 1)
                    for b in range(B):
                        sp.dma_start(v_d[b, bass.ds(g * HG + heads.start, HG // 2)].rearrange("h s n -> s h n"),
                                     v_st[(b % 2) * S:(b % 2 + 1) * S, par, b // 2, heads]).then_inc(
                                         s_vstored[par], 16)
                if last >= 2:
                    sp.wait_ge(s_aunit, HG * (g + 1))
                    sp.wait_ge(s_vunit, HG * (g + 1))
                    load_qo(g + 2, par)
            groups(sp, step)
            for par in range(2):
                sp.wait_ge(s_vstored[par], STORES * (NG // 2 + 1))

        @block.tensor
        def _(pe):
            pe.wait_ge(s_ctx, 16)

            def project(g, par, i):
                pe.wait_ge(s_wkv[par], 32 * (i + 1))
                pe.wait_ge(s_k, GK * (g + 1))
                for h in range(GK):
                    for c in range(CC):
                        mm = pe.matmul(k_ps[:, h, 0:BS], wk_sb[:, par, c, h * DH:(h + 1) * DH], ctx_sb[:, c, :],
                                       start=(c == 0), stop=(c == CC - 1))
                mm.then_inc(s_kproj, 1)
                pe.wait_ge(s_v, g + 1)
                for h in range(GK):
                    for c in range(CC):
                        mm = pe.matmul(v_ps[:, h, 0:BS], wv_sb[:, par, c, h * DH:(h + 1) * DH], ctx_sb[:, c, :],
                                       start=(c == 0), stop=(c == CC - 1))
                mm.then_inc(s_vproj, 1)

            def key_sums(g):
                if normed:
                    if g == 0:
                        pe.wait_ge(s_g, 1)
                    pe.wait_ge(s_sq, 2 * (g + 1))
                    for h in range(GK):
                        mm = pe.matmul(k_ps[:, h, 0:BS], ones[:], ksq[:, h, :], start=True, stop=True)
                    mm.then_inc(s_ss, 1)

            def units(g, par, some):
                for u in some:
                    pe.wait_ge(s_vcopy, HG * g + u + 1)
                    h = u // rep
                    for p in range(2):
                        mm = pe.matmul(unit_ps[:, 0, p * 512:(p + 1) * 512], vT[:, par, h, p * P:(p + 1) * P],
                                       wo_sb[:, par, u, :], start=True, stop=True)
                    mm.then_inc(s_vunit, 1)
                    if u % rep == 0:
                        pe.wait_ge(s_k, GK * (g + 1) + h + 1)
                    pe.wait_ge(s_acopy, HG * g + u + 1)
                    for c in range(KC):
                        mm = pe.matmul(unit_ps[:, 1, c * BS:(c + 1) * BS], wq_sb[:, par, u, c * P:(c + 1) * P],
                                       kT[:, par, h, :], start=True, stop=True)
                    mm.then_inc(s_aunit, 1)

            def step(g, par, i, last):
                if last:
                    project(g + 1, 1 - par, i + par)
                pe.wait_ge(s_wqo[par], 32 * (i + 1))
                pe.wait_ge(s_v, g + 2)
                units(g, par, range(1))
                if last:
                    key_sums(g + 1)
                units(g, par, range(1, HG))
            project(0, 0, 0)
            key_sums(0)
            groups(pe, step)

        @block.scalar
        def _(act):
            act.sem_inc(s_acopy, 1)
            for par in range(2):
                act.sem_inc(s_astored[par], STORES)

            def squares(g):
                if normed:
                    act.wait_ge(s_sq, 2 * g + 1)
                    act.wait_ge(s_rs, g + 1)
                    act.activation(ksq[:], k_ps[:, :, 0:BS], ACT.Square).then_inc(s_sq, 1)

            def roots(g):
                if normed:
                    act.wait_ge(s_ss, g + 1)
                    act.activation(krs[:], k_ps[:, :, 0:BS], ACT.Sqrt, scale=1.0 / DH, bias=eps[:, 0:1]).then_inc(
                        s_root, 1)

            def a_copies(g, par, some):
                for u in some:
                    act.wait_ge(s_aunit, HG * g + u + 1)
                    act.activation(a_st[:, par, :, :, u * S:(u + 1) * S],
                                   unit_ps[:, 1, :].rearrange("p (c b s) -> p c b s", c=KC, b=B),
                                   ACT.Copy).then_inc(s_acopy, 1)

            def stores(g, par, half):
                heads = half * HG // 2
                act.wait_ge(s_acopy, HG * g + heads + HG // 2 + 1)
                for b in range(B):
                    act.dma_start(a_d[b].rearrange("p (c n) -> p c n", c=KC)[
                        :, :, bass.ds((g * HG + heads) * S, HG // 2 * S)],
                                  a_st[:, par, :, b, heads * S:(heads + HG // 2) * S]).then_inc(s_astored[par], 16)

            def step(g, par, i, last):
                if last:
                    squares(g + 1)
                act.wait_ge(s_astored[par], STORES * (i + 1))
                a_copies(g, par, range(1))
                if last:
                    roots(g + 1)
                a_copies(g, par, range(1, HG // 2))
                stores(g, par, 0)
                a_copies(g, par, range(HG // 2, HG))
                stores(g, par, 1)
            if normed:
                act.wait_ge(s_g, 1)
            squares(0)
            roots(0)
            groups(act, step)
            for par in range(2):
                act.wait_ge(s_astored[par], STORES * (NG // 2 + 1))

        @block.vector
        def _(dve):
            dve.sem_inc(s_vcopy, 1)
            dve.sem_inc(s_k, GK)
            dve.sem_inc(s_v, 1)
            if normed:
                dve.memset(ones[:], 1.0)
                dve.memset(eps[:], EPS)
            dve.wait_ge(s_small, 32)
            if mask is not None:
                dve.tensor_copy(maskcol[:], mask_u8[:]).then_inc(s_maskcol, 1)
            else:
                dve.memset(maskcol[:], 1.0).then_inc(s_maskcol, 1)
            if normed:
                dve.sem_inc(s_rs, 1)
                dve.tensor_tensor(g_sb[:], gq_sb[:], gk_sb[:], ALU.mult).then_inc(s_g, 1)

            def projected(g, par):
                dve.wait_ge(s_kproj, g + 1)
                if normed:
                    dve.tensor_scalar(kT[:, par], k_ps[:, :, 0:BS], g_sb[:, 0:1], None, ALU.mult).then_inc(s_sq, 1)
                else:
                    dve.tensor_copy(kT[:, par], k_ps[:, :, 0:BS]).then_inc(s_k, GK)
                dve.wait_ge(s_vproj, g + 1)
                dve.tensor_copy(vT[:, par], v_ps[:, :, 0:BS]).then_inc(s_v, 1)

            def normalise(g, par, heads):
                if normed:
                    dve.wait_ge(s_root, g + 1)
                    for h in heads:
                        dve.reciprocal(krs[:, h], krs[:, h]).then_inc(s_rec, 1)
                        dve.wait_ge(s_rec, GK * g + h + 1)
                        dve.tensor_tensor(kT[:, par, h], kT[:, par, h], krs[:, h], ALU.mult).then_inc(s_k, 1)
                    if GK - 1 in heads:
                        dve.wait_ge(s_k, GK * (g + 2))
                        dve.sem_inc(s_rs, 1)

            def v_copies(g, par, some):
                for u in some:
                    dve.wait_ge(s_vunit, HG * g + u + 1)
                    dve.tensor_tensor(v_st[:, par, :, u, :], unit_ps[:, 0, :].rearrange("p (a n) -> p a n", a=2),
                                      maskcol[:].unsqueeze(2).to_broadcast([P, 2, D]), ALU.mult).then_inc(s_vcopy, 1)

            def step(g, par, i, last):
                if last:
                    projected(g + 1, 1 - par)
                dve.wait_ge(s_vstored[par], STORES * (i + 1))
                v_copies(g, par, range(2))
                if last:
                    normalise(g + 1, 1 - par, range(GK // 2))
                v_copies(g, par, range(2, 3))
                if last:
                    normalise(g + 1, 1 - par, range(GK // 2, GK))
                v_copies(g, par, range(3, HG))
            if normed:
                dve.wait_ge(s_g, 1)
            projected(0, 0)
            normalise(0, 0, range(GK))
            dve.wait_ge(s_maskcol, 1)
            groups(dve, step)

        @block.gpsimd
        def _(pool):
            if mask is not None:
                for p in range(2):
                    pool.dma_start(mask_u8[:, p:p + 1], mask[2 * p:2 * p + 2, :].rearrange("b (s o) -> (b s) o", o=1)
                                   ).then_inc(s_small, 16)
            else:
                pool.dma_start(gq_sb[:], gq.rearrange("(d o) -> d o", o=1)).then_inc(s_small, 16)
                pool.dma_start(gk_sb[:], gk.rearrange("(d o) -> d o", o=1)).then_inc(s_small, 16)


def moments(dve, sem, count, x, stats, mv, carrier):
    dve.bn_stats(stats, x).then_inc(sem, 1)
    dve.wait_ge(sem, count + 1)
    dve.memset(carrier, 0.0)
    dve.bn_aggr(mv, stats).then_inc(sem, 1)
    dve.wait_ge(sem, count + 2)
    dve.tensor_scalar(mv[:, 1:2], mv[:, 1:2], EPS, None, ALU.add).then_inc(sem, 1)


def tiles(eng, step):
    step(0, 0, 0, NT)
    with eng.Fori(0, B - 1) as b:
        for j in range(1, TB + 1):
            step(TB * b + j, j % TB, b + j // TB, TB)
    for t in range(TB * (B - 1) + 1, NT):
        step(t, t % TB, B - 1, NT - t)


def wq_staged(a_raw, v_raw, n):
    return (a_raw, v_raw)[n // 2][:, n % 2 * KC * 512:(n % 2 + 1) * KC * 512].rearrange("p (c n) -> p c n", c=KC)


def attend(nc, tag, x, s_x, a_raw, v_raw, s_wqraw, x_in, x_out, xn_out, logits, gate_t, a_d, v_d, mask, ident,
           s_ident, zero_rows=None):
    normed = s_wqraw is not None
    with ExitStack() as ctx:
        sb, ps, sem = names(ctx, nc, tag)
        a_hi = sb("a_hi", [P, KC, HS], F32R)
        a_lo = sb("a_lo", [P, KC, HS], F32R)
        v_hi = sb("v_hi", [P, NQ, D], F32R)
        v_lo = sb("v_lo", [P, NQ, D], F32R)
        xn = sb("xn", [P, D])
        stats = sb("stats", [P, 6])
        mv = sb("mv", [P, 2])
        carrier = sb("carrier", [P, 1])
        rstd = sb("rstd", [P, 1])
        power = sb("power", [P, 1])
        x_hi = sb("x_hi", [P, 2, KC, P], F32R)
        x_lo = sb("x_lo", [P, 2, KC, P], F32R)
        top = sb("top", [P, H])
        z = sb("z", [P, H, S])
        p_sb = sb("p", [P, H, S])
        total = sb("total", [P, H])
        recip = sb("recip", [P, H])
        p_hi = sb("p_hi", [P, NQ, P], F32R)
        p_lo = sb("p_lo", [P, NQ, P], F32R)
        y = sb("y", [P, D])
        mv2 = sb("mv2", [P, 2])
        rstd2 = sb("rstd2", [P, 1])
        xn2 = sb("xn2", [P, D])
        xT2 = sb("xT2", [P, KC, P])
        gate_sb = sb("gate", [P, KC, E])
        if normed:
            wq_hi = sb("wq_hi", [P, KC, H * DH], F32R)
            wq_lo = sb("wq_lo", [P, KC, H * DH], F32R)
            qsq = sb("qsq", [P, 512])
            ssq = sb("ssq", [P, H])
            rq = sb("rq", [P, H])
        if zero_rows is not None:
            zeros = sb("zeros", [P, D])
        if mask is not None:
            mask_u8 = sb("mask_u8", [1, BS], U8)
            maskf = sb("maskf", [1, B, S])
            bias = sb("bias", [1, B, S], F32R)
            one_f = sb("one_f", [1, P])
            one_row = sb("one_row", [1, P], F32R)
        xt_ps = ps("xt_ps", [P, KC, P])
        s_ps = ps("s_ps", [P, H, S])
        pt_ps = ps("pt_ps", [P, NQ, P])
        o_ps = ps("o_ps", [P, D])
        NQG = H * DH // 512
        a_raw3 = a_raw[:].rearrange("p (c n) -> p c n", c=KC)
        v_raw3 = v_raw[:].rearrange("p (q n) -> p q n", q=NQ)
        a_part = lambda a, i: a[:, :, i * HS // PARTS:(i + 1) * HS // PARTS]
        v_part = lambda v, i: v[:, i * NQ // PARTS:(i + 1) * NQ // PARTS, :]
        if normed:
            wq_raw = lambda n: wq_staged(a_raw, v_raw, n)
            wq_part = lambda w, n: w[:, :, n * 512:(n + 1) * 512]
        if normed:
            q_ps = ps("q_ps", [P, 2, 512])

        s_araw = [sem(f"araw{i}") for i in range(PARTS)]
        s_vraw = [sem(f"vraw{i}") for i in range(PARTS)]
        s_ahi = sem("ahi")
        s_alo = [sem(f"alo{i}") for i in range(2)]
        s_vhi = sem("vhi")
        s_vlo = [sem(f"vlo{i}") for i in range(2)]
        s_ln = sem("ln")
        s_rstd = sem("rstd")
        s_xn = sem("xn")
        s_xt = sem("xt")
        s_xhi = sem("xhi")
        s_xlo = sem("xlo")
        s_scores = sem("scores")
        s_top = sem("top")
        s_sub = sem("sub")
        s_zq = sem("zq")
        s_exp = sem("exp")
        s_sum = sem("sum")
        s_rec = sem("rec")
        s_prob = sem("prob")
        s_pt = sem("pt")
        s_phi = sem("phi")
        s_plo = sem("plo")
        s_o = sem("o")
        s_y = sem("y")
        s_store = sem("store")
        s_ln2 = sem("ln2")
        s_rstd2 = sem("rstd2")
        s_xn2 = sem("xn2")
        s_keep = sem("keep")
        s_xt2 = sem("xt2")
        s_xT2 = sem("xT2")
        s_gatew = sem("gatew")
        s_gate = sem("gate")
        s_logits = sem("logits")
        s_q = sem("q")
        s_qsq = sem("qsq")
        s_qsum = sem("qsum")
        s_rq = sem("rq")
        s_rqp = sem("rqp")
        s_wqhi = sem("wqhi")
        s_wqlo = [sem(f"wqlo{i}") for i in range(2)]
        s_mask = sem("mask")
        s_bias = sem("bias")
        s_zero = sem("zero")
        s_zeroed = sem("zeroed")

        block = ctx.enter_context(nc.Block())

        @block.sync
        def _(sp):
            def load_a(b):
                a_b = a_d[bass.ds(b, 1)].rearrange("b p (c n) -> p (b c) n", c=KC)
                for i in range(PARTS):
                    sp.dma_start(a_part(a_raw3, i), a_part(a_b, i)).then_inc(s_araw[i], 16)

            def load_v(b):
                v_b = v_d[bass.ds(b, 1)].rearrange("b (q a) s n -> (a s) (b q) n", a=2)
                for i in range(PARTS):
                    sp.dma_start(v_part(v_raw3, i), v_part(v_b, i)).then_inc(s_vraw[i], 16)

            sp.sem_inc(s_keep, 16)
            sp.sem_inc(s_store, 16)
            if mask is not None:
                sp.dma_start(mask_u8[:], mask.rearrange("(o b) s -> o (b s)", o=1)).then_inc(s_mask, 16)
            if normed:
                sp.wait_ge(s_wqlo[0], 2)
            load_a(0)
            sp.dma_start(gate_sb[:], gate_t.rearrange("(c p) e -> p c e", p=P)).then_inc(s_gatew, 16)
            if normed:
                sp.wait_ge(s_wqlo[1], 2)
            load_v(0)

            def step(t, j, b, left):
                if left >= 4 and not isinstance(t, int):
                    sp.dma_start(x[:, (j + 3) % TB], x_in[bass.ds((t + 3) * P, P), :]).then_inc(
                        s_x[(j + 3) % TB], 16)
                if j == 1 and left >= 4:
                    for half in range(2):
                        sp.wait_ge(s_alo[half], 2 * (b + 1))
                    load_a(b + 1)
                    for half in range(2):
                        sp.wait_ge(s_vlo[half], 2 * (b + 1))
                    load_v(b + 1)
                if zero_rows is not None and left >= TB:
                    sp.wait_ge(s_zero, 1)
                    sp.dma_start(zero_rows[bass.ds(t * ZERO_BLOCKS * P, ZERO_BLOCKS * P), :].rearrange(
                        "(n p) d -> p n d", p=P), zeros[:].unsqueeze(1).to_broadcast([P, ZERO_BLOCKS, D])
                                 ).then_inc(s_zeroed, 16)
                sp.wait_ge(s_y, t + 2)
                sp.dma_start(x_out[bass.ds(t * P, P), :], y[:]).then_inc(s_store, 16)
                sp.wait_ge(s_xn2, t + 1)
                sp.dma_start(xn_out[bass.ds(t * P, P), :], xn2[:]).then_inc(s_keep, 16)
            tiles(sp, step)
            sp.wait_ge(s_store, 16 * (NT + 1))
            sp.wait_ge(s_keep, 16 * (NT + 1))
            if zero_rows is not None:
                sp.wait_ge(s_zeroed, 16 * (MAX_BLOCKS // ZERO_BLOCKS))

        @block.tensor
        def _(pe):
            def transposes(t):
                pe.wait_ge(s_xn, t + 1)
                pe.wait_ge(s_xlo, t + 1)
                if not isinstance(t, int) or t >= 3:
                    pe.wait_ge(s_xT2, t - 2)
                for c in range(KC):
                    mm = pe.transpose(xt_ps[:, c, :], xn[:, c * P:(c + 1) * P], ident[:])
                mm.then_inc(s_xt, 1)

            def queries(t, j):
                pe.wait_ge(s_xlo, t + 2)
                for n in range(NQG):
                    if isinstance(t, int) and t == 0:
                        pe.wait_ge(s_wqlo[n // 2], n % 2 + 1)
                    pe.wait_ge(s_qsq, NQG * t + n + 1)
                    for c in range(KC):
                        mm = matmul3(pe, q_ps[:, n % 2, :], x_hi[:, j % 2, c, :], x_lo[:, j % 2, c, :],
                                     wq_hi[:, c, n * 512:(n + 1) * 512], wq_lo[:, c, n * 512:(n + 1) * 512],
                                     c == 0, c == KC - 1)
                    mm.then_inc(s_q, 1)

            def scores(t, j, b, half):
                if half == 0:
                    pe.wait_ge(s_xlo, t + 2)
                    pe.wait_ge(s_sub, t + 1)
                if j == 0:
                    pe.wait_ge(s_alo[half], 2 * (b + 1))
                out = s_ps[:, half * 8:(half + 1) * 8, :]
                cols = slice(half * 512, (half + 1) * 512)
                for c in range(KC):
                    mm = matmul3(pe, out, x_hi[:, j % 2, c, :], x_lo[:, j % 2, c, :], a_hi[:, c, cols],
                                 a_lo[:, c, cols], c == 0, c == KC - 1 and mask is None)
                if mask is not None:
                    mm = pe.matmul(out, one_row[:], bias[:, bass.ds(b, 1), :].to_broadcast([1, H // 2, S]),
                                   start=False, stop=True)
                mm.then_inc(s_scores, 1)

            def prob_transposes(t):
                pe.wait_ge(s_prob, t + 1)
                pe.wait_ge(s_plo, t + 1)
                for q in range(NQ):
                    mm = pe.transpose(pt_ps[:, q, :], p_sb[:, 2 * q:2 * q + 2, :].rearrange("p a s -> p (a s)"),
                                      ident[:])
                mm.then_inc(s_pt, 1)

            def outputs(t, j, b):
                pe.wait_ge(s_plo, t + 2)
                pe.wait_ge(s_y, t + 1)
                after(pe, s_logits, t)
                for q in range(NQ):
                    if j == 0 and q % (NQ // 2) == 0:
                        pe.wait_ge(s_vlo[q // (NQ // 2)], 2 * (b + 1))
                    mm = matmul3(pe, o_ps[:], p_hi[:, q, :], p_lo[:, q, :], v_hi[:, q, :], v_lo[:, q, :],
                                 q == 0, q == NQ - 1)
                mm.then_inc(s_o, 1)

            def result_transposes(t):
                pe.wait_ge(s_xn2, t + 1)
                for c in range(KC):
                    mm = pe.transpose(xt_ps[:, c, :], xn2[:, c * P:(c + 1) * P], ident[:])
                mm.then_inc(s_xt2, 1)

            def gate_products(t):
                pe.wait_ge(s_xT2, t + 1)
                if isinstance(t, int) and t == 0:
                    pe.wait_ge(s_gatew, 16)
                for c in range(KC):
                    mm = pe.matmul(o_ps[:, 0:E], xT2[:, c, :], gate_sb[:, c, :], start=(c == 0), stop=(c == KC - 1))
                mm.then_inc(s_gate, 1)

            def step(t, j, b, left):
                jn, bn = (j + 1) % TB, b + (j + 1) // TB
                first = isinstance(t, int) and t == 0
                if left >= 2:
                    if normed:
                        queries(t + 1, jn)
                    scores(t + 1, jn, bn, 0)
                prob_transposes(t)
                if not first:
                    result_transposes(t - 1)
                if left >= 2:
                    scores(t + 1, jn, bn, 1)
                if not first:
                    gate_products(t - 1)
                if left >= 3:
                    transposes(t + 2)
                outputs(t, j, b)

            pe.wait_ge(s_ident, 16)
            transposes(0)
            if normed:
                queries(0, 0)
            transposes(1)
            if mask is not None:
                pe.wait_ge(s_bias, 4)
            scores(0, 0, 0, 0)
            scores(0, 0, 0, 1)
            tiles(pe, step)
            result_transposes(NT - 1)
            pe.wait_ge(s_y, NT + 1)
            gate_products(NT - 1)

        @block.scalar
        def _(act):
            def split_x(t, j):
                act.wait_ge(s_xt, t + 1)
                if not isinstance(t, int) or t >= 2:
                    act.wait_ge(s_scores, 2 * (t - 1))
                act.activation(x_hi[:, j % 2], xt_ps[:], ACT.Copy).then_inc(s_xhi, 1)

            def query_squares(t, between=None):
                for n in range(NQG):
                    act.wait_ge(s_q, NQG * t + n + 1)
                    act.wait_ge(s_qsum, NQG * t + n + 1)
                    act.activation(qsq[:], q_ps[:, n % 2, :], ACT.Square).then_inc(s_qsq, 1)
                    if between is not None:
                        between(n)

            def split_a(b, i):
                act.wait_ge(s_araw[i], 16 * (b + 1))
                after(act, s_scores, 2 * TB * b - (1 if i < PARTS // 2 else 0) if not isinstance(b, int) or b else 0)
                act.activation(a_part(a_hi, i), a_part(a_raw3, i), ACT.Copy).then_inc(s_ahi, 1)

            def split_v(b, i):
                act.wait_ge(s_vraw[i], 16 * (b + 1))
                after(act, s_o, TB * b + 1)
                act.activation(v_part(v_hi, i), v_part(v_raw3, i), ACT.Copy).then_inc(s_vhi, 1)

            def exps(t):
                if normed:
                    act.wait_ge(s_zq, t + 1)
                else:
                    act.wait_ge(s_sub, t + 2)
                act.wait_ge(s_pt, t + 1)
                act.activation(p_sb[:], z[:], ACT.Exp, scale=1.0 if normed else SCALE).then_inc(s_exp, 1)

            def split_p(t):
                act.wait_ge(s_pt, t + 2)
                act.wait_ge(s_o, t + 1)
                act.activation(p_hi[:], pt_ps[:], ACT.Copy).then_inc(s_phi, 1)

            def result_copy(t):
                act.wait_ge(s_xt2, t + 1)
                after(act, s_gate, t)
                act.activation(xT2[:], xt_ps[:], ACT.Copy).then_inc(s_xT2, 1)

            def step(t, j, b, left):
                if normed and left >= 2:
                    if j == TB - 1:
                        query_squares(t + 1, lambda i: split_a(b + 1, i))
                    elif j == 0:
                        query_squares(t + 1, lambda i: split_v(b, i))
                    else:
                        query_squares(t + 1)
                split_p(t)
                if not isinstance(t, int) or t > 0:
                    result_copy(t - 1)
                if not normed and j == TB - 2 and left >= 3:
                    for i in range(PARTS // 2):
                        split_a(b + 1, i)
                if left >= 3:
                    split_x(t + 2, (j + 2) % TB)
                if not normed and j == TB - 2 and left >= 3:
                    for i in range(PARTS // 2, PARTS):
                        split_a(b + 1, i)
                if left >= 2:
                    exps(t + 1)
                if not normed and j == TB - 1 and left >= 2:
                    for i in range(PARTS):
                        split_v(b + 1, i)

            if normed:
                act.sem_inc(s_qsq, 2)
            if normed:
                def wq_high(some):
                    for n in some:
                        act.wait_ge(s_wqraw[n], 16)
                        act.activation(wq_part(wq_hi, n), wq_raw(n), ACT.Copy).then_inc(s_wqhi, 1)
                wq_high(range(PARTS // 2))
                split_x(0, 0)
                wq_high(range(PARTS // 2, PARTS))
                query_squares(0, lambda i: split_a(0, i))
            else:
                split_x(0, 0)
                for i in range(PARTS):
                    split_a(0, i)
            split_x(1, 1)
            if not normed:
                for i in range(PARTS):
                    split_v(0, i)
            exps(0)
            tiles(act, step)
            result_copy(NT - 1)

        @block.vector
        def _(dve):
            def norm_start(t, j, b):
                dve.wait_ge(s_x[j], 16 * (b + 1))
                moments(dve, s_ln, 3 * t, x[:, j, :], stats[:], mv[:], carrier[:])

            def norm_end(t, j):
                dve.wait_ge(s_rstd, t + 2)
                after(dve, s_xt, t)
                dve.tensor_scalar(xn[:], x[:, j, :], mv[:, 0:1], rstd[:, 0:1], ALU.subtract, ALU.mult).then_inc(
                    s_xn, 1)

            def split_x(t, j):
                dve.wait_ge(s_xhi, t + 1)
                dve.tensor_tensor(x_lo[:, j % 2], xt_ps[:], x_hi[:, j % 2].bitcast(F32), ALU.subtract).then_inc(
                    s_xlo, 1)

            def query_sums(t, between=None):
                for n in range(NQG):
                    dve.wait_ge(s_qsq, NQG * t + n + 3)
                    if n == 0:
                        after(dve, s_rq, t)
                    dve.tensor_reduce(ssq[:, 4 * n:4 * n + 4], qsq[:].rearrange("p (h d) -> p h d", d=DH), AX,
                                      ALU.add).then_inc(s_qsum, 1)
                    if between is not None and n < PARTS // 2:
                        between(n)
                dve.wait_ge(s_qsum, NQG * (t + 1) + 1)
                after(dve, s_zq, t)
                dve.tensor_scalar(rq[:], ssq[:], DH * EPS, None, ALU.add).then_inc(s_rq, 1)

            def split_a(b, i):
                dve.wait_ge(s_ahi, PARTS * b + i + 1)
                dve.tensor_tensor(a_part(a_lo, i), a_part(a_raw3, i), a_part(a_hi, i).bitcast(F32),
                                  ALU.subtract).then_inc(s_alo[0], 1)

            def split_v(b, i):
                dve.wait_ge(s_vhi, PARTS * b + i + 1)
                dve.tensor_tensor(v_part(v_lo, i), v_part(v_raw3, i), v_part(v_hi, i).bitcast(F32),
                                  ALU.subtract).then_inc(s_vlo[0], 1)

            def shift(t):
                dve.wait_ge(s_scores, 2 * (t + 1))
                dve.tensor_reduce(top[:], s_ps[:], AX, ALU.max).then_inc(s_top, 1)
                dve.wait_ge(s_top, t + 1)
                after(dve, s_exp, t)
                dve.tensor_tensor(z[:], s_ps[:], top[:].unsqueeze(2).to_broadcast([P, H, S]),
                                  ALU.subtract).then_inc(s_sub, 1)

            def sums(t):
                dve.wait_ge(s_exp, t + 1)
                dve.tensor_reduce(total[:], p_sb[:], AX, ALU.add).then_inc(s_sum, 1)
                dve.wait_ge(s_sum, t + 1)
                after(dve, s_prob, t)
                dve.reciprocal(recip[:], total[:]).then_inc(s_rec, 1)

            def split_p(t):
                dve.wait_ge(s_phi, t + 1)
                dve.tensor_tensor(p_lo[:], pt_ps[:], p_hi[:].bitcast(F32), ALU.subtract).then_inc(s_plo, 1)

            def add_output(t, j):
                dve.wait_ge(s_o, t + 2)
                dve.wait_ge(s_store, 16 * (t + 1))
                dve.tensor_tensor(y[:], x[:, j, :], o_ps[:], ALU.add).then_inc(s_y, 1)

            def result_norm(t):
                dve.wait_ge(s_y, t + 2)
                moments(dve, s_ln2, 3 * t, y[:], stats[:], mv2[:], carrier[:])
                dve.wait_ge(s_rstd2, t + 1)
                after(dve, s_xt2, t)
                dve.wait_ge(s_keep, 16 * (t + 1))
                dve.tensor_scalar(xn2[:], y[:], mv2[:, 0:1], rstd2[:, 0:1], ALU.subtract, ALU.mult).then_inc(
                    s_xn2, 1)

            def keep_logits(t):
                dve.wait_ge(s_gate, t + 1)
                dve.tensor_copy(logits[:, bass.ds(t, 1), :].rearrange("p t e -> p (t e)"), o_ps[:, 0:E]).then_inc(
                    s_logits, 1)

            def step(t, j, b, left):
                if normed and left >= 2:
                    if j == TB - 1:
                        query_sums(t + 1, lambda i: split_a(b + 1, i))
                    elif j == 0:
                        query_sums(t + 1, lambda i: split_v(b, i))
                    else:
                        query_sums(t + 1)
                split_p(t)
                if not isinstance(t, int) or t > 0:
                    keep_logits(t - 1)
                if not normed and j == TB - 2 and left >= 3:
                    for i in range(PARTS // 2):
                        split_a(b + 1, i)
                if left >= 2:
                    shift(t + 1)
                if left >= 3:
                    split_x(t + 2, (j + 2) % TB)
                if left >= 4:
                    norm_start(t + 3, (j + 3) % TB, b + (j + 3) // TB)
                if left >= 2:
                    sums(t + 1)
                if left >= 4:
                    norm_end(t + 3, (j + 3) % TB)
                add_output(t, j)
                result_norm(t)
                if not normed and j == TB - 1 and left >= 2:
                    for i in range(PARTS // 2):
                        split_v(b + 1, i)

            for s in (s_xlo, s_sub, s_pt, s_plo, s_o, s_y):
                dve.sem_inc(s, 1)
            norm_start(0, 0, 0)
            norm_end(0, 0)
            if normed:
                dve.sem_inc(s_qsum, 1)
            if mask is not None:
                dve.wait_ge(s_mask, 16)
                dve.memset(one_f[:], 1.0).then_inc(s_bias, 1)
                dve.tensor_copy(maskf[:].rearrange("o b s -> o (b s)"), mask_u8[:]).then_inc(s_bias, 1)
                dve.wait_ge(s_bias, 2)
                dve.tensor_copy(one_row[:], one_f[:]).then_inc(s_bias, 1)
                dve.tensor_scalar(bias[:], maskf[:], -MASKED, MASKED, ALU.mult, ALU.add).then_inc(s_bias, 1)
            def wq_low(n):
                dve.wait_ge(s_wqhi, n + 1)
                dve.tensor_tensor(wq_part(wq_lo, n), wq_raw(n), wq_part(wq_hi, n).bitcast(F32),
                                  ALU.subtract).then_inc(s_wqlo[0], 1)
            if normed:
                wq_low(0)
            split_x(0, 0)
            if normed:
                wq_low(1)
            norm_start(1, 1, 0)
            norm_end(1, 1)
            if normed:
                query_sums(0, lambda i: split_a(0, i))
            else:
                for i in range(PARTS // 2):
                    split_a(0, i)
            split_x(1, 1)
            norm_start(2, 2, 0)
            norm_end(2, 2)
            if not normed:
                for i in range(PARTS // 2):
                    split_v(0, i)
            shift(0)
            sums(0)
            tiles(dve, step)
            keep_logits(NT - 1)

        @block.gpsimd
        def _(pool):
            def power_half(t):
                pool.wait_ge(s_ln, 3 * (t + 1))
                after(pool, s_xn, t)
                pool.tensor_tensor(rstd[:], mv[:, 1:2], power[:], ALU.pow).then_inc(s_rstd, 1)

            def query_factors(t):
                pool.wait_ge(s_rq, t + 1)
                pool.tensor_tensor(rq[:], rq[:], power[:].to_broadcast([P, H]), ALU.pow).then_inc(s_rqp, 1)

            def scale_scores(t):
                pool.wait_ge(s_rqp, t + 1)
                pool.wait_ge(s_sub, t + 2)
                pool.tensor_tensor(z[:], z[:], rq[:].unsqueeze(2).to_broadcast([P, H, S]), ALU.mult).then_inc(s_zq, 1)

            def normalise(t):
                pool.wait_ge(s_rec, t + 1)
                pool.tensor_tensor(p_sb[:], p_sb[:], recip[:].unsqueeze(2).to_broadcast([P, H, S]),
                                   ALU.mult).then_inc(s_prob, 1)

            def result_power(t):
                pool.wait_ge(s_ln2, 3 * (t + 1))
                pool.tensor_tensor(rstd2[:], mv2[:, 1:2], power[:], ALU.pow).then_inc(s_rstd2, 1)

            def split_a(b):
                for i in range(PARTS // 2, PARTS):
                    pool.wait_ge(s_ahi, PARTS * b + i + 1)
                    pool.tensor_tensor(a_part(a_lo, i), a_part(a_raw3, i), a_part(a_hi, i).bitcast(F32),
                                       ALU.subtract).then_inc(s_alo[1], 1)

            def split_v(b):
                for i in range(PARTS // 2, PARTS):
                    pool.wait_ge(s_vhi, PARTS * b + i + 1)
                    pool.tensor_tensor(v_part(v_lo, i), v_part(v_raw3, i), v_part(v_hi, i).bitcast(F32),
                                       ALU.subtract).then_inc(s_vlo[1], 1)

            def step(t, j, b, left):
                if left >= 2 and normed:
                    if j == TB - 1:
                        split_a(b + 1)
                    elif j == 0:
                        split_v(b)
                if left >= 3 and not normed and j == TB - 2:
                    split_a(b + 1)
                if left >= 2:
                    if normed:
                        query_factors(t + 1)
                        scale_scores(t + 1)
                    if left >= 4:
                        power_half(t + 3)
                    normalise(t + 1)
                result_power(t)
                if left >= 2 and not normed and j == TB - 1:
                    split_v(b + 1)

            pool.memset(power[:], -0.5).then_inc(s_rstd, 1)
            pool.wait_ge(s_rstd, 1)
            power_half(0)
            if normed:
                for n in range(PARTS // 2, PARTS):
                    pool.wait_ge(s_wqhi, n + 1)
                    pool.tensor_tensor(wq_part(wq_lo, n), wq_raw(n), wq_part(wq_hi, n).bitcast(F32),
                                       ALU.subtract).then_inc(s_wqlo[1], 1)
                    if n == PARTS // 2:
                        power_half(1)
            else:
                power_half(1)
            split_a(0)
            if normed:
                query_factors(0)
            power_half(2)
            if not normed:
                split_v(0)
            if normed:
                scale_scores(0)
            normalise(0)
            if zero_rows is not None:
                pool.memset(zeros[:], 0.0).then_inc(s_zero, 1)
            tiles(pool, step)


def route(nc, tag, logits, weight, slot, block_expert, load_weights, split_high, split_low, clear_lap):
    with ExitStack() as ctx:
        sb, ps, sem = names(ctx, nc, tag)
        best = sb("best", [P, NT])
        probs = sb("probs", [P, NT, E])
        left = sb("left", [P, NT, E])
        equal = sb("equal", [P, NT, E])
        chosen = sb("chosen", [P, 2, NT, E])
        padded = sb("padded", [P, 2 * NT - 1, E], F32R)
        rank_code = sb("rank_code", [P, E])
        earlier = sb("earlier", [P, P])
        ones = sb("ones", [P, P])
        earlier_r = sb("earlier_r", [P, P], F32R)
        ones_r = sb("ones_r", [P, P], F32R)
        zeros = sb("zeros", [P, NT - 1, E])
        taken_f = sb("taken_f", [P, E])
        taken = sb("taken", [P, E], F32R)
        s_taken = sem("taken")
        count = sb("count", [P, E])
        count_i = sb("count_i", [P, E], I32)
        rest = sb("rest", [P, E])
        ends = [sb(f"ends{i}", [P, E]) for i in range(3)]
        row = sb("row", [P, NT, E])
        slot_f = sb("slot_f", [P, 2, NT])
        block_start = sb("block_start", [1, MAX_BLOCKS + 1])
        past = sb("past", [1, MAX_BLOCKS + 1, E])
        expert_f = sb("expert_f", [1, MAX_BLOCKS + 1])
        rank_ps = ps("rank_ps", [P, NT, E])
        count_ps = ps("count_ps", [P, E])
        s_const = sem("const")
        s_step = sem("step")
        s_shift = sem("shift")
        s_exp = sem("exp")
        s_either = sem("either")
        s_rank = sem("rank")
        block = ctx.enter_context(nc.Block())

        @block.gpsimd
        def _(pool):
            pool.iota(rank_code[:], [[-1, E]], base=E, channel_multiplier=0,
                      allow_small_or_imprecise_dtypes=True).then_inc(s_const, 1)
            pool.iota(block_start[:], [[P, MAX_BLOCKS + 1]], base=0, channel_multiplier=0,
                      allow_small_or_imprecise_dtypes=True).then_inc(s_const, 1)
            pool.memset(ones[:], 1.0).then_inc(s_const, 1)
            pool.wait_ge(s_const, 3)
            pool.affine_select(out=earlier[:], in_=ones[:], compare_op=ALU.is_gt, fill=0.0, base=0,
                               pattern=[[1, P]], channel_multiplier=-1).then_inc(s_const, 1)
            pool.tensor_copy(ones_r[:], ones[:]).then_inc(s_const, 1)
            pool.wait_ge(s_const, 5)
            pool.tensor_copy(earlier_r[:], earlier[:]).then_inc(s_const, 1)
            clear_lap(pool)
            split_low(pool)

        @block.sync
        def _(sp):
            load_weights(sp)

        @block.scalar
        def _(act):
            act.wait_ge(s_shift, 1)
            act.activation(probs[:], left[:], ACT.Exp).then_inc(s_exp, 1)
            split_high(act)

        @block.tensor
        def _(pe):
            pe.wait_ge(s_const, 6)
            pe.wait_ge(s_either, 1)
            pe.matmul(rank_ps[:], earlier_r[:], padded[:, NT - 1:, :], start=True, stop=False)
            for d in range(1, NT):
                pe.matmul(rank_ps[:], ones_r[:], padded[:, NT - 1 - d:2 * NT - 1 - d, :], start=False,
                          stop=(d == NT - 1))
            pe.wait_ge(s_taken, 1)
            pe.matmul(count_ps[:], ones_r[:], taken[:], start=True, stop=True).then_inc(s_rank, 1)

        @block.vector
        def _(dve):
            step = Chain(dve, s_step)
            def over_experts(a):
                return a.unsqueeze(2).to_broadcast([P, NT, E])
            codes = rank_code[:].unsqueeze(1).to_broadcast([P, NT, E])
            step(dve.memset(zeros[:], 0.0))
            step(dve.tensor_copy(padded[:, 0:NT - 1, :], zeros[:]))
            step(dve.tensor_reduce(best[:], logits[:], AX, ALU.max))
            dve.tensor_tensor(left[:], logits[:], over_experts(best[:]), ALU.subtract).then_inc(s_shift, 1)
            dve.wait_ge(s_exp, 1)
            step(dve.tensor_reduce(best[:], probs[:], AX, ALU.add))
            step(dve.reciprocal(best[:], best[:]))
            step(dve.tensor_tensor(probs[:], probs[:], over_experts(best[:]), ALU.mult))
            dve.wait_ge(s_const, 3)
            scores = probs
            for k in range(2):
                step(dve.tensor_reduce(weight[:, k], scores[:], AX, ALU.max))
                step(dve.tensor_tensor(equal[:], scores[:], over_experts(weight[:, k]), ALU.is_equal))
                step(dve.tensor_tensor(equal[:], equal[:], codes, ALU.mult))
                step(dve.tensor_reduce(best[:], equal[:], AX, ALU.max))
                step(dve.tensor_tensor(chosen[:, k], codes, over_experts(best[:]), ALU.is_equal))
                if k == 0:
                    step(dve.scalar_tensor_tensor(left[:], chosen[:, 0], -4.0, probs[:], ALU.mult, ALU.add))
                    scores = left
            dve.tensor_tensor(padded[:, NT - 1:, :], chosen[:, 0], chosen[:, 1], ALU.add).then_inc(s_either, 1)
            dve.wait_ge(s_either, 1)
            step(dve.tensor_reduce(taken_f[:], padded[:, NT - 1:, :].bitcast(F32).rearrange("p t e -> p e t"), AX,
                                   ALU.add))
            dve.tensor_copy(taken[:], taken_f[:]).then_inc(s_taken, 1)
            dve.wait_ge(s_rank, 1)
            step(dve.tensor_scalar(count[:], count_ps[:], float(P - 1), None, ALU.add))
            step(dve.tensor_copy(count_i[:], count[:]))
            step(dve.tensor_scalar(count_i[:], count_i[:], ~(P - 1) & 0xffff, None, ALU.bitwise_and))
            step(dve.tensor_copy(count[:], count_i[:]))
            end = count
            for i, d in enumerate((1, 2, 4)):
                dve.tensor_copy(ends[i][:, 0:d], end[:, 0:d])
                step(dve.tensor_tensor(ends[i][:, d:E], end[:, d:E], end[:, 0:E - d], ALU.add))
                end = ends[i]
            step(dve.tensor_tensor(past[:], end[0:1, :].unsqueeze(1).to_broadcast([1, MAX_BLOCKS + 1, E]),
                                   block_start[:].unsqueeze(2).to_broadcast([1, MAX_BLOCKS + 1, E]), ALU.is_le))
            step(dve.tensor_reduce(expert_f[:], past[:], AX, ALU.add))
            step(dve.tensor_scalar(expert_f[:], expert_f[:], float(E - 1), None, ALU.min))
            step(dve.tensor_copy(block_expert[:], expert_f[:]))
            step(dve.tensor_tensor(rest[:], end[:], count[:], ALU.subtract))
            step(dve.tensor_tensor(row[:], rank_ps[:], rest[:].unsqueeze(1).to_broadcast([P, NT, E]), ALU.add))
            for k in range(2):
                step(dve.tensor_tensor(equal[:], row[:], chosen[:, k], ALU.mult))
                step(dve.tensor_reduce(slot_f[:, k], equal[:], AX, ALU.add))
            step(dve.tensor_copy(slot[:], slot_f[:]))


def stored(eng, s_store, count):
    for par in range(2):
        eng.wait_ge(s_store[par], 16 * ((count + 1 - par) // 2 + 1))


def blocks(nc, tag, kind, w, src_tile, res_tile, out_tile, count, ident, s_ident, y, s_store, before=None,
           early=None, beside=None, raw=None, loaded=None,
           block_expert=None, load_next=None, next_loaded=None, slot=None, scatter_to=None, gather_from=None,
           weight=None):
    streamed = kind == "experts"
    with ExitStack() as ctx:
        sb, ps, sem = names(ctx, nc, tag)
        if early is None:
            src = sb("src", [P, 2, D])
            s_src = [sem(f"src{i}") for i in range(2)]
        else:
            src, res, s_src, s_res = early
        xT = sb("xT", [P, 2, KC, P], F32R)
        act_gate = sb("act_gate", [P, 2, F])
        hidden = sb("hidden", [P, 2, F])
        hT = sb("hT", [P, FC, P], F32R)
        xT_lo = sb("xT_lo", [P, 2, KC, P], F32R)
        hT_lo = sb("hT_lo", [P, FC, P], F32R)
        gu_hi, gu_lo, d_hi, d_lo = w
        if gather_from is not None:
            rows = sb("rows", [P, 2, 2, D])
            part = sb("part", [P, 2, D])
        xt_ps = ps("xt_ps", [P, KC, P])
        gu_ps = ps("gu_ps", [P, 2, 2, 512])
        ht_ps = ps("ht_ps", [P, FC, P])
        y_ps = ps("y_ps", [P, 2, D])
        s_rows = [sem(f"rows{i}") for i in range(2)]
        s_scatter = [sem(f"scatter{i}") for i in range(2)]
        s_xt = sem("xt")
        s_xT = sem("xT")
        s_xTl = sem("xTl")
        s_gu_ps = sem("gu_ps")
        s_guhi = sem("guhi")
        s_gulo = [sem(f"gulo{i}") for i in range(2)]
        s_gu_used = sem("gu_used")
        s_dhi = sem("dhi")
        s_dlo = sem("dlo")
        s_d_used = sem("d_used")
        s_gate = sem("gate")
        s_h = sem("h")
        s_ht = sem("ht")
        s_hT = sem("hT")
        s_hTl = sem("hTl")
        s_down = sem("down")
        s_part = sem("part")
        s_y = sem("y")
        block = ctx.enter_context(nc.Block())
        loops = (count - 3) // 2
        middle = NT // 2 if streamed else None

        def stream(eng, step, between=None):
            for start, end in ((0, loops),) if middle is None else ((0, middle), (middle, loops)):
                with eng.Fori(start, end) as i:
                    for u in range(2):
                        step(2 * i + u, u, i, 4)
                if between is not None and start == 0:
                    between()
            for n in range(2 * loops, count):
                step(n, n % 2, n // 2, count - n)

        class Expert:

            def __init__(self, eng):
                self.eng, self.least = eng, 0

            def past_middle(self):
                self.least = 1

            def __call__(self, m):
                if isinstance(m, int) and m == count:
                    return 0
                return self.eng.value_load(block_expert[0:1, bass.ds(m, 1)], min_val=self.least, max_val=E - 1)

        def gu_raw(e, c):
            return raw[0][:, bass.ds(e, 1), c].rearrange("p e n -> p (e n)")

        def d_raw(e, j):
            return raw[1][:, bass.ds(e, 1), j].rearrange("p e n -> p (e n)")

        @block.sync
        def _(sp):
            for par in range(2):
                sp.sem_inc(s_store[par], 16)
                if early is None:
                    sp.dma_start(src[:, par], src_tile(par)).then_inc(s_src[par], 16)

            def load_rows(m, par, i):
                sp.wait_ge(s_xt, m - 1)
                if scatter_to is not None:
                    sp.wait_ge(s_scatter[par], 32 * i)
                sp.dma_start(src[:, par], src_tile(m)).then_inc(s_src[par], 16)

            def step(m, par, i, left):
                if left >= 4:
                    load_rows(m + 3, 1 - par, i + 1 + par)
                if beside is not None and par == 0:
                    beside(sp, i)
                sp.wait_ge(s_y, m + 3)
                sp.dma_start(out_tile(m), y[:, par]).then_inc(s_store[par], 16)
                if left >= 3 and not streamed:
                    sp.dma_start(res[:, par], res_tile(m + 2)).then_inc(s_res[par], 16)
            if before is not None:
                before(sp)
            load_rows(2, 0, 1)
            if streamed:
                with sp.Fori(0, middle + 1) as i:
                    for u in range(2):
                        step(2 * i + u, u, i, 4)
                resume = middle + 1 + -(-len(load_next) // 2)
                for n in range(2 * middle + 2, 2 * resume):
                    if n - 2 * middle - 2 < len(load_next):
                        load_next[n - 2 * middle - 2](sp)
                    step(n, n % 2, n // 2, count - n)
                with sp.Fori(resume, loops) as i:
                    for u in range(2):
                        step(2 * i + u, u, i, 4)
                for n in range(2 * loops, count):
                    step(n, n % 2, n // 2, count - n)
            else:
                stream(sp, step)
            if gather_from is not None:
                stored(sp, s_store, count)
            if scatter_to is not None:
                for par in range(2):
                    sp.wait_ge(s_scatter[par], 32 * ((count + 1 - par) // 2))

        @block.tensor
        def _(pe):
            def transposes(m, par, i):
                pe.wait_ge(s_src[par], 16 * (i + 1))
                pe.wait_ge(s_xT, m + 1)
                pe.wait_ge(s_xTl, m + 1)
                for c in range(KC):
                    mm = pe.transpose(xt_ps[:, c, :], src[:, par, c * P:(c + 1) * P], ident[:])
                mm.then_inc(s_xt, 1)

            def gate_up(n, u, pieces):
                if 0 in pieces:
                    pe.wait_ge(s_xTl, n + 2)
                    pe.wait_ge(s_gate, n + 1)
                    pe.wait_ge(s_h, n + 1)
                for c in pieces:
                    if streamed:
                        pe.wait_ge(s_gulo[c % 2], 2 * n + c // 2 + 1)
                    for k in range(2):
                        f = slice(k * F, (k + 1) * F)
                        mm = matmul3(pe, gu_ps[:, u, k, 0:F], xT[:, u, c, :], xT_lo[:, u, c, :], gu_hi[:, c, f],
                                     gu_lo[:, c, f], c == 0, c == KC - 1)
                    if streamed:
                        mm.then_inc(s_gu_used, 1)
                if KC - 1 in pieces and not streamed:
                    mm.then_inc(s_gu_ps, 1)

            def hidden_transposes(n, u):
                pe.wait_ge(s_h, n + 3)
                pe.wait_ge(s_hT, n + 1)
                pe.wait_ge(s_hTl, n + 1)
                for j in range(FC):
                    f0 = min(j * P, F - P)
                    mm = pe.transpose(ht_ps[:, j, :], hidden[:, u, f0:f0 + P], ident[:])
                mm.then_inc(s_ht, 1)

            def down(n, u):
                pe.wait_ge(s_hTl, n + 2)
                pe.wait_ge(s_y, n + 1)
                for j in range(FC):
                    if streamed:
                        pe.wait_ge(s_dlo, FC * n + j + 1)
                    mm = matmul3(pe, y_ps[:, u, :], hT[:, j, :], hT_lo[:, j, :], d_hi[:, j, :], d_lo[:, j, :],
                                 j == 0, j == FC - 1)
                    if streamed:
                        mm.then_inc(s_d_used, 1)
                if not streamed:
                    mm.then_inc(s_down, 1)

            def step(n, u, i, left):
                if left >= 2:
                    gate_up(n + 1, 1 - u, range(KC // 2))
                hidden_transposes(n, u)
                if left >= 3:
                    transposes(n + 2, u, i + 1)
                if left >= 2:
                    gate_up(n + 1, 1 - u, range(KC // 2, KC))
                down(n, u)

            pe.wait_ge(s_ident, 16)
            transposes(0, 0, 0)
            transposes(1, 1, 0)
            gate_up(0, 0, range(KC))
            stream(pe, step)

        def products_done(eng, n):
            if streamed:
                eng.wait_ge(s_gu_used, KC * (n + 1))
            else:
                eng.wait_ge(s_gu_ps, n + 1)

        def result_done(eng, n):
            if streamed:
                eng.wait_ge(s_d_used, FC * (n + 1))
            else:
                eng.wait_ge(s_down, n + 1)

        @block.scalar
        def _(act):
            expert = Expert(act)

            def rows_copy(m, par):
                act.wait_ge(s_xt, m + 1)
                if not isinstance(m, int) or m >= 2:
                    products_done(act, m - 2)
                act.activation(xT[:, par], xt_ps[:], ACT.Copy).then_inc(s_xT, 1)

            def silu(n, u):
                products_done(act, n)
                act.wait_ge(s_h, n + 1)
                act.activation(act_gate[:, u], gu_ps[:, u, 0, 0:F], ACT.Silu).then_inc(s_gate, 1)

            def gu_high(m, c, e):
                if not isinstance(m, int) or m >= 1:
                    act.wait_ge(s_gu_used, KC * (m - 1) + c + 1)
                act.activation(gu_hi[:, c], gu_raw(e, c), ACT.Copy).then_inc(s_guhi, 1)

            def d_high(m, e):
                for j in range(FC):
                    if not isinstance(m, int) or m >= 1:
                        act.wait_ge(s_d_used, FC * (m - 1) + j + 1)
                    act.activation(d_hi[:, j], d_raw(e, j), ACT.Copy).then_inc(s_dhi, 1)

            def hidden_copy(n):
                act.wait_ge(s_ht, n + 3)
                if not isinstance(n, int) or n >= 1:
                    result_done(act, n - 1)
                act.activation(hT[:], ht_ps[:], ACT.Copy).then_inc(s_hT, 1)

            def step(n, u, i, left):
                if streamed:
                    if left >= 2:
                        if left == 2:
                            act.wait_ge(next_loaded, 64)
                        e = expert(n + 2)
                        gu_high(n + 2, 0, e)
                        gu_high(n + 2, 1, e)
                    hidden_copy(n)
                    if left >= 3:
                        rows_copy(n + 2, u)
                    if left >= 2:
                        gu_high(n + 2, 2, e)
                        gu_high(n + 2, 3, e)
                        silu(n + 1, 1 - u)
                    d_high(n + 1, expert(n + 1))
                else:
                    hidden_copy(n)
                    if left >= 3:
                        rows_copy(n + 2, u)
                    if left >= 2:
                        silu(n + 1, 1 - u)
            act.sem_inc(s_xT, 1)
            act.sem_inc(s_gate, 2)
            act.sem_inc(s_hT, 1)
            rows_copy(0, 0)
            if streamed:
                act.wait_ge(loaded, 48 * E)
                e0, e1 = expert(0), expert(1)
                for c in range(KC):
                    gu_high(0, c, e0)
                rows_copy(1, 1)
                for c in range(KC):
                    gu_high(1, c, e1)
                silu(0, 0)
                d_high(0, e0)
            else:
                rows_copy(1, 1)
                silu(0, 0)
            stream(act, step, between=expert.past_middle)

        @block.vector
        def _(dve):
            expert = Expert(dve)

            def rows_low(m, par):
                dve.wait_ge(s_xT, m + 2)
                dve.tensor_tensor(xT_lo[:, par], xt_ps[:], xT[:, par].bitcast(F32), ALU.subtract).then_inc(s_xTl, 1)

            def product(n, u):
                dve.wait_ge(s_gate, n + 3)
                dve.wait_ge(s_ht, n + 1)
                dve.tensor_tensor(hidden[:, u], act_gate[:, u], gu_ps[:, u, 1, 0:F], ALU.mult).then_inc(s_h, 1)

            def gu_low(m, c, e):
                dve.wait_ge(s_guhi, KC * m + c + 1)
                dve.tensor_tensor(gu_lo[:, c], gu_raw(e, c), gu_hi[:, c].bitcast(F32), ALU.subtract).then_inc(
                    s_gulo[0], 1)

            def d_low(m, e):
                for j in range(FC):
                    dve.wait_ge(s_dhi, FC * m + j + 1)
                    dve.tensor_tensor(d_lo[:, j], d_raw(e, j), d_hi[:, j].bitcast(F32), ALU.subtract).then_inc(
                        s_dlo, 1)

            def gathered(m, par, i):
                dve.wait_ge(s_rows[par], 32 * (i + 1))
                dve.wait_ge(s_res[par], 16 * (i + 1))
                dve.scalar_tensor_tensor(part[:, 0], rows[:, par, 0], weight[:, 0, bass.ds(m, 1)], res[:, par],
                                         ALU.mult, ALU.add).then_inc(s_part, 1)
                dve.wait_ge(s_part, 2 * m + 1)
                dve.scalar_tensor_tensor(part[:, 1], rows[:, par, 1], weight[:, 1, bass.ds(m, 1)], part[:, 0],
                                         ALU.mult, ALU.add).then_inc(s_part, 1)
                dve.wait_ge(s_part, 2 * m + 2)

            def result(n, u, i):
                if gather_from is not None:
                    gathered(n, u, i)
                result_done(dve, n)
                dve.wait_ge(s_store[u], 16 * (i + 1))
                if gather_from is not None:
                    dve.tensor_tensor(y[:, u], part[:, 1], y_ps[:, u], ALU.add).then_inc(s_y, 1)
                elif streamed:
                    dve.tensor_copy(y[:, u], y_ps[:, u]).then_inc(s_y, 1)
                else:
                    dve.wait_ge(s_res[u], 16 * (i + 1))
                    dve.tensor_tensor(y[:, u], res[:, u], y_ps[:, u], ALU.add).then_inc(s_y, 1)

            def step(n, u, i, left):
                if streamed and left >= 2:
                    e = expert(n + 2)
                    gu_low(n + 2, 0, e)
                dve.wait_ge(s_hT, n + 2)
                dve.tensor_tensor(hT_lo[:], ht_ps[:], hT[:].bitcast(F32), ALU.subtract).then_inc(s_hTl, 1)
                if left >= 3:
                    rows_low(n + 2, u)
                if streamed and left >= 2:
                    gu_low(n + 2, 2, e)
                if left >= 2:
                    product(n + 1, 1 - u)
                if streamed:
                    d_low(n + 1, expert(n + 1))
                result(n, u, i)
            dve.sem_inc(s_xTl, 1)
            dve.sem_inc(s_hTl, 1)
            dve.sem_inc(s_h, 2)
            dve.sem_inc(s_ht, 2)
            dve.sem_inc(s_y, 2)
            if before is not None:
                before(dve)
            rows_low(0, 0)
            if streamed:
                e0, e1 = expert(0), expert(1)
                gu_low(0, 0, e0)
                gu_low(0, 2, e0)
                rows_low(1, 1)
                gu_low(1, 0, e1)
                gu_low(1, 2, e1)
                product(0, 0)
                d_low(0, e0)
            else:
                rows_low(1, 1)
                product(0, 0)
            stream(dve, step, between=expert.past_middle)

        @block.gpsimd
        def _(pool):
            if gather_from is not None:
                before(pool)
            for m in range(count if slot is not None else 0):
                if scatter_to is not None:
                    pool.wait_ge(s_src[m % 2], 16 * (m // 2 + 1))
                    for k in range(2):
                        pool.indirect_dma_start(out=scatter_to, out_offset=bass.IndirectOffsetOnAxis(
                            ap=slot[:, k, m:m + 1], axis=0), in_=src[:, m % 2], in_offset=None).then_inc(
                                s_scatter[m % 2], 16)
                if gather_from is not None:
                    after(pool, s_part, 2 * (m - 1))
                    for k in range(2):
                        pool.indirect_dma_start(out=rows[:, m % 2, k], out_offset=None, in_=gather_from,
                                                in_offset=bass.IndirectOffsetOnAxis(ap=slot[:, k, m:m + 1], axis=0)
                                                ).then_inc(s_rows[m % 2], 16)
            if not streamed:
                return
            expert = Expert(pool)

            def gu_low(m):
                e = expert(m)
                for c in range(1, KC, 2):
                    pool.wait_ge(s_guhi, KC * m + c + 1)
                    pool.tensor_tensor(gu_lo[:, c], gu_raw(e, c), gu_hi[:, c].bitcast(F32), ALU.subtract).then_inc(
                        s_gulo[1], 1)

            def step(n, u, i, left):
                if left >= 2:
                    gu_low(n + 2)
            gu_low(0)
            gu_low(1)
            stream(pool, step, between=expert.past_middle)


def mixture(nc, tag, x_in, x_mid, x_out, xn_d, logits, sorted_d, y_d, gu, dn, ident, s_ident):
    with ExitStack() as ctx:
        sb, ps, sem = names(ctx, nc, tag)
        weight = sb("weight", [P, 2, NT])
        slot = sb("slot", [P, 2, NT], I32)
        block_expert = sb("block_expert", [1, MAX_BLOCKS + 1], I32)
        gu_hi = sb("gu_hi", [P, KC, 2 * F], F32R)
        gu_lo = sb("gu_lo", [P, KC, 2 * F], F32R)
        d_hi = sb("d_hi", [P, FC, D], F32R)
        d_lo = sb("d_lo", [P, FC, D], F32R)
        shared_w = (gu_hi, gu_lo, d_hi, d_lo)
        src = sb("src", [P, 2, D])
        res = sb("res", [P, 2, D])
        y = sb("y", [P, 2, D])
        s_stores = [[sem(f"store{n}_{i}") for i in range(2)] for n in range(3)]
        s_first = [[sem(f"{what}{u}_{i}") for i in range(2)] for what in ("src", "res") for u in range(2)]

        def shared_early(pass_):
            return src, res, s_first[pass_], s_first[2 + pass_]

        def load_early(sp, pass_, residual):
            for par in range(2):
                sp.dma_start(src[:, par], xn_d[par * P:(par + 1) * P, :]).then_inc(s_first[pass_][par], 16)
                sp.dma_start(res[:, par], residual[par * P:(par + 1) * P, :]).then_inc(s_first[2 + pass_][par], 16)
        s_rawgu = sem("rawgu")
        s_rawd = sem("rawd")
        s_raw2 = sem("raw2")
        s_high = sem("high")
        s_experts = sem("experts")
        s_lap = sem("lap")
        full = (FC - 1) * P

        with ExitStack() as inner:
            w_gu = inner.enter_context(nc.sbuf_tensor(tag + "w_gu", [P, E, KC, 2 * F], F32))
            w_d = inner.enter_context(nc.sbuf_tensor(tag + "w_d", [P, E, FC, D], F32))
            raw = E - 1

            def load_first(sp):
                sp.dma_start(w_gu[:, raw], gu[E]).then_inc(s_rawgu, 16)
                sp.dma_start(w_d[:, raw, 0:FC - 1], dn[E, 0:full].rearrange("(j p) n -> p j n", p=P)).then_inc(
                    s_rawd, 16)
                sp.dma_start(w_d[LAP:P, raw, FC - 1], dn[E, full:F]).then_inc(s_rawd, 16)
                load_early(sp, 0, x_in)

            def load_expert(sp, e):
                gu_e, gu_s = w_gu[:, bass.ds(e, 1)], gu[bass.ds(e, 1)]
                dn_e, dn_s = w_d[:, bass.ds(e, 1)], dn[bass.ds(e, 1)]
                sp.dma_start(gu_e.rearrange("p e c n -> p (e c) n"), gu_s.rearrange("e p c n -> p (e c) n")).then_inc(
                    s_experts, 16)
                sp.dma_start(dn_e[:, :, 0:FC - 1].rearrange("p e j n -> p (e j) n"),
                             dn_s[:, 0:full].rearrange("e (j p) n -> p (e j) n", p=P)).then_inc(s_experts, 16)
                sp.dma_start(dn_e[LAP:P, :, FC - 1].rearrange("p e n -> p (e n)"),
                             dn_s[:, full:F].rearrange("e p n -> p (e n)")).then_inc(s_experts, 16)

            def clear_lap(pool):
                pool.memset(w_d[0:LAP, raw, FC - 1, :], 0.0).then_inc(s_lap, 1)
                pool.memset(w_d[0:LAP, 0:raw, FC - 1, :], 0.0).then_inc(s_lap, 1)

            def split_high(act):
                act.wait_ge(s_rawgu, 16)
                for c in range(KC):
                    act.activation(gu_hi[:, c], w_gu[:, raw, c], ACT.Copy).then_inc(s_high, 1)
                act.wait_ge(s_lap, 1)
                act.wait_ge(s_rawd, 32)
                act.activation(d_hi[:], w_d[:, raw], ACT.Copy).then_inc(s_high, 1)

            def split_low(pool):
                for c in range(KC):
                    pool.wait_ge(s_high, c + 1)
                    pool.tensor_tensor(gu_lo[:, c], w_gu[:, raw, c], gu_hi[:, c].bitcast(F32), ALU.subtract)
                pool.wait_ge(s_high, KC + 1)
                pool.tensor_tensor(d_lo[:], w_d[:, raw], d_hi[:].bitcast(F32), ALU.subtract)

            route(nc, tag + "r", logits, weight, slot, block_expert, load_first, split_high, split_low, clear_lap)
            tile_of = lambda a: lambda m: a[bass.ds(m * P, P), :]
            blocks(nc, tag + "s", "shared", shared_w, tile_of(xn_d), tile_of(x_in), tile_of(x_mid), NT, ident, s_ident,
                   y, s_stores[0], early=shared_early(0), beside=load_expert, slot=slot, scatter_to=sorted_d)
            gu_2, dn_2 = gu[E + 1], dn[E + 1]
            load_second = [
                lambda sp: sp.dma_start(w_gu[:, 0, 0:KC // 2], gu_2[:, 0:KC // 2]).then_inc(s_raw2, 16),
                lambda sp: sp.dma_start(w_gu[:, 0, KC // 2:KC], gu_2[:, KC // 2:KC]).then_inc(s_raw2, 16),
                lambda sp: sp.dma_start(w_d[:, 0, 0:FC - 1], dn_2[0:full].rearrange("(j p) n -> p j n", p=P)
                                        ).then_inc(s_raw2, 16),
                lambda sp: sp.dma_start(w_d[LAP:P, 0, FC - 1], dn_2[full:F]).then_inc(s_raw2, 16),
                lambda sp: load_early(sp, 1, x_mid)]

            blocks(nc, tag + "e", "experts", shared_w, tile_of(sorted_d), None, tile_of(y_d), MAX_BLOCKS, ident,
                   s_ident, y, s_stores[1], before=lambda eng: stored(eng, s_stores[0], NT),
                   raw=(w_gu, w_d), loaded=s_experts, block_expert=block_expert,
                   load_next=load_second, next_loaded=s_raw2)
        blocks(nc, tag + "f", "shared", shared_w, tile_of(xn_d), tile_of(x_mid), tile_of(x_out), NT, ident, s_ident,
               y, s_stores[2], before=lambda eng: stored(eng, s_stores[1], MAX_BLOCKS), early=shared_early(1), slot=slot, gather_from=y_d, weight=weight)


def program(nc, ins, out):
    def dram(name, shape):
        return nc.dram_tensor(name, shape, F32, kind="Internal").ap()
    x = ins["x"].rearrange("b t d -> (b t) d")
    out = out.rearrange("b t d -> (b t) d")
    sorted_d = dram("sorted_rows", (MAX_BLOCKS * P, D))
    y_d = dram("expert_rows", (MAX_BLOCKS * P, D))
    a_d = dram("a", (B, P, KC * HS))
    v_d = dram("v", (B, H, S, D))
    x1, x2, x3, x4, x5 = (dram(f"x{i}", (B * T, D)) for i in range(1, 6))
    xn_d = dram("xn", (B * T, D))

    with ExitStack() as whole:
        sb, ps, sem = names(whole, nc, "all")
        ident = sb("ident", [P, P])
        s_ident = sem("ident")
        for layer, x_in, x_att, x_mid, x_out in ((0, x, x1, x2, x3), (1, x3, x4, x5, out)):
            w = lambda name: ins[f"{name}{layer}"]
            mask, gq, gk, wq = (ins["mask"], None, None, None) if layer == 0 else (
                None, ins["gq"], ins["gk"], ins["wq1"])
            s_x = [sem(f"x{layer}_{i}") for i in range(TB)]
            with ExitStack() as ctx:
                logits = ctx.enter_context(nc.sbuf_tensor(f"logits{layer}", [P, NT, E], F32))
                with ExitStack() as attention:
                    a_raw = attention.enter_context(nc.sbuf_tensor(f"a_raw{layer}", [P, KC * HS], F32))
                    v_raw = attention.enter_context(nc.sbuf_tensor(f"v_raw{layer}", [P, NQ * D], F32))
                    s_wqraw = [sem(f"wqraw{i}") for i in range(PARTS)] if wq is not None else None
                    tiles_x = attention.enter_context(nc.sbuf_tensor(f"x{layer}_tiles", [P, TB, D], F32))

                    def early(sp):
                        for t in range(TB):
                            sp.dma_start(tiles_x[:, t], x_in[t * P:(t + 1) * P, :]).then_inc(s_x[t], 16)
                        if wq is not None:
                            for n in range(PARTS):
                                sp.dma_start(wq_staged(a_raw, v_raw, n), wq.rearrange("(c p) n -> p c n", p=P)[
                                    :, :, n * 512:(n + 1) * 512]).then_inc(s_wqraw[n], 16)
                        if layer == 0:
                            sp.dma_start(ident[:], ins["ident"]).then_inc(s_ident, 16)
                    prep(nc, f"p{layer}", 8 * (layer + 1), ins["ctx_t"], w("wk"), w("wv"), w("wq_t"), w("wo"), gq, gk,
                         mask, a_d, v_d, early)
                    attend(nc, f"t{layer}", tiles_x, s_x, a_raw, v_raw, s_wqraw, x_in,
                           x_att, xn_d, logits, w("gate_t"), a_d, v_d, mask, ident, s_ident,
                           zero_rows=sorted_d if layer == 0 else None)
                mixture(nc, f"m{layer}", x_att, x_mid, x_out, xn_d, logits, sorted_d, y_d,
                        w("gu"), w("dn"), ident, s_ident)


def kernel(**inputs):
    import numpy as np
    import concourse.bacc as bacc
    from concourse.bass_utils import run_bass_kernel_spmd as run

    a = {k: np.asarray(v) for k, v in inputs.items()}

    def chunks(w):
        return np.swapaxes(w.reshape(w.shape[:-2] + (KC, P, w.shape[-1])), -3, -2)

    def gate_up(experts, shared_gate, shared_up):
        halves = np.concatenate([shared_gate.reshape(NJ, F, D), shared_up.reshape(NJ, F, D)], axis=1)
        return chunks(np.swapaxes(np.concatenate([experts, halves], axis=0), 1, 2))

    def down(experts, shared):
        return np.concatenate([np.swapaxes(experts, 1, 2), shared.T.reshape(NJ, F, D)], axis=0)

    sgu = a["L0_ffn_shared_gate_up"]
    data = {
        "x": a["x"], "ctx_t": a["ctx_1024"].reshape(BS, CD).T, "mask": a["mask_BxS2_bf1"],
        "ident": np.eye(P, dtype=np.float32),
        "wk0": a["L0_xattn_Wk"], "wv0": a["L0_xattn_Wv"], "wq_t0": a["L0_xattn_Wq"].T, "wo0": a["L0_xattn_Wo"],
        "wk1": a["L1_xattn_Wk"], "wv1": a["L1_xattn_Wv"], "wq_t1": a["L1_xattn_Wq"].T, "wo1": a["L1_xattn_Wo"],
        "wq1": a["L1_xattn_Wq"], "gq": a["L1_xattn_gq"], "gk": a["L1_xattn_gk"],
        "gate_t0": a["L0_ffn_gate_weight"].T,
        "gu0": gate_up(a["L0_ffn_gate_up_weights"], sgu[:NJ * F], sgu[NJ * F:]),
        "dn0": down(a["L0_ffn_down_weights"], a["L0_ffn_shared_down"]),
        "gate_t1": a["L1_ffn_gate_w"].T,
        "gu1": gate_up(np.concatenate([a["L1_ffn_w1"], a["L1_ffn_w2"]], axis=1), a["L1_ffn_sw1"], a["L1_ffn_sw2"]),
        "dn1": down(a["L1_ffn_w3"], a["L1_ffn_sw3"]),
    }
    nc = bacc.Bacc("TRN2", target_bir_lowering=False, num_devices=1)
    arrays, ins = {}, {}
    for name, value in data.items():
        value = np.ascontiguousarray(value)
        arrays[f"in_{name}"] = value
        ins[name] = nc.dram_tensor(f"in_{name}", value.shape, mybir.dt.from_np(value.dtype), kind="ExternalInput").ap()
    out = nc.dram_tensor("out", (B, T, D), F32, kind="ExternalOutput").ap()
    program(nc, ins, out)
    return run(nc, [arrays], core_ids=[0]).results[0]["out"]
```
